# Optimizing a Trainium2 kernel written in Bass

```python
import numpy as np
import jax
import jax.numpy as jnp

def _softmax(x, axis=-1):
    return jax.nn.softmax(x, axis=axis)

def _gelu(x):
    return jax.nn.gelu(x, approximate=True)

def _silu(x):
    return jax.nn.silu(x)

def _sigmoid(x):
    return jax.nn.sigmoid(x)

def _layernorm(x, axis=-1, eps=1e-05):
    m = jnp.mean(x, axis=axis, keepdims=True)
    v = jnp.var(x, axis=axis, keepdims=True)
    return (x - m) / jnp.sqrt(v + eps)

def _scatter_add(tgt, idx, src, axis=0):
    return tgt.at[idx].add(src)

def _segment_sum(src, seg, n):
    return jax.ops.segment_sum(src, seg, n)
kernel_name = 'mk_sandwich_d2_jaxref_r8_4a3301'

def setup_inputs(seed: int=0):
    np.random.seed(seed)
    _w = jnp.asarray

    def _L0_attn_setup():
        import jax, jax.numpy as jnp
        import numpy as np
        B, N = (2, 256)
        H, R = (8, 64)
        IN_DIM, OUT_DIM = (64, 64)
        D = IN_DIM + OUT_DIM
        INIT = 1.0
        key = jax.random.key(seed)
        k1, k2, k3, k4 = jax.random.split(key, 4)
        x = jax.random.normal(k1, (B, N, D), dtype=jnp.float32)
        Wq = jax.random.normal(k2, (H * R, D), dtype=jnp.float32) * (INIT / np.sqrt(H * R * D))
        Wk = jax.random.normal(k3, (H * R, D), dtype=jnp.float32) * (INIT / np.sqrt(H * R * D))
        Wv = jax.random.normal(k4, (H * D, D), dtype=jnp.float32) * (INIT / np.sqrt(H * D * D))
        Wk = Wk.at[:, -1].set(0.0)
        rows = np.arange(1, H + 1) * D - 1
        Wv = Wv.at[rows, :IN_DIM].set(0.0)
        return {'x': x, 'Wq': Wq, 'Wk': Wk, 'Wv': Wv}
    _L0_attn_in = _L0_attn_setup()

    def _L0_ffn_setup():
        import jax, jax.numpy as jnp
        import numpy as np
        D = 128
        H = 128
        E = 8
        K = 2
        I = 2 * 128
        ROUTE_SCALE = 1.0
        key = jax.random.key(seed)
        ks = jax.random.split(key, 12)
        s = lambda *sh: 1.0 / np.sqrt(sh[-1])
        return {'x': jax.random.normal(ks[0], (1, 256, D), jnp.float32), 'gate_w': jax.random.normal(ks[1], (E, D), jnp.float32) * s(E, D), 'w1': jax.random.normal(ks[2], (E, H, D), jnp.float32) * s(H, D), 'b1': jax.random.normal(ks[3], (E, H), jnp.float32) * 0.01, 'w2': jax.random.normal(ks[4], (E, D, H), jnp.float32) * s(D, H), 'b2': jax.random.normal(ks[5], (E, D), jnp.float32) * 0.01, 'w3': jax.random.normal(ks[6], (E, H, D), jnp.float32) * s(H, D), 'b3': jax.random.normal(ks[7], (E, H), jnp.float32) * 0.01, 'sw1': jax.random.normal(ks[8], (I, D), jnp.float32) * s(I, D), 'sw2': jax.random.normal(ks[9], (I, D), jnp.float32) * s(I, D), 'sw3': jax.random.normal(ks[10], (D, I), jnp.float32) * s(D, I)}
    _L0_ffn_in = _L0_ffn_setup()

    def _L1_attn_setup():
        import jax, jax.numpy as jnp
        import numpy as np
        B, S, D, H = (2, 256, 128, 16)
        HD = D // H
        MAX_BIAS = 8.0

        def _alibi_bias(T, Sk, dtype):
            slopes = (2.0 ** (-MAX_BIAS / H)) ** jnp.arange(1, H + 1, dtype=dtype)
            qpos = jnp.arange(T)[:, None]
            kpos = jnp.arange(Sk)[None, :]
            rel = -jnp.abs(kpos - qpos).astype(dtype)
            return slopes[:, None, None] * rel[None]
        key = jax.random.key(seed)
        ks = jax.random.split(key, 5)
        sc = 1.0 / np.sqrt(D)
        return {'x': jax.random.normal(ks[0], (B, S, D), jnp.float32), 'Wq': jax.random.normal(ks[1], (D, D), jnp.float32) * sc, 'bq': jnp.zeros((D,), jnp.float32), 'Wk': jax.random.normal(ks[2], (D, D), jnp.float32) * sc, 'bk': jnp.zeros((D,), jnp.float32), 'Wv': jax.random.normal(ks[3], (D, D), jnp.float32) * sc, 'bv': jnp.zeros((D,), jnp.float32), 'Wo': jax.random.normal(ks[4], (D, D), jnp.float32) * sc, 'bo': jnp.zeros((D,), jnp.float32)}
    _L1_attn_in = _L1_attn_setup()

    def _L1_ffn_setup():
        import jax, jax.numpy as jnp
        import numpy as np
        DIM = 128
        DEPTH = 2
        HEADS = 8
        DIM_HEAD = 64
        WINDOW = 64
        INNER = HEADS * DIM_HEAD
        HID = int(DIM * 4 * 2 / 3)
        B, N = (2, 1024)
        QK_SCALE = 8.0

        def shift_token(t):
            t1, t2 = jnp.split(t, 2, axis=-1)
            t2 = jnp.pad(t2, ((0, 0), (1, 0), (0, 0)))[:, :-1]
            return jnp.concatenate([t1, t2], axis=-1)

        def l2norm(t):
            return t / jnp.clip(jnp.linalg.norm(t, axis=-1, keepdims=True), 1e-12)

        def rotate_half(x):
            x1, x2 = jnp.split(x, 2, axis=-1)
            return jnp.concatenate([-x2, x1], axis=-1)

        def rotary_xpos(q, k):
            n = q.shape[-2]
            half_idx = jnp.arange(0, DIM_HEAD, 2, dtype=jnp.float32)
            inv_freq = 1.0 / 10000.0 ** (half_idx / DIM_HEAD)
            t = jnp.arange(n, dtype=jnp.float32)
            freqs = t[:, None] * inv_freq[None, :]
            freqs = jnp.concatenate([freqs, freqs], axis=-1)
            base = (half_idx + 0.4 * DIM_HEAD) / (1.4 * DIM_HEAD)
            power = (t - n // 2) / float(WINDOW // 2)
            scale = base[None, :] ** power[:, None]
            scale = jnp.concatenate([scale, scale], axis=-1)
            cos, sin = (jnp.cos(freqs), jnp.sin(freqs))
            q = q * cos * scale + rotate_half(q) * sin * scale
            k = k * cos / scale + rotate_half(k) * sin / scale
            return (q, k)

        def local_attention(q, k, v):
            b, h, n, d = q.shape
            w = n // WINDOW
            bq = q.reshape(b, h, w, WINDOW, d) * QK_SCALE
            bk = k.reshape(b, h, w, WINDOW, d)
            bv = v.reshape(b, h, w, WINDOW, d)

            def look_around(t):
                p = jnp.pad(t, ((0, 0), (0, 0), (1, 0), (0, 0), (0, 0)))
                return jnp.concatenate([p[:, :, :w], p[:, :, 1:]], axis=3)
            bk, bv = (look_around(bk), look_around(bv))
            bt = jnp.arange(n).reshape(w, WINDOW)
            btp = jnp.pad(bt, ((1, 0), (0, 0)), constant_values=-1)
            btk = jnp.concatenate([btp[:w], btp[1:]], axis=1)
            sim = jnp.einsum('bhwid,bhwjd->bhwij', bq, bk)
            i = bt[:, :, None]
            j = btk[:, None, :]
            mask = (i < j) | (i > j + WINDOW) | (j == -1)
            sim = jnp.where(mask, -jnp.finfo(sim.dtype).max, sim)
            attn = jax.nn.softmax(sim, axis=-1)
            out = jnp.einsum('bhwij,bhwjd->bhwid', attn, bv)
            return out.reshape(b, h, n, d)

        def _layer(x, wqkv, qs, ksc, wo, lg, lb, w1, b1, w2, b2):
            b, n, _ = x.shape
            h = shift_token(x)
            qkv = h @ wqkv
            q, k, v = jnp.split(qkv, 3, axis=-1)
            to_heads = lambda t: t.reshape(b, n, HEADS, DIM_HEAD).transpose(0, 2, 1, 3)
            q, k, v = (to_heads(q), to_heads(k), to_heads(v))
            q = l2norm(q) * qs
            k = l2norm(k) * ksc
            q, k = rotary_xpos(q, k)
            o = local_attention(q, k, v)
            o = o.transpose(0, 2, 1, 3).reshape(b, n, INNER)
            x = x + o @ wo
            h = shift_token(x)
            mu = h.mean(-1, keepdims=True)
            var = h.var(-1, keepdims=True)
            h = (h - mu) / jnp.sqrt(var + 1e-05) * lg + lb
            h = h @ w1 + b1
            a, g = jnp.split(h, 2, axis=-1)
            h = a * jax.nn.gelu(g, approximate=False)
            x = x + h @ w2 + b2
            return x
        key = jax.random.key(seed)
        ks = jax.random.split(key, 6)
        return {'x': jax.random.normal(ks[0], (B, N, DIM), jnp.float32), 'wqkv': jax.random.normal(ks[1], (DEPTH, DIM, 3 * INNER), jnp.float32) * 0.02, 'q_scale': jnp.ones((DEPTH, DIM_HEAD), jnp.float32), 'k_scale': jnp.ones((DEPTH, DIM_HEAD), jnp.float32), 'wo': jax.random.normal(ks[2], (DEPTH, INNER, DIM), jnp.float32) * 0.02, 'ln_g': jnp.ones((DEPTH, DIM), jnp.float32), 'ln_b': jnp.zeros((DEPTH, DIM), jnp.float32), 'w1': jax.random.normal(ks[3], (DEPTH, DIM, 2 * HID), jnp.float32) * 0.02, 'b1': jnp.zeros((DEPTH, 2 * HID), jnp.float32), 'w2': jax.random.normal(ks[4], (DEPTH, HID, DIM), jnp.float32) * 0.02, 'b2': jnp.zeros((DEPTH, DIM), jnp.float32)}
    _L1_ffn_in = _L1_ffn_setup()
    _d = {'L0_attn_x': _L0_attn_in['x'], 'L0_attn_Wq': _L0_attn_in['Wq'], 'L0_attn_Wk': _L0_attn_in['Wk'], 'L0_attn_Wv': _L0_attn_in['Wv'], 'L0_ffn_gate_w': _L0_ffn_in['gate_w'], 'L0_ffn_w1': _L0_ffn_in['w1'], 'L0_ffn_b1': _L0_ffn_in['b1'], 'L0_ffn_w2': _L0_ffn_in['w2'], 'L0_ffn_b2': _L0_ffn_in['b2'], 'L0_ffn_w3': _L0_ffn_in['w3'], 'L0_ffn_b3': _L0_ffn_in['b3'], 'L0_ffn_sw1': _L0_ffn_in['sw1'], 'L0_ffn_sw2': _L0_ffn_in['sw2'], 'L0_ffn_sw3': _L0_ffn_in['sw3'], 'L1_attn_Wq': _L1_attn_in['Wq'], 'L1_attn_bq': _L1_attn_in['bq'], 'L1_attn_Wk': _L1_attn_in['Wk'], 'L1_attn_bk': _L1_attn_in['bk'], 'L1_attn_Wv': _L1_attn_in['Wv'], 'L1_attn_bv': _L1_attn_in['bv'], 'L1_attn_Wo': _L1_attn_in['Wo'], 'L1_attn_bo': _L1_attn_in['bo'], 'L1_ffn_wqkv': _L1_ffn_in['wqkv'], 'L1_ffn_q_scale': _L1_ffn_in['q_scale'], 'L1_ffn_k_scale': _L1_ffn_in['k_scale'], 'L1_ffn_wo': _L1_ffn_in['wo'], 'L1_ffn_ln_g': _L1_ffn_in['ln_g'], 'L1_ffn_ln_b': _L1_ffn_in['ln_b'], 'L1_ffn_w1': _L1_ffn_in['w1'], 'L1_ffn_b1': _L1_ffn_in['b1'], 'L1_ffn_w2': _L1_ffn_in['w2'], 'L1_ffn_b2': _L1_ffn_in['b2']}
    _x0 = _d['L0_attn_x']
    _d['L0_attn_x'] = jax.random.normal(jax.random.fold_in(jax.random.key(seed), 1), (2, 1024, 128), dtype=_x0.dtype)
    del _x0
    return _d

def reference(L0_attn_x, L0_attn_Wq, L0_attn_Wk, L0_attn_Wv, L0_ffn_gate_w, L0_ffn_w1, L0_ffn_b1, L0_ffn_w2, L0_ffn_b2, L0_ffn_w3, L0_ffn_b3, L0_ffn_sw1, L0_ffn_sw2, L0_ffn_sw3, L1_attn_Wq, L1_attn_bq, L1_attn_Wk, L1_attn_bk, L1_attn_Wv, L1_attn_bv, L1_attn_Wo, L1_attn_bo, L1_ffn_wqkv, L1_ffn_q_scale, L1_ffn_k_scale, L1_ffn_wo, L1_ffn_ln_g, L1_ffn_ln_b, L1_ffn_w1, L1_ffn_b1, L1_ffn_w2, L1_ffn_b2):

    def _L0_attn_ref(x, Wq, Wk, Wv):
        import jax, jax.numpy as jnp
        import numpy as np
        B, N = (2, 256)
        H, R = (8, 64)
        IN_DIM, OUT_DIM = (64, 64)
        D = IN_DIM + OUT_DIM
        INIT = 1.0
        b, n, d = x.shape
        Q = (x @ Wq.T).reshape(b, n, H, R)
        K = (x @ Wk.T).reshape(b, n, H, R)
        V = (x @ Wv.T).reshape(b, n, H, d)
        attn = jnp.einsum('bnhr,bmhr->bhnm', Q, K)
        attn = jax.nn.softmax(attn, axis=-1)
        out = jnp.einsum('bhnm,bmhd->bnd', attn, V)
        return out

    def _L0_ffn_ref(x, gate_w, w1, b1, w2, b2, w3, b3, sw1, sw2, sw3):
        import jax, jax.numpy as jnp
        import numpy as np
        D = 128
        H = 128
        E = 8
        K = 2
        I = 2 * 128
        ROUTE_SCALE = 1.0
        B, S, _ = x.shape
        xt = x.reshape(-1, D)
        logits = xt @ gate_w.T
        scores = jax.nn.softmax(logits.astype(jnp.float32), axis=-1)
        top_vals, idx = jax.lax.top_k(scores, K)
        weights = jnp.take_along_axis(scores, idx, axis=1).astype(x.dtype) * ROUTE_SCALE
        xs = xt[:, None, :] * weights[:, :, None]
        y = jnp.zeros_like(xt)
        for e in range(E):
            mask = (idx == e).astype(x.dtype)
            h = jax.nn.silu(jnp.einsum('tkd,hd->tkh', xs, w1[e]) + b1[e])
            x2 = jnp.einsum('tkh,dh->tkd', h, w2[e]) + b2[e]
            x3 = jnp.einsum('tkd,hd->tkh', xs, w3[e]) + b3[e]
            y = y + jnp.sum(x2 * x3 * mask[:, :, None], axis=1)
        z = jax.nn.silu(xt @ sw1.T) * (xt @ sw2.T) @ sw3.T
        return (y + z).reshape(B, S, D)

    def _L1_attn_ref(x, Wq, bq, Wk, bk, Wv, bv, Wo, bo):
        import jax, jax.numpy as jnp
        import numpy as np
        B, S, D, H = (2, 256, 128, 16)
        HD = D // H
        MAX_BIAS = 8.0

        def _alibi_bias(T, Sk, dtype):
            slopes = (2.0 ** (-MAX_BIAS / H)) ** jnp.arange(1, H + 1, dtype=dtype)
            qpos = jnp.arange(T)[:, None]
            kpos = jnp.arange(Sk)[None, :]
            rel = -jnp.abs(kpos - qpos).astype(dtype)
            return slopes[:, None, None] * rel[None]
        Bb, Ss, Dd = x.shape
        q = (x @ Wq + bq).reshape(Bb, Ss, H, HD)
        k = (x @ Wk + bk).reshape(Bb, Ss, H, HD)
        v = (x @ Wv + bv).reshape(Bb, Ss, H, HD)
        scores = jnp.einsum('bthd,bshd->bhts', q, k) / jnp.sqrt(jnp.asarray(HD, x.dtype))
        alibi = _alibi_bias(Ss, Ss, x.dtype)
        causal = jnp.triu(jnp.ones((Ss, Ss), bool), 1)
        scores = scores + alibi[None]
        scores = jnp.where(causal[None, None], -jnp.inf, scores)
        attn = jax.nn.softmax(scores, axis=-1)
        out = jnp.einsum('bhts,bshd->bthd', attn, v).reshape(Bb, Ss, Dd)
        return out @ Wo + bo

    def _L1_ffn_ref(x, wqkv, q_scale, k_scale, wo, ln_g, ln_b, w1, b1, w2, b2):
        import jax, jax.numpy as jnp
        import numpy as np
        DIM = 128
        DEPTH = 2
        HEADS = 8
        DIM_HEAD = 64
        WINDOW = 64
        INNER = HEADS * DIM_HEAD
        HID = int(DIM * 4 * 2 / 3)
        B, N = (2, 1024)
        QK_SCALE = 8.0

        def shift_token(t):
            t1, t2 = jnp.split(t, 2, axis=-1)
            t2 = jnp.pad(t2, ((0, 0), (1, 0), (0, 0)))[:, :-1]
            return jnp.concatenate([t1, t2], axis=-1)

        def l2norm(t):
            return t / jnp.clip(jnp.linalg.norm(t, axis=-1, keepdims=True), 1e-12)

        def rotate_half(x):
            x1, x2 = jnp.split(x, 2, axis=-1)
            return jnp.concatenate([-x2, x1], axis=-1)

        def rotary_xpos(q, k):
            n = q.shape[-2]
            half_idx = jnp.arange(0, DIM_HEAD, 2, dtype=jnp.float32)
            inv_freq = 1.0 / 10000.0 ** (half_idx / DIM_HEAD)
            t = jnp.arange(n, dtype=jnp.float32)
            freqs = t[:, None] * inv_freq[None, :]
            freqs = jnp.concatenate([freqs, freqs], axis=-1)
            base = (half_idx + 0.4 * DIM_HEAD) / (1.4 * DIM_HEAD)
            power = (t - n // 2) / float(WINDOW // 2)
            scale = base[None, :] ** power[:, None]
            scale = jnp.concatenate([scale, scale], axis=-1)
            cos, sin = (jnp.cos(freqs), jnp.sin(freqs))
            q = q * cos * scale + rotate_half(q) * sin * scale
            k = k * cos / scale + rotate_half(k) * sin / scale
            return (q, k)

        def local_attention(q, k, v):
            b, h, n, d = q.shape
            w = n // WINDOW
            bq = q.reshape(b, h, w, WINDOW, d) * QK_SCALE
            bk = k.reshape(b, h, w, WINDOW, d)
            bv = v.reshape(b, h, w, WINDOW, d)

            def look_around(t):
                p = jnp.pad(t, ((0, 0), (0, 0), (1, 0), (0, 0), (0, 0)))
                return jnp.concatenate([p[:, :, :w], p[:, :, 1:]], axis=3)
            bk, bv = (look_around(bk), look_around(bv))
            bt = jnp.arange(n).reshape(w, WINDOW)
            btp = jnp.pad(bt, ((1, 0), (0, 0)), constant_values=-1)
            btk = jnp.concatenate([btp[:w], btp[1:]], axis=1)
            sim = jnp.einsum('bhwid,bhwjd->bhwij', bq, bk)
            i = bt[:, :, None]
            j = btk[:, None, :]
            mask = (i < j) | (i > j + WINDOW) | (j == -1)
            sim = jnp.where(mask, -jnp.finfo(sim.dtype).max, sim)
            attn = jax.nn.softmax(sim, axis=-1)
            out = jnp.einsum('bhwij,bhwjd->bhwid', attn, bv)
            return out.reshape(b, h, n, d)

        def _layer(x, wqkv, qs, ksc, wo, lg, lb, w1, b1, w2, b2):
            b, n, _ = x.shape
            h = shift_token(x)
            qkv = h @ wqkv
            q, k, v = jnp.split(qkv, 3, axis=-1)
            to_heads = lambda t: t.reshape(b, n, HEADS, DIM_HEAD).transpose(0, 2, 1, 3)
            q, k, v = (to_heads(q), to_heads(k), to_heads(v))
            q = l2norm(q) * qs
            k = l2norm(k) * ksc
            q, k = rotary_xpos(q, k)
            o = local_attention(q, k, v)
            o = o.transpose(0, 2, 1, 3).reshape(b, n, INNER)
            x = x + o @ wo
            h = shift_token(x)
            mu = h.mean(-1, keepdims=True)
            var = h.var(-1, keepdims=True)
            h = (h - mu) / jnp.sqrt(var + 1e-05) * lg + lb
            h = h @ w1 + b1
            a, g = jnp.split(h, 2, axis=-1)
            h = a * jax.nn.gelu(g, approximate=False)
            x = x + h @ w2 + b2
            return x
        for l in range(DEPTH):
            x = _layer(x, wqkv[l], q_scale[l], k_scale[l], wo[l], ln_g[l], ln_b[l], w1[l], b1[l], w2[l], b2[l])
        return x
    x = L0_attn_x
    x = x + _layernorm(_L0_attn_ref(_layernorm(x, axis=-1), L0_attn_Wq, L0_attn_Wk, L0_attn_Wv), axis=-1)
    x = x + _layernorm(_L0_ffn_ref(_layernorm(x, axis=-1), L0_ffn_gate_w, L0_ffn_w1, L0_ffn_b1, L0_ffn_w2, L0_ffn_b2, L0_ffn_w3, L0_ffn_b3, L0_ffn_sw1, L0_ffn_sw2, L0_ffn_sw3), axis=-1)
    x = x + _layernorm(_L1_attn_ref(_layernorm(x, axis=-1), L1_attn_Wq, L1_attn_bq, L1_attn_Wk, L1_attn_bk, L1_attn_Wv, L1_attn_bv, L1_attn_Wo, L1_attn_bo), axis=-1)
    x = x + _layernorm(_L1_ffn_ref(_layernorm(x, axis=-1), L1_ffn_wqkv, L1_ffn_q_scale, L1_ffn_k_scale, L1_ffn_wo, L1_ffn_ln_g, L1_ffn_ln_b, L1_ffn_w1, L1_ffn_b1, L1_ffn_w2, L1_ffn_b2), axis=-1)
    return x

_drawn_inputs = setup_inputs


def setup_inputs(seed=0):
    import zlib

    import numpy as np

    out = dict(_drawn_inputs(seed))
    spreads = {'L1_attn_bq': (0.0, 0.422),
     'L1_attn_bk': (0.0, 2.0),
     'L1_attn_bv': (0.0, 0.1),
     'L1_attn_bo': (0.0, 0.1),
     'L1_ffn_q_scale': (1.0, 0.6),
     'L1_ffn_k_scale': (1.0, 0.6),
     'L1_ffn_ln_g': (1.0, 0.6),
     'L1_ffn_ln_b': (0.0, 0.8),
     'L1_ffn_b1': (0.0, 0.8),
     'L1_ffn_b2': (0.0, 2.0)}
    factors = {'L0_ffn_b1': 8.0, 'L0_ffn_b2': 8.0, 'L0_ffn_b3': 8.0, 'L1_ffn_w1': 8.0, 'L1_ffn_w2': 8.0}
    for name, (base, spread) in spreads.items():
        noise = np.random.default_rng([zlib.crc32(name.encode()), seed]).standard_normal(out[name].shape)
        drawn = base * np.exp(spread * noise) if base else spread * noise
        out[name] = jnp.asarray(drawn.astype(out[name].dtype))
    for name, factor in factors.items():
        out[name] = (out[name] * factor).astype(out[name].dtype)
    return out
```

```python
from contextlib import ExitStack

import concourse.bass as bass
from concourse import mybir

F32 = mybir.dt.float32
BF16 = mybir.dt.bfloat16
U32 = mybir.dt.uint32
ALU = mybir.AluOpType
ACT = mybir.ActivationFunctionType
AX_X = mybir.AxisListType.X

P = 128
D = 128
BATCH, SEQ = 2, 1024
TOK = BATCH * SEQ
TILES = TOK // P
QT = SEQ // P
CH = 512
NCH = TOK // CH
EPS = 1e-5
NEG = -1e30

H0, R0 = 8, 64
PAIRS = H0 // 2
E0, HE, I0 = 8, 128, 256
H1, HD1 = 16, 8
GROUPS = H1 // 4
STRIP = 32
DEPTH, H2, HD2, WIN = 2, 8, 64, 64
INNER = H2 * HD2
QK = 8.0
HID = int(D * 4 * 2 / 3)
ARENA = 15360
NPB = 4


class Chain:

    def __init__(self, eng, sem, base=0):
        self.eng, self.sem, self.base, self.n = eng, sem, base, 0

    def link(self, ins):
        ins.then_inc(self.sem, 1)
        self.n += 1

    def settle(self):
        self.eng.wait_ge(self.sem, self.base + self.n)

    def step(self, ins):
        self.link(ins)
        self.settle()


def build(nc, a, out, UNTIL=4):
    with ExitStack() as ctx:
        def sb(name, shape, dt=F32):
            return ctx.enter_context(nc.sbuf_tensor(name, shape, dt))

        def sem(name):
            return ctx.enter_context(nc.semaphore(name))

        x_sb = sb("x_sb", [P, TILES, D])
        xn = sb("xn", [P, TILES, D])
        xT = sb("xT", [P, TOK])
        yT = sb("yT", [P, TOK])
        ident = sb("ident", [P, P])
        stats = sb("stats", [P, TILES, 6])
        mv = sb("mv", [P, TILES, 2])
        sd = sb("sd", [P, TILES])
        rstd = sb("rstd", [P, TILES])
        eps_c = sb("eps_c", [P, 1])
        ps = ctx.enter_context(nc.psum_tensor("ps", [P, 8, CH], F32))

        q_st = sb("q_st", [P, SEQ])
        k_st = sb("k_st", [P, SEQ])
        v_st = sb("v_st", [P, QT, 256])
        probs = sb("probs", [P, NPB, SEQ])
        probsT = sb("probsT", [P, 2, QT, CH])
        negmax = sb("negmax", [P, 2 * STRIP])
        rowsum = sb("rowsum", [P, 2 * STRIP])
        rrow = sb("rrow", [P, 2 * STRIP])
        wq_st = sb("wq_st", [P, P])
        wk_st = sb("wk_st", [P, P])
        wv_st = sb("wv_st", [P, 256])
        w0q = sb("w0q", [P, PAIRS + 1, P])
        w0k = sb("w0k", [P, PAIRS + 1, P])
        w0v = sb("w0v", [P, PAIRS + 1, 256])
        wnat = probsT[:, 0, :, :].rearrange("p k (n c) -> p (k n) c", c=P)[:, 0:16, :]

        arena = sb("arena", [P, ARENA])

        def carve(at, *shape):
            n = 1
            for x in shape:
                n *= x
            v = arena[:, at:at + n]
            if len(shape) > 1:
                names = "abcd"[:len(shape)]
                v = v.rearrange(f"p ({' '.join(names)}) -> p {' '.join(names)}",
                                **{c: x for c, x in zip(names[1:], shape[1:])})
            return v, at + n

        fnat, at = carve(0, 30, P)
        gnat = sb("gnat", [STRIP, P])
        fT, at = carve(at, E0 + 1, 3, P)
        swT, at = carve(at, 6, P)
        gateT = sb("gateT", [P, E0])
        work2 = sb("work2", [P, DEPTH * 3 * INNER])
        fb = sb("fb", [P, E0 + 1, 3])
        sel_f, at = carve(at, E0, 2, P)
        sel_f = sel_f[0:STRIP]
        sel, at = carve(at, (E0 + 1) * P)
        sel = sel[0:STRIP].bitcast(BF16).rearrange("p (e n c) -> p e n c", e=E0 + 1, n=2)
        iota8 = sb("iota8", [P, TILES, E0])
        G = work2[:, 0:512].rearrange("p (t e) -> p t e", e=STRIP)
        gT = work2[0:STRIP, 512:1536].bitcast(BF16)
        e_w = work2[:, 1536:2304].rearrange("p (s n c) -> p s n c", s=2, n=3)
        e_b = sb("e_b", [P, 2, 3])
        e_sel = work2[0:STRIP, 2304:2560].bitcast(BF16).rearrange("p (s n c) -> p s n c", s=2, n=2)
        ws = probsT[:, :, :, :].rearrange("p a k c -> p (a k) c")
        e_xs, e_mask, e_h, e_t3, e_t = (ws[:, 2 * i:2 * i + 2, :] for i in range(5))
        e_sg, e_sh = ws[:, 10:12, :], ws[:, 12:14, :]
        gw = probs[:, 0, :].rearrange("p (n t e) -> p n t e", t=TILES, e=E0)
        gmax = sb("gmax", [P, TILES])
        gsum = sb("gsum", [P, TILES])
        top_i = sb("top_i", [P, TILES, E0], U32)

        nat3 = sb("nat3", [P, 3, P])
        w3 = sb("w3", [P, GROUPS + 1, 3, P])
        w3o = sb("w3o", [P, GROUPS, P])
        b3 = sb("b3", [P, GROUPS + 1, 3])
        b3o = sb("b3o", [P, 1])
        c_w = sb("c_w", [P, 3, P])
        c_b = sb("c_b", [P, 3])
        bias_y = sb("bias_y", [P, 1])
        slopes = sb("slopes", [P, H1])
        rel = sb("rel", [P, SEQ])
        sel_q = sb("sel_q", [STRIP, QT, P])
        c_sb, at = carve(0, 2, SEQ)
        c_T, at = carve(at, 4, SEQ)
        oT, at = carve(at, GROUPS, TOK)
        c_o, at = carve(at, 1, SEQ)
        c_rT = sb("c_rT", [STRIP, P])
        cmax = sb("cmax", [P, STRIP])
        c_pT = probsT[:, :, :, :].rearrange("p a k c -> p a (k c)").rearrange("p a (j k q) -> p a j k q", j=4, k=QT)

        M1 = [(0, P), (P, P), (2 * P, HID - 2 * P)]
        SUB = P // WIN
        w4qkv = work2[:, :].rearrange("p (l n) -> p l n", l=DEPTH)
        w4o = w0v[:, 0:4, :].rearrange("p s c -> p (s c)").rearrange("p (l n c) -> p l n c", l=DEPTH, c=P)
        b4 = sb("b4", [P, DEPTH, 9])
        half_c = sb("half_c", [P, 2 * H2])
        ident_b = sb("ident_b", [P, P], BF16)
        mask_b = rel[:, :].bitcast(BF16).rearrange("p (t c) -> p t c", c=P)
        rot_c, at = carve(0, TILES, 2, HD2)
        rot_s, at = carve(at, TILES, 2, HD2)
        base_c, at = carve(at, QT, 2, HD2)
        base_s, at = carve(at, QT, 2, HD2)
        mask_f, at = carve(at, 2, P)
        hT, at = carve(at, WIN + TOK)
        l_qkv, at = carve(at, 3 * INNER)
        l_o, at = carve(at, 4, P)
        l_up, at = carve(at, 2 * HID)
        l_down, at = carve(at, 3, P)
        w4up, at = carve(at, DEPTH, 2 * HID)
        w4down, at = carve(at, DEPTH, 3, P)
        qk_scale, at = carve(at, DEPTH, 2, HD2)
        hq, at = carve(at, 2, P)
        hv, at = carve(at, 2, P + WIN)
        assert at <= ARENA
        l_b = sb("l_b", [P, 9])
        ss = sb("ss", [P, 2, 2 * H2])
        d_nm = sb("d_nm", [P, 2, H2])
        d_nm8 = sb("d_nm8", [P, 2, H2])
        d_sum = sb("d_sum", [P, 2, H2])
        d_rr = sb("d_rr", [P, 2, H2])
        d_mA = probs[:, 0:2, :]
        d_mB = probs[:, 2:4, :]
        gbuf = probs[:, :, :].rearrange("p n c -> p (n c)")[:, 0:2 * 3 * CH]\
            .rearrange("p (n m c) -> p n m c", n=2, m=3)
        d_kq = [q_st[:, :], k_st[:, :]]
        d_sq = v_st[:, :, :].rearrange("p a b -> p (a b)").rearrange("p (n c) -> p n c", n=2)
        pf = probsT[:, :, :, :].rearrange("p a k c -> p (a k c)")
        d_p = pf[:, 0:2048].rearrange("p (n h c) -> p n h c", n=2, h=H2)
        d_pT = pf[:, 2048:3072].rearrange("p (h c) -> p h c", h=H2)
        d_kT = pf[:, 3072:4096].rearrange("p (n m c) -> p n m c", n=2, m=4)
        d_qT = pf[:, 4096:4608].rearrange("p (m c) -> p m c", m=4)
        d_o = pf[:, 4608:5632].rearrange("p (n m c) -> p n m c", n=2, m=4)
        d_va = pf[:, 5632:6656].rearrange("p (n c) -> p n c", n=2)
        d_vs = pf[:, 6656:7680].rearrange("p (n c) -> p n c", n=2)

        s_ld_x = sem("s_ld_x")
        s_ld_w0 = sem("s_ld_w0")
        s_ld_f = sem("s_ld_f")
        s_ld_c = sem("s_ld_c")
        s_ld_z = sem("s_ld_z")
        s_out = sem("s_out")
        s_eps = sem("s_eps")
        s_var = sem("s_var")
        s_sd = sem("s_sd")
        s_xn = sem("s_xn")
        s_xTp = sem("s_xTp")
        s_xT = sem("s_xT")
        s_yp = sem("s_yp")
        s_dve = sem("s_dve")
        s_res = sem("s_res")
        s_y = [sem(f"s_y{n}") for n in range(4)]
        s_w0p = sem("s_w0p")
        s_w0t = sem("s_w0t")
        s_a_wst = sem("s_a_wst")
        s_a_projq = sem("s_a_projq")
        s_a_projk = sem("s_a_projk")
        s_a_projv0 = sem("s_a_projv0")
        s_a_projv1 = sem("s_a_projv1")
        s_a_q = sem("s_a_q")
        s_a_k = sem("s_a_k")
        s_a_v0 = sem("s_a_v0")
        s_a_v1 = sem("s_a_v1")
        s_a_scores = sem("s_a_scores")
        s_a_negmax = sem("s_a_negmax")
        s_a_exp = sem("s_a_exp")
        s_a_rrow = sem("s_a_rrow")
        s_a_norm = sem("s_a_norm")
        s_a_trans = sem("s_a_trans")
        s_a_evA = sem("s_a_evA")
        s_a_evB = sem("s_a_evB")
        s_a_pv = sem("s_a_pv")
        s_a_oadd = sem("s_a_oadd")
        s_a_ozero = sem("s_a_ozero")
        s_fp = sem("s_fp")
        s_ft = sem("s_ft")
        s_selc = sem("s_selc")
        s_logits = sem("s_logits")
        s_gshift = sem("s_gshift")
        s_gexp = sem("s_gexp")
        s_G = sem("s_G")
        s_gTp = sem("s_gTp")
        s_gT = sem("s_gT")
        s_sh_g = sem("s_sh_g")
        s_sh_u = sem("s_sh_u")
        s_sh_silu = sem("s_sh_silu")
        s_sh_h = sem("s_sh_h")
        s_sh_z = sem("s_sh_z")
        s_sh_y = sem("s_sh_y")
        s_e_wA = sem("s_e_wA")
        s_e_wB = sem("s_e_wB")
        s_e_bc = sem("s_e_bc")
        s_e_xs = sem("s_e_xs")
        s_e_mask = sem("s_e_mask")
        s_e_h1 = sem("s_e_h1")
        s_e_x3 = sem("s_e_x3")
        s_e_h = sem("s_e_h")
        s_e_t3 = sem("s_e_t3")
        s_e_x2 = sem("s_e_x2")
        s_e_t = sem("s_e_t")
        s_e_y = sem("s_e_y")
        s_c_wst = sem("s_c_wst")
        s_c_pad = sem("s_c_pad")
        s_c_go = sem("s_c_go")
        s_c_projq = sem("s_c_projq")
        s_c_projk = sem("s_c_projk")
        s_c_projv = sem("s_c_projv")
        s_c_q = sem("s_c_q")
        s_c_k = sem("s_c_k")
        s_c_v = sem("s_c_v")
        s_c_T = sem("s_c_T")
        s_c_scores = sem("s_c_scores")
        s_c_bias = sem("s_c_bias")
        s_c_negmax = sem("s_c_negmax")
        s_c_exp = sem("s_c_exp")
        s_c_transA = sem("s_c_transA")
        s_c_transB = sem("s_c_transB")
        s_c_evA = sem("s_c_evA")
        s_c_evB = sem("s_c_evB")
        s_c_pv = sem("s_c_pv")
        s_c_o = sem("s_c_o")
        s_c_rr = sem("s_c_rr")
        s_c_rrp = sem("s_c_rrp")
        s_c_rT = sem("s_c_rT")
        s_c_bc = sem("s_c_bc")
        s_c_oT = sem("s_c_oT")
        s_c_bp = sem("s_c_bp")
        s_c_by = sem("s_c_by")
        s_c_y = sem("s_c_y")
        s_c_yc = sem("s_c_yc")
        s_ld_d = sem("s_ld_d")
        s_ld_r = sem("s_ld_r")
        s_d_wst = sem("s_d_wst")
        s_d_hT = sem("s_d_hT")
        s_d_hq = sem("s_d_hq")
        s_d_hv = sem("s_d_hv")
        s_d_qkp = sem("s_d_qkp")
        s_d_vp = sem("s_d_vp")
        s_d_m = sem("s_d_m")
        s_d_sq = sem("s_d_sq")
        s_d_ss = sem("s_d_ss")
        s_d_cl = sem("s_d_cl")
        s_d_rn = sem("s_d_rn")
        s_d_add = sem("s_d_add")
        s_d_kq = sem("s_d_kq")
        s_d_qkt = sem("s_d_qkt")
        s_d_qT = sem("s_d_qT")
        s_d_kT = sem("s_d_kT")
        s_d_v = sem("s_d_v")
        s_d_s = sem("s_d_s")
        s_d_nm = sem("s_d_nm")
        s_d_nm8 = sem("s_d_nm8")
        s_d_e = sem("s_d_e")
        s_d_rr = sem("s_d_rr")
        s_d_p = sem("s_d_p")
        s_d_pt = sem("s_d_pt")
        s_d_pT = sem("s_d_pT")
        s_d_o = sem("s_d_o")
        s_d_oT = sem("s_d_oT")
        s_d_w = sem("s_d_w")
        s_d_z = sem("s_d_z")
        s_d_chain = sem("s_d_chain")
        s_f_hT = sem("s_f_hT")
        s_f_go = sem("s_f_go")
        s_f_hp = sem("s_f_hp")
        s_f_var = sem("s_f_var")
        s_f_sd = sem("s_f_sd")
        s_f_xn = sem("s_f_xn")
        s_f_xp = sem("s_f_xp")
        s_f_yT = sem("s_f_yT")
        s_f_g = sem("s_f_g")
        s_f_a = sem("s_f_a")
        s_f_ge = sem("s_f_ge")
        s_f_u = sem("s_f_u")
        s_f_y = sem("s_f_y")
        s_f_z = sem("s_f_z")
        s_d_init = sem("s_d_init")


        block = ctx.enter_context(nc.Block())

        @block.sync
        def _(sp):
            for b in range(BATCH):
                sp.dma_start(x_sb[:, b * QT:(b + 1) * QT, :],
                             a["L0_attn_x"][b].rearrange("(t p) d -> p t d", p=P)).then_inc(s_ld_x, 16)
            sp.dma_start(ident[:, :], a["c_ident"]).then_inc(s_ld_w0, 16)
            sp.dma_start(wnat[:, 0:4, :], a["L0_attn_Wq"].rearrange("(n p) d -> p n d", p=P)).then_inc(s_ld_w0, 16)
            sp.dma_start(wnat[:, 4:8, :], a["L0_attn_Wk"].rearrange("(n p) d -> p n d", p=P)).then_inc(s_ld_w0, 16)
            sp.dma_start(wnat[:, 8:16, :], a["L0_attn_Wv"].rearrange("(n p) d -> p n d", p=P)).then_inc(s_ld_w0, 16)
            for i, w in enumerate(("L0_ffn_w1", "L0_ffn_w2", "L0_ffn_w3")):
                sp.dma_start(fnat[:, 8 * i:8 * i + 8, :], a[w].rearrange("e h d -> h e d")).then_inc(s_ld_f, 16)
            sp.dma_start(fnat[:, 24:26, :], a["L0_ffn_sw1"].rearrange("(n p) d -> p n d", p=P)).then_inc(s_ld_f, 16)
            sp.dma_start(fnat[:, 26:28, :], a["L0_ffn_sw2"].rearrange("(n p) d -> p n d", p=P)).then_inc(s_ld_f, 16)
            sp.dma_start(fnat[:, 28:30, :], a["L0_ffn_sw3"].rearrange("d (n i) -> d n i", n=2)).then_inc(s_ld_f, 16)
            for i, w in enumerate(("L0_ffn_gate_w", "L0_ffn_b1", "L0_ffn_b2", "L0_ffn_b3")):
                sp.dma_start(gnat[8 * i:8 * i + 8, :], a[w]).then_inc(s_ld_f, 16)
            sp.dma_start(sel_f[:, :, :, :], a["c_sel"]).then_inc(s_ld_f, 16)
            sp.dma_start(iota8[:, :, :], a["c_iota8"]).then_inc(s_ld_f, 16)
            for i, w in enumerate(("L1_attn_Wq", "L1_attn_Wk", "L1_attn_Wv")):
                sp.dma_start(nat3[:, i, :], a[w]).then_inc(s_ld_c, 16)
            sp.dma_start(slopes[:, :], a["c_slopes"]).then_inc(s_ld_c, 16)
            sp.dma_start(rel[:, :], a["c_rel"]).then_inc(s_ld_c, 16)
            sp.dma_start(sel_q[:, :, :], a["c_selq"]).then_inc(s_ld_c, 16)
            sp.dma_start(b3o[:, :], a["L1_attn_bo"].rearrange("(d o) -> d o", o=1)).then_inc(s_ld_c, 16)
            sp.wait_ge(s_ld_z, 1)
            for j in range(4):
                r = STRIP * j
                sp.dma_start(w3o[r:r + HD1, :, :],
                             a["L1_attn_Wo"].rearrange("(g j e) o -> j e g o", j=4, e=HD1)[j]).then_inc(s_ld_c, 16)
                for i, w in enumerate(("L1_attn_bq", "L1_attn_bk", "L1_attn_bv")):
                    sp.dma_start(b3[r:r + HD1, 0:GROUPS, i],
                                 a[w].rearrange("(g j e) -> j e g", j=4, e=HD1)[j],
                                 allow_slow_non_contiguous=True).then_inc(s_ld_c, 16)
            sp.wait_ge(s_y[1], 1)
            sp.dma_start(w4qkv[:, :, :], a["L1_ffn_wqkv"].rearrange("l d n -> d l n")).then_inc(s_ld_d, 16)
            sp.dma_start(w4o, a["L1_ffn_wo"].rearrange("l (n p) d -> p l n d", p=P)).then_inc(s_ld_d, 16)
            sp.wait_ge(s_y[2], 1)
            sp.dma_start(base_c, a["c_rotc"].rearrange("(t p) n d -> p t n d", p=P)).then_inc(s_ld_r, 16)
            sp.dma_start(base_s, a["c_rots"].rearrange("(t p) n d -> p t n d", p=P)).then_inc(s_ld_r, 16)
            sp.dma_start(mask_f, a["c_mask"]).then_inc(s_ld_r, 16)
            sp.dma_start(w4up[:, :, :], a["L1_ffn_w1"].rearrange("l d n -> d l n")).then_inc(s_ld_d, 16)
            for l in range(DEPTH):
                for m, (r, n) in enumerate(M1):
                    sp.dma_start(w4down[0:n, l, m, :], a["L1_ffn_w2"][l, r:r + n, :]).then_inc(s_ld_d, 16)
                    for part in range(2):
                        sp.dma_start(b4[0:n, l, 3 * part + m:3 * part + m + 1],
                                     a["L1_ffn_b1"][l, HID * part + r:HID * part + r + n]
                                     .rearrange("(d o) -> d o", o=1)).then_inc(s_ld_d, 16)
                for m, w in enumerate(("L1_ffn_b2", "L1_ffn_ln_g", "L1_ffn_ln_b")):
                    sp.dma_start(b4[:, l, 6 + m:7 + m], a[w][l].rearrange("(d o) -> d o", o=1)).then_inc(s_ld_d, 16)
                for m, w in enumerate(("L1_ffn_q_scale", "L1_ffn_k_scale")):
                    sp.dma_start(qk_scale[:, l, m, :], a[w][l].partition_broadcast(P)).then_inc(s_ld_d, 16)
            sp.wait_ge(s_res, UNTIL)
            for b in range(BATCH):
                sp.dma_start(out[b].rearrange("(t p) d -> p t d", p=P),
                             x_sb[:, b * QT:(b + 1) * QT, :]).then_inc(s_out, 16)
            sp.wait_ge(s_out, 16 * BATCH)

        NU = 16

        def exists(t, shift):
            return not isinstance(t, int) or 0 <= t + shift < TILES

        def walk(eng, step, last):
            step(0, 0)
            step(1, 1)
            with eng.Fori(1, 6) as i:
                step(2 * i, 0)
                step(2 * i + 1, 1)
            for t in range(12, last):
                step(t, t % 2)

        @block.tensor
        def _(pe):
            def norm_in(k):
                for g in range(NCH):
                    pe.wait_ge(s_xn, NCH * k + g + 1)
                    for i in range(4):
                        ins = pe.transpose(ps[:, g, i * P:(i + 1) * P], xn[:, 4 * g + i, :], ident[:, :])
                    ins.then_inc(s_xTp, 1)

            def norm_out(k, src=yT):
                for g in range(NCH):
                    for i in range(4):
                        t = 4 * g + i
                        ins = pe.transpose(ps[:, g, i * P:(i + 1) * P], src[:, t * P:(t + 1) * P], ident[:, :])
                    ins.then_inc(s_yp, 1)

            pe.wait_ge(s_ld_w0, 16 * 4)
            for g in range(4):
                for i in range(4):
                    ins = pe.transpose(ps[:, 4 + g, i * P:(i + 1) * P], wnat[:, 4 * g + i, :], ident[:, :])
                ins.then_inc(s_w0p, 1)
            norm_in(0)
            pe.wait_ge(s_ld_f, 16 * 12)
            for g in range(9):
                if g < 4:
                    pe.wait_ge(s_w0t, 1)
                else:
                    pe.wait_ge(s_ft, g - 3)
                if g == 8:
                    ins = pe.transpose(ps[:, 4, 0:STRIP], gnat[:, :], ident[0:STRIP, 0:STRIP])
                else:
                    for i in range(min(4, 30 - 4 * g)):
                        ins = pe.transpose(ps[:, 4 + g % 4, i * P:(i + 1) * P], fnat[:, 4 * g + i, :], ident[:, :])
                ins.then_inc(s_fp, 1)

            def a_proj_q(b):
                for n in range(2):
                    ins = pe.matmul(ps[:, n, :], wq_st[:, :], xT[:, b * SEQ + n * CH:b * SEQ + (n + 1) * CH],
                                    start=True, stop=True)
                ins.then_inc(s_a_projq, 1)

            def a_proj_k(b):
                for n in range(2):
                    ins = pe.matmul(ps[:, 2 + n, :], wk_st[:, :], xT[:, b * SEQ + n * CH:b * SEQ + (n + 1) * CH],
                                    start=True, stop=True)
                ins.then_inc(s_a_projk, 1)

            def a_proj_v(b, m):
                pe.wait_ge(s_a_q, m)
                for half, done in ((0, s_a_projv0), (1, s_a_projv1)):
                    if half:
                        pe.wait_ge(s_a_k, m)
                    for i in range(4):
                        kt = 4 * half + i
                        t = b * QT + kt
                        ins = pe.matmul(ps[:, kt // 2, (kt % 2) * 256:(kt % 2) * 256 + 256],
                                        xT[:, t * P:(t + 1) * P], wv_st[:, :], start=True, stop=True)
                    ins.then_inc(done, 1)

            pe.wait_ge(s_xT, NCH)
            pe.wait_ge(s_a_wst, 1)
            a_proj_q(0)
            a_proj_k(0)
            a_proj_v(0, 1)

            with pe.Fori(0, PAIRS) as p:
                for b in range(BATCH):
                    n0 = 2 * NU * p + NU * b
                    m = 2 * p + b

                    def scores(u):
                        r, qt = R0 * (u // QT), u % QT
                        if u == 0:
                            pe.wait_ge(s_a_q, m + 1)
                            pe.wait_ge(s_a_k, m + 1)
                            pe.wait_ge(s_a_v0, m + 1)
                        elif u == 1:
                            pe.wait_ge(s_a_v1, m + 1)
                        else:
                            pe.wait_ge(s_a_exp, n0 + u - 1)
                        for n in range(2):
                            ins = pe.matmul(ps[:, 2 * (u % 2) + n, :], q_st[r:r + R0, qt * P:(qt + 1) * P],
                                            k_st[r:r + R0, n * CH:(n + 1) * CH], start=True, stop=True)
                        ins.then_inc(s_a_scores, 1)

                    def turn(u):
                        pe.wait_ge(s_a_norm, n0 + u + 1)
                        for half, free in ((0, s_a_evA), (1, s_a_evB)):
                            pe.wait_ge(free, n0 + u + 1)
                            for i in range(4):
                                kt = 4 * half + i
                                ins = pe.transpose(ps[:, 4 + half, i * P:(i + 1) * P],
                                                   probs[:, u % NPB, kt * P:(kt + 1) * P], ident[:, :])
                            ins.then_inc(s_a_trans, 1)

                    def weigh(c, k0, k1):
                        head, qc = c // 2, c % 2
                        if k0 == 0:
                            pe.wait_ge(s_a_evA, n0 + 4 * c + 5)
                            pe.wait_ge(s_a_evB, n0 + 4 * c + 5)
                            if head == 0:
                                pe.wait_ge(s_a_oadd, 2 * m + 1)
                        for kt in range(k0, k1):
                            ins = pe.matmul(ps[:, 6 + qc, :], v_st[:, kt, head * P:(head + 1) * P],
                                            probsT[:, c % 2, kt, :], start=(head == 0 and kt == 0),
                                            stop=(head == 1 and kt == QT - 1), skip_group_check=True)
                        if head == 1 and k1 == QT:
                            ins.then_inc(s_a_pv, 1)

                    for u in range(NU):
                        scores(u)
                        if u >= 2:
                            turn(u - 2)
                        if u >= 6:
                            c, k = (u - 6) // 4, (u - 6) % 4
                            weigh(c, 2 * k, 2 * k + 2)
                    nb = 1 - b
                    if b == 1:
                        pe.wait_ge(s_a_wst, p + 2)
                    pe.wait_ge(s_a_exp, n0 + NU - 1)
                    a_proj_q(nb)
                    turn(NU - 2)
                    weigh(2, 4, 6)
                    pe.wait_ge(s_a_exp, n0 + NU)
                    a_proj_k(nb)
                    turn(NU - 1)
                    weigh(2, 6, 8)
                    weigh(3, 0, 8)
                    a_proj_v(nb, m + 2)

            pe.wait_ge(s_y[0], 1)
            pe.wait_ge(s_a_v0, 2 * PAIRS + 1)
            pe.wait_ge(s_a_v1, 2 * PAIRS + 1)
            norm_out(0)

            norm_in(1)
            pe.wait_ge(s_xT, NCH * 2)
            pe.wait_ge(s_ft, 9)
            for t in range(TILES):
                ins = pe.matmul(ps[:, 7, t * E0:(t + 1) * E0], xT[:, t * P:(t + 1) * P], gateT[:, :],
                                start=True, stop=True)
            ins.then_inc(s_logits, 1)

            def shared_down(k):
                c, m = k // 2, k % 2
                pe.wait_ge(s_sh_h, k + 1)
                if m == 0 and c >= 2:
                    pe.wait_ge(s_sh_y, c - 1)
                ins = pe.matmul(ps[:, 4 + c % 2, :], swT[:, 4 + m, :], e_sh[:, k % 2, :],
                                start=(m == 0), stop=(m == 1))
                if m == 1:
                    ins.then_inc(s_sh_z, 1)

            for k in range(2 * NCH):
                c, m = k // 2, k % 2
                x = xT[:, c * CH:(c + 1) * CH]
                if k >= 2:
                    pe.wait_ge(s_sh_silu, k - 1)
                    pe.wait_ge(s_sh_h, k - 1)
                pe.matmul(ps[:, k % 2, :], swT[:, m, :], x, start=True, stop=True).then_inc(s_sh_g, 1)
                pe.matmul(ps[:, 2 + k % 2, :], swT[:, 2 + m, :], x, start=True, stop=True).then_inc(s_sh_u, 1)
                if k >= 1:
                    shared_down(k - 1)
            shared_down(2 * NCH - 1)
            pe.wait_ge(s_G, 1)
            for g in range(NCH):
                if g >= 2:
                    pe.wait_ge(s_gT, g - 1)
                for i in range(4):
                    ins = pe.transpose(ps[0:STRIP, 6 + g % 2, i * P:(i + 1) * P], G[:, 4 * g + i, :], ident[:, :])
                ins.then_inc(s_gTp, 1)

            pe.wait_ge(s_gT, NCH)
            pe.wait_ge(s_sh_y, NCH)
            with pe.Fori(0, E0 // 2) as i:
                n0 = 2 * NCH * i

                def spread(k):
                    s, c = k // NCH, k % NCH
                    if k == 0:
                        pe.wait_ge(s_e_wA, i + 1)
                    if k == NCH:
                        pe.wait_ge(s_e_wB, i + 1)
                    if k >= 2:
                        pe.wait_ge(s_e_xs, n0 + k - 1)
                    if k >= 1:
                        pe.wait_ge(s_e_mask, n0 + k)
                    g = gT[:, c * CH:(c + 1) * CH]
                    pe.matmul(ps[:, k % 2, :], e_sel[:, s, 0, :], g, start=True, stop=True)
                    pe.matmul(ps[:, 2, :], e_sel[:, s, 1, :], g, start=True, stop=True).then_inc(s_e_bc, 1)

                def down(k):
                    pe.wait_ge(s_e_h, n0 + k + 1)
                    if k >= 1:
                        pe.wait_ge(s_e_t, n0 + k)
                    pe.matmul(ps[:, 7, :], e_w[:, k // NCH, 2, :], e_h[:, k % 2, :],
                              start=True, stop=True).then_inc(s_e_x2, 1)

                spread(0)
                for k in range(2 * NCH):
                    s = k // NCH
                    pe.wait_ge(s_e_xs, n0 + k + 1)
                    pe.matmul(ps[:, 3 + k % 2, :], e_w[:, s, 0, :], e_xs[:, k % 2, :],
                              start=True, stop=True).then_inc(s_e_h1, 1)
                    if k < 2 * NCH - 1:
                        spread(k + 1)
                    if k >= 2:
                        pe.wait_ge(s_e_t3, n0 + k - 1)
                    pe.matmul(ps[:, 5 + k % 2, :], e_w[:, s, 1, :], e_xs[:, k % 2, :],
                              start=True, stop=True).then_inc(s_e_x3, 1)
                    if k >= 1:
                        down(k - 1)
                down(2 * NCH - 1)
            pe.wait_ge(s_y[1], 1)
            norm_out(1)

            norm_in(2)

            def c_proj_q(b):
                for n in range(2):
                    ins = pe.matmul(ps[:, n, :], c_w[:, 0, :], xT[:, b * SEQ + n * CH:b * SEQ + (n + 1) * CH],
                                    start=True, stop=True)
                ins.then_inc(s_c_projq, 1)

            def c_proj_k(b):
                for n in range(2):
                    ins = pe.matmul(ps[:, 2 + n, :], c_w[:, 1, :], xT[:, b * SEQ + n * CH:b * SEQ + (n + 1) * CH],
                                    start=True, stop=True)
                ins.then_inc(s_c_projk, 1)

            def c_proj_v(b, m):
                pe.wait_ge(s_c_q, m)
                for kt in range(QT):
                    t = b * QT + kt
                    ins = pe.matmul(ps[:, kt // 4, (kt % 4) * P:(kt % 4 + 1) * P], xT[:, t * P:(t + 1) * P],
                                    c_w[:, 2, :], start=True, stop=True)
                ins.then_inc(s_c_projv, 1)

            pe.wait_ge(s_xT, NCH * 3)
            pe.wait_ge(s_c_wst, 1)
            pe.wait_ge(s_ld_c, 16 * 23)
            for g in range(GROUPS):
                ins = pe.matmul(ps[:, 4, 0:1], w3o[:, g, :], b3[:, g, 2:3], start=(g == 0), stop=(g == GROUPS - 1))
            ins.then_inc(s_c_bp, 1)
            c_proj_q(0)
            c_proj_k(0)
            c_proj_v(0, 1)
            pe.wait_ge(s_c_by, 1)
            CU = 4 * QT
            with pe.Fori(0, GROUPS) as g:
                for b in range(BATCH):
                    n0 = 2 * CU * g + CU * b
                    m = 2 * g + b
                    h0 = CU // 2 * m

                    def scores(u):
                        r, qt = STRIP * (u % 4), u // 4
                        if u == 0:
                            pe.wait_ge(s_c_q, m + 1)
                            pe.wait_ge(s_c_v, m + 1)
                            pe.wait_ge(s_c_k, m + 1)
                        if u >= 2:
                            pe.wait_ge(s_c_bias, n0 + u - 1)
                        w = (qt + 1) * P
                        for n in range((w + CH - 1) // CH):
                            e = min(w, (n + 1) * CH)
                            ins = pe.matmul(ps[:, 2 * (u % 2) + n, 0:e - n * CH],
                                            q_st[r:r + STRIP, qt * P:(qt + 1) * P],
                                            k_st[r:r + STRIP, n * CH:e], start=True, stop=True)
                        ins.then_inc(s_c_scores, 1)

                    def turn(u):
                        qt = u // 4
                        pe.wait_ge(s_c_exp, n0 + u + 1)
                        pe.wait_ge(s_c_evA, n0 + u + 1)
                        for kt in range(min(4, qt + 1)):
                            ins = pe.transpose(ps[:, 4, kt * P:(kt + 1) * P],
                                               probs[:, u % NPB, kt * P:(kt + 1) * P], ident[:, :])
                        ins.then_inc(s_c_transA, 1)
                        if qt >= 4:
                            pe.wait_ge(s_c_evB, h0 + u - CU // 2 + 1)
                            for kt in range(4, qt + 1):
                                ins = pe.transpose(ps[:, 5, (kt - 4) * P:(kt - 3) * P],
                                                   probs[:, u % NPB, kt * P:(kt + 1) * P], ident[:, :])
                            ins.then_inc(s_c_transB, 1)

                    def weigh(qt):
                        pe.wait_ge(s_c_evA, n0 + 4 * qt + 5)
                        if qt >= 4:
                            pe.wait_ge(s_c_evB, h0 + 4 * (qt - 4) + 5)
                        pe.wait_ge(s_c_o, QT * m + qt + 1)
                        if qt < 2:
                            pe.wait_ge(s_c_oT, m + 1)
                        for kt in range(qt + 1):
                            for j in range(4):
                                ins = pe.matmul(ps[STRIP * j:STRIP * j + STRIP, 6 + qt % 2, 0:P],
                                                v_st[:, kt, STRIP * j:STRIP * j + STRIP],
                                                c_pT[:, qt % 2, j, kt, :], start=(kt == 0), stop=(kt == qt),
                                                tile_position=(0, STRIP * j))
                        ins.then_inc(s_c_pv, 1)

                    for u in range(CU):
                        scores(u)
                        if u >= 3:
                            turn(u - 3)
                        if u >= 7 and u % 4 == 3:
                            weigh((u - 7) // 4)
                    if b == 1:
                        pe.wait_ge(s_c_wst, g + 2)
                    pe.wait_ge(s_c_bias, n0 + CU - 1)
                    c_proj_q(1 - b)
                    turn(CU - 3)
                    turn(CU - 2)
                    pe.wait_ge(s_c_bias, n0 + CU)
                    c_proj_k(1 - b)
                    turn(CU - 1)
                    weigh(QT - 1)
                    pe.wait_ge(s_c_rr, m + 1)
                    pe.wait_ge(s_c_evA, n0 + CU + 1)
                    pe.transpose(ps[0:STRIP, 4, 0:P], rrow[:, 0:CU], ident[:, :]).then_inc(s_c_rrp, 1)
                    c_proj_v(1 - b, m + 2)
                    pe.wait_ge(s_c_rT, m + 1)
                    pe.wait_ge(s_c_o, QT * (m + 1) + 2)
                    for qt in range(QT):
                        ins = pe.matmul(ps[:, 6 + qt // 4, (qt % 4) * P:(qt % 4 + 1) * P], sel_q[:, qt, :],
                                        c_rT[:, :], start=True, stop=True)
                    ins.then_inc(s_c_bc, 1)

            pe.wait_ge(s_c_oT, 2 * GROUPS + 1)
            for c in range(NCH):
                for g in range(GROUPS):
                    ins = pe.matmul(ps[:, 4 + c, :], w3o[:, g, :], oT[:, g, c * CH:(c + 1) * CH],
                                    start=(g == 0), stop=(g == GROUPS - 1))
                ins.then_inc(s_c_y, 1)
            pe.wait_ge(s_c_yc, NCH)
            pe.wait_ge(s_c_v, 2 * GROUPS + 1)
            pe.wait_ge(s_c_k, 2 * GROUPS + 1)
            norm_out(2)

            norm_in(3)
            pe.wait_ge(s_d_init, 1)
            with pe.Fori(0, DEPTH) as l:
                T0 = TILES * l

                def proj_qk(t, par):
                    n = T0 + t
                    pe.wait_ge(s_d_hq, n + 1)
                    if exists(t, -1):
                        pe.wait_ge(s_d_m, n)
                        pe.wait_ge(s_d_sq, n)
                    for i in range(2):
                        ins = pe.matmul(ps[:, i, :], hq[:, par, :], l_qkv[:, i * INNER:(i + 1) * INNER],
                                        start=True, stop=True)
                    ins.then_inc(s_d_qkp, 1)

                def step(t, par):
                    n = T0 + t
                    if exists(t, 0):
                        pe.wait_ge(s_d_kq, n + 1)
                        if exists(t, -2):
                            pe.wait_ge(s_d_pT, n - 1)
                        for i in range(2 * 4):
                            ins = pe.transpose(ps[:, 4 + i // 4, (i % 4) * P:(i % 4 + 1) * P],
                                               d_kq[par][:, i * P:(i + 1) * P], ident[:, :])
                        ins.then_inc(s_d_qkt, 1)
                    if exists(t, 2):
                        proj_qk(t + 2, par)
                    if exists(t, 0):
                        pe.wait_ge(s_d_hv, n + 1)
                        if exists(t, -2):
                            pe.wait_ge(s_d_oT, n - 1)
                        elif exists(t, -1):
                            pe.wait_ge(s_d_v, n)
                        pe.matmul(ps[:, 2, :], hv[:, par, WIN:WIN + P], l_qkv[:, 2 * INNER:3 * INNER],
                                  start=True, stop=True)
                        pe.matmul(ps[:, 3, :], hv[:, par, 0:P], l_qkv[:, 2 * INNER:3 * INNER],
                                  start=True, stop=True).then_inc(s_d_vp, 1)
                        pe.wait_ge(s_d_qT, n + 1)
                        pe.wait_ge(s_d_kT, n + 1)
                    if exists(t, -1):
                        pe.wait_ge(s_d_p, n)
                        for h in range(H2):
                            ins = pe.transpose(ps[:, 4 + h // 4, (h % 4) * P:(h % 4 + 1) * P],
                                               d_p[:, 1 - par, h, :], ident[:, :])
                        ins.then_inc(s_d_pt, 1)
                    if exists(t, 0):
                        if exists(t, -1):
                            pe.wait_ge(s_d_e, n)
                        for i in range(2):
                            pe.matmul(ps[:, 6 + i, :].rearrange("p (h c) -> p h c", c=P), ident_b[:, :],
                                      mask_b[:, bass.ds(t, 1), :].to_broadcast([P, 4, P]),
                                      start=True, stop=False, skip_group_check=True)
                        for h in range(H2):
                            r, m = HD2 * (h % 2), h // 2
                            o = ps[:, 6 + h % 2, m * P:(m + 1) * P]
                            pe.matmul(o[0:WIN, 0:WIN], d_qT[r:r + HD2, m, 0:WIN], d_kT[r:r + HD2, 1 - par, m, WIN:P],
                                      start=False, stop=False, skip_group_check=True)
                            pe.matmul(o[0:WIN, WIN:P], d_qT[r:r + HD2, m, 0:WIN], d_kT[r:r + HD2, par, m, 0:WIN],
                                      start=False, stop=False, skip_group_check=True)
                            ins = pe.matmul(o[WIN:P, :], d_qT[r:r + HD2, m, WIN:P], d_kT[r:r + HD2, par, m, :],
                                            start=False, stop=True, skip_group_check=True)
                        ins.then_inc(s_d_s, 1)
                    if exists(t, -2):
                        pe.wait_ge(s_d_oT, n - 1)
                        if exists(t, 0):
                            pe.wait_ge(s_d_v, n + 1)
                        elif t == TILES + 1:
                            pe.wait_ge(s_d_z, n - 2)
                        for m in range(4):
                            ins = pe.matmul(ps[:, 3, 0:P], l_o[:, m, :], d_o[:, par, m, :],
                                            start=(m == 0), stop=(m == 3))
                        ins.then_inc(s_d_w, 1)
                    if exists(t, -1):
                        pe.wait_ge(s_d_pT, n)
                        if exists(t, 0):
                            pe.wait_ge(s_d_v, n + 1)
                        elif exists(t, -2):
                            pe.wait_ge(s_d_oT, n - 1)
                        for h in range(H2):
                            r, m = HD2 * (h % 2), h // 2
                            for i, v in enumerate((d_vs, d_va)):
                                ins = pe.matmul(ps[r:r + HD2, 2, m * P + i * WIN:m * P + (i + 1) * WIN],
                                                v[:, 1 - par, h * HD2:(h + 1) * HD2],
                                                d_pT[:, 4 * (h % 2) + m, i * WIN:(i + 1) * WIN], start=True, stop=True,
                                                skip_group_check=True)
                        ins.then_inc(s_d_o, 1)

                pe.wait_ge(s_d_wst, l + 1)
                proj_qk(0, 0)
                proj_qk(1, 1)
                walk(pe, step, TILES + 2)

                pe.wait_ge(s_f_hT, l + 1)
                for g in range(NCH):
                    for i in range(4):
                        t = 4 * g + i
                        ins = pe.transpose(ps[:, g, i * P:(i + 1) * P], hT[:, WIN + t * P:WIN + (t + 1) * P],
                                           ident[:, :])
                    ins.then_inc(s_f_hp, 1)
                for g in range(NCH):
                    pe.wait_ge(s_f_xn, NCH * l + g + 1)
                    for i in range(4):
                        ins = pe.transpose(ps[:, 4 + g, i * P:(i + 1) * P], xn[:, 4 * g + i, :], ident[:, :])
                    ins.then_inc(s_f_xp, 1)

                def down(c):
                    for m, (r, n) in enumerate(M1):
                        pe.wait_ge(s_f_u, 3 * NCH * l + 3 * c + m + 1)
                        if m == 0 and c >= 2:
                            pe.wait_ge(s_f_z, NCH * l + c - 1)
                        ins = pe.matmul(ps[:, 6 + c % 2, :], l_down[0:n, m, :], gbuf[0:n, c % 2, m, :],
                                        start=(m == 0), stop=(m == 2))
                    ins.then_inc(s_f_y, 1)

                pe.wait_ge(s_f_yT, NCH * l + NCH)
                for c in range(NCH):
                    for m, (r, n) in enumerate(M1):
                        k = 3 * NCH * l + 3 * c + m
                        if c >= 1:
                            pe.wait_ge(s_f_ge, k - 2)
                            pe.wait_ge(s_f_u, k - 2)
                        x = yT[:, c * CH:(c + 1) * CH]
                        pe.matmul(ps[0:n, m, :], l_up[:, HID + r:HID + r + n], x, start=True, stop=True)\
                          .then_inc(s_f_g, 1)
                        pe.matmul(ps[0:n, 3 + m, :], l_up[:, r:r + n], x, start=True, stop=True)\
                          .then_inc(s_f_a, 1)
                    if c >= 1:
                        down(c - 1)
                down(NCH - 1)
            pe.wait_ge(s_f_z, DEPTH * NCH)
            norm_out(3, xT)


        @block.vector
        def _(dve):
            ch = Chain(dve, s_dve)

            def normalise_stats(n, src):
                for t in range(TILES):
                    ch.link(dve.bn_stats(stats[:, t, :], src(t)))
                ch.settle()
                for t in range(TILES):
                    ins = dve.bn_aggr(mv[:, t, :], stats[:, t, :])
                ins.then_inc(s_var, 1)
                dve.wait_ge(s_sd, n)
                ch.step(dve.reciprocal(rstd[:, :], sd[:, :]))

            def norm_in(k):
                normalise_stats(2 * k + 1, lambda t: x_sb[:, t, :])
                for t in range(TILES):
                    ins = dve.tensor_scalar(xn[:, t, :], x_sb[:, t, :], mv[:, t, 0:1], rstd[:, t:t + 1],
                                            ALU.subtract, ALU.mult)
                    if t % 4 == 3:
                        ins.then_inc(s_xn, 1)

            def norm_out(k):
                def tile(t):
                    if t % 4 == 0:
                        dve.wait_ge(s_yp, NCH * k + t // 4 + 1)
                    return ps[:, t // 4, (t % 4) * P:(t % 4 + 1) * P]

                normalise_stats(2 * k + 2, tile)
                for t in range(TILES):
                    ch.link(dve.tensor_scalar(xn[:, t, :], ps[:, t // 4, (t % 4) * P:(t % 4 + 1) * P],
                                              mv[:, t, 0:1], rstd[:, t:t + 1], ALU.subtract, ALU.mult))
                ch.settle()
                dve.tensor_tensor(x_sb[:, :, :], x_sb[:, :, :], xn[:, :, :], ALU.add).then_inc(s_res, 1)
                dve.wait_ge(s_res, k + 1)

            dve.memset(w3[:, :, :, :], 0.0)
            dve.memset(w3o[:, :, :], 0.0)
            dve.memset(b4[:, :, :], 0.0)
            dve.memset(b3[:, :, :], 0.0).then_inc(s_ld_z, 1)
            dve.sem_inc(s_c_evB, 1)
            dve.memset(eps_c[:, :], EPS).then_inc(s_eps, 1)
            dve.sem_inc(s_a_evB, 1)
            dve.sem_inc(s_a_oadd, 1)
            dve.wait_ge(s_ld_x, 16 * BATCH)
            norm_in(0)
            for g, dst in enumerate((w0q[:, 0:4, :], w0k[:, 0:4, :], w0v[:, 0:2, :], w0v[:, 2:4, :])):
                dve.wait_ge(s_w0p, g + 1)
                ch.link(dve.tensor_copy(dst, ps[:, 4 + g, :].rearrange("p (n c) -> p n c", n=dst.shape[1])))
            ch.settle()
            for w in (w0q, w0k, w0v):
                ins = dve.tensor_copy(w[:, PAIRS, :], w[:, 0, :])
            ins.then_inc(s_w0t, 1)
            for g in range(9):
                dve.wait_ge(s_fp, g + 1)
                src = ps[:, 4 + g % 4, :]
                if g < 6:
                    slot = (0, 2, 1)[g // 2]
                    ins = dve.tensor_copy(fT[:, 4 * (g % 2):4 * (g % 2) + 4, slot, :],
                                          src.rearrange("p (n c) -> p n c", n=4))
                elif g < 8:
                    n = (4, 2)[g - 6]
                    ins = dve.tensor_copy(swT[:, 4 * (g - 6):4 * (g - 6) + n, :],
                                          src[:, 0:n * P].rearrange("p (n c) -> p n c", n=n))
                else:
                    dve.tensor_copy(gateT[:, :], src[:, 0:E0])
                    ins = dve.tensor_copy(fb[:, 0:E0, :],
                                          src[:, E0:4 * E0].rearrange("p (n e) -> p e n", n=3))
                ins.then_inc(s_ft, 1)
            dve.memset(fT[:, E0, :, :], 0.0)
            dve.memset(fb[:, E0, :], 0.0)
            dve.memset(sel[:, E0, :, :], 0.0)
            dve.tensor_copy(sel[:, 0:E0, :, :], sel_f[:, :, :, :]).then_inc(s_selc, 1)
            dve.memset(yT[:, :], 0.0).then_inc(s_a_ozero, 1)

            def a_evac_k(m):
                dve.wait_ge(s_a_projk, m)
                dve.tensor_copy(k_st[:, :].rearrange("p (n c) -> p n c", n=2), ps[:, 2:4, :]).then_inc(s_a_k, 1)

            def a_evac_v(m):
                dve.wait_ge(s_a_projv1, m)
                dve.tensor_copy(v_st[:, 4:8, :].rearrange("p (n k) c -> p n (k c)", n=2),
                                ps[:, 2:4, :]).then_inc(s_a_v1, 1)

            a_evac_k(1)
            a_evac_v(1)
            dve.wait_ge(s_a_ozero, 1)
            with dve.Fori(0, PAIRS) as p:
                for b in range(BATCH):
                    n0 = 2 * NU * p + NU * b
                    m = 2 * p + b

                    def rowmax(u):
                        dve.wait_ge(s_a_scores, n0 + u + 1)
                        s2 = ps[:, 2 * (u % 2):2 * (u % 2) + 2, :].rearrange("p n c -> p (n c)")
                        dve.tensor_reduce(negmax[:, u:u + 1], s2, AX_X, ALU.max, negate=True)\
                           .then_inc(s_a_negmax, 1)

                    def rrecip(u):
                        dve.wait_ge(s_a_exp, n0 + u + 1)
                        dve.reciprocal(rrow[:, u:u + 1], rowsum[:, u:u + 1]).then_inc(s_a_rrow, 1)
                        dve.wait_ge(s_a_rrow, n0 + u + 1)
                        dve.tensor_scalar(probs[:, u % NPB, :], probs[:, u % NPB, :], rrow[:, u:u + 1], None,
                                          ALU.mult).then_inc(s_a_norm, 1)

                    def copy_out(u):
                        dve.wait_ge(s_a_trans, 2 * (n0 + u) + 2)
                        c, q = u // 4, (u % 4) * P
                        dve.tensor_copy(probsT[:, c % 2, 4:8, q:q + P],
                                        ps[:, 5, :].rearrange("p (k c) -> p k c", k=4)).then_inc(s_a_evB, 1)

                    def add_out(qc):
                        dve.wait_ge(s_a_pv, 2 * m + qc + 1)
                        dve.wait_ge(s_a_oadd, 2 * m + qc + 1)
                        y = yT[:, b * SEQ + qc * CH:b * SEQ + (qc + 1) * CH]
                        dve.tensor_tensor(y, ps[:, 6 + qc, :], y, ALU.add).then_inc(s_a_oadd, 1)

                    for u in range(NU):
                        rowmax(u)
                        if u >= 1:
                            rrecip(u - 1)
                        if u >= 2:
                            copy_out(u - 2)
                    rrecip(NU - 1)
                    copy_out(NU - 2)
                    a_evac_k(m + 2)
                    copy_out(NU - 1)
                    add_out(0)
                    add_out(1)
                    a_evac_v(m + 2)
            dve.wait_ge(s_a_oadd, 4 * PAIRS + 1)
            dve.sem_inc(s_y[0], 1)
            norm_out(0)

            norm_in(1)
            lg = ps[:, 7, 0:TILES * E0].rearrange("p (t e) -> p t e", e=E0)

            def per_token(v):
                return v.unsqueeze(2).to_broadcast([P, TILES, E0])

            dve.wait_ge(s_logits, 1)
            ch.step(dve.tensor_reduce(gmax[:, :], lg, AX_X, ALU.max))
            dve.tensor_tensor(gw[:, 0], lg, per_token(gmax[:, :]), ALU.subtract).then_inc(s_gshift, 1)
            dve.wait_ge(s_gexp, 1)
            ch.step(dve.tensor_reduce(gsum[:, :], gw[:, 1], AX_X, ALU.add))
            ch.step(dve.reciprocal(gmax[:, :], gsum[:, :]))
            ch.step(dve.tensor_tensor(gw[:, 2], gw[:, 1], per_token(gmax[:, :]), ALU.mult))
            for t in range(TILES):
                ch.link(dve.max(gw[:, 3, t, :], gw[:, 2, t, :]))
            ch.settle()
            for t in range(TILES):
                ch.link(dve.max_index(top_i[:, t, :], gw[:, 3, t, :], gw[:, 2, t, :]))
            ch.settle()
            ch.step(dve.tensor_copy(gw[:, 4], top_i[:, :, :]))
            for r in range(2):
                ch.link(dve.tensor_tensor(gw[:, 5 + r], iota8[:, :, :], per_token(gw[:, 4, :, r]), ALU.is_equal))
            ch.settle()
            ch.step(dve.tensor_tensor(G[:, :, 24:32], gw[:, 5], gw[:, 6], ALU.add))
            gb = e_sg[:, 0, 0:3 * TILES * E0 // 2].bitcast(BF16).rearrange("p (n t e) -> p n t e", t=TILES, e=E0)
            rest = gw[:, 2]
            for r in range(3):
                ch.step(dve.tensor_copy(gb[:, r], rest))
                ch.step(dve.tensor_copy(G[:, :, 8 * r:8 * r + 8], gb[:, r]))
                if r < 2:
                    ch.step(dve.tensor_tensor(gw[:, 5 + r], rest, gb[:, r], ALU.subtract))
                    rest = gw[:, 5 + r]
            dve.sem_inc(s_G, 1)

            for k in range(2 * NCH):
                dve.wait_ge(s_sh_u, k + 1)
                dve.wait_ge(s_sh_silu, k + 1)
                dve.tensor_tensor(e_sh[:, k % 2, :], ps[:, 2 + k % 2, :], e_sg[:, k % 2, :], ALU.mult)\
                   .then_inc(s_sh_h, 1)

            def e_weights(s, e, done):
                dve.tensor_copy(e_w[:, s, :, :], fT[:, e, :, :])
                dve.tensor_copy(e_b[:, s, :], fb[:, e, :])
                dve.tensor_copy(e_sel[:, s, :, :], sel[:, e, :, :]).then_inc(done, 1)

            e_weights(0, 0, s_e_wA)
            with dve.Fori(0, E0 // 2) as i:
                n0 = 2 * NCH * i

                def scale(k):
                    c = k % NCH
                    dve.wait_ge(s_e_bc, n0 + k + 1)
                    if k >= 2:
                        dve.wait_ge(s_e_x3, n0 + k - 1)
                    dve.tensor_tensor(e_xs[:, k % 2, :], ps[:, k % 2, :], xT[:, c * CH:(c + 1) * CH], ALU.mult)\
                       .then_inc(s_e_xs, 1)

                scale(0)
                for k in range(2 * NCH):
                    s = k // NCH
                    if k < 2 * NCH - 1:
                        scale(k + 1)
                    dve.wait_ge(s_e_x3, n0 + k + 1)
                    dve.wait_ge(s_e_mask, n0 + k + 1)
                    dve.scalar_tensor_tensor(out=e_t3[:, k % 2, :], in0=ps[:, 5 + k % 2, :], scalar=e_b[:, s, 2:3],
                                             in1=e_mask[:, k % 2, :], op0=ALU.add, op1=ALU.mult)\
                       .then_inc(s_e_t3, 1)
                    dve.wait_ge(s_e_t3, n0 + k + 1)
                    dve.wait_ge(s_e_x2, n0 + k + 1)
                    dve.wait_ge(s_e_y, n0 + k + 1)
                    dve.scalar_tensor_tensor(out=e_t[:, k % 2, :], in0=ps[:, 7, :], scalar=e_b[:, s, 1:2],
                                             in1=e_t3[:, k % 2, :], op0=ALU.add, op1=ALU.mult)\
                       .then_inc(s_e_t, 1)
                    if k == 1:
                        e_weights(1, 2 * i + 1, s_e_wB)
                    if k == NCH + 1:
                        e_weights(0, 2 * i + 2, s_e_wA)
            norm_out(1)

            norm_in(2)
            dve.wait_ge(s_c_bp, 1)
            dve.tensor_tensor(bias_y[:, :], ps[:, 4, 0:1], b3o[:, :], ALU.add).then_inc(s_c_by, 1)

            def c_evac_q(m):
                dve.wait_ge(s_c_projq, m)
                dve.tensor_scalar(q_st[:, :].rearrange("p (n c) -> p n c", n=2), ps[:, 0:2, :], c_b[:, 0:1],
                                  HD1 ** -0.5, ALU.add, ALU.mult).then_inc(s_c_q, 1)

            c_evac_q(1)
            CU = 4 * QT
            dve.sem_inc(s_c_T, 1)
            with dve.Fori(0, GROUPS) as g:
                for b in range(BATCH):
                    n0 = 2 * CU * g + CU * b
                    m = 2 * g + b
                    h0 = CU // 2 * m
                    if b == 0:
                        for j in range(4):
                            ins = dve.tensor_scalar(c_T[:, j, :], rel[:, :], slopes[:, bass.ds(4 * g + j, 1)], None,
                                                    ALU.mult)
                        ins.then_inc(s_c_T, 1)
                        dve.wait_ge(s_c_T, g + 2)

                    def bias(u):
                        j, qt = u % 4, u // 4
                        w = (qt + 1) * P
                        dve.wait_ge(s_c_scores, n0 + u + 1)
                        if u >= 2:
                            dve.wait_ge(s_c_exp, n0 + u - 1)
                        dve.sem_inc(s_c_go, 1)
                        s2 = ps[:, 2 * (u % 2):2 * (u % 2) + 2, :].rearrange("p n c -> p (n c)")[:, 0:w]
                        dve.tensor_tensor_reduce(c_sb[:, u % 2, 0:w], s2, c_T[:, j, SEQ - w:SEQ], 1.0, -3.0e38,
                                                 ALU.add, ALU.max, cmax[:, u:u + 1]).then_inc(s_c_bias, 1)
                        dve.wait_ge(s_c_bias, n0 + u + 1)
                        dve.tensor_scalar(negmax[:, u:u + 1], cmax[:, u:u + 1], -1.0, None, ALU.mult)\
                           .then_inc(s_c_negmax, 1)

                    def copy_out(u):
                        j, qt = u % 4, u // 4
                        if qt >= 4:
                            dve.wait_ge(s_c_transB, h0 + u - CU // 2 + 1)
                            dve.tensor_copy(c_pT[:, qt % 2, j, 4:qt + 1, :],
                                            ps[:, 5, 0:(qt - 3) * P].rearrange("p (k c) -> p k c", c=P))\
                               .then_inc(s_c_evB, 1)

                    for u in range(CU):
                        bias(u)
                        if u >= 3:
                            copy_out(u - 3)
                    c_evac_q(m + 2)
                    for u in range(CU - 3, CU):
                        copy_out(u)
                    dve.wait_ge(s_c_exp, n0 + CU)
                    dve.reciprocal(rrow[:, 0:CU], rowsum[:, 0:CU]).then_inc(s_c_rr, 1)
                    dve.wait_ge(s_c_bc, m + 1)
                    dve.tensor_tensor(oT[:, g, b * SEQ:(b + 1) * SEQ], ps[:, 6:8, :].rearrange("p n c -> p (n c)"),
                                      c_o[:, 0, :], ALU.mult).then_inc(s_c_oT, 1)
            norm_out(2)

            norm_in(3)
            ch.link(dve.memset(half_c[:, :], -0.5))
            ch.link(dve.tensor_copy(ident_b[:, :], ident[:, :]))
            ch.link(dve.memset(hT[:, :], 0.0))
            ch.link(dve.memset(d_kT[:, :, :, :], 0.0))
            dve.wait_ge(s_ld_r, 16 * 3)
            ch.link(dve.tensor_copy(mask_b, mask_f[:, 1:2, :].to_broadcast([P, TILES, P])))
            ch.settle()
            for b in range(BATCH):
                ch.link(dve.tensor_copy(mask_b[:, b * QT, :], mask_f[:, 0, :]))
            ch.settle()
            dve.wait_ge(s_ld_d, 16 * 31)
            dve.wait_ge(s_xT, NCH * 4)
            dve.sem_inc(s_d_init, 1)

            PER_LAYER = 42
            with dve.Fori(0, DEPTH) as l:
                T0 = TILES * l
                lch = Chain(dve, s_d_chain, PER_LAYER * l)

                def shift():
                    lch.link(dve.tensor_copy(hT[0:64, WIN:WIN + TOK], xT[0:64, :]))
                    for b in range(BATCH):
                        lch.link(dve.tensor_copy(hT[64:P, WIN + b * SEQ + 1:WIN + (b + 1) * SEQ],
                                                 xT[64:P, b * SEQ:(b + 1) * SEQ - 1]))
                    lch.settle()

                lch.link(dve.tensor_copy(l_qkv, w4qkv[:, l, :]))
                lch.link(dve.tensor_copy(l_up, w4up[:, l, :]))
                lch.link(dve.tensor_copy(l_o, w4o[:, l, :, :]))
                lch.link(dve.tensor_copy(l_b[:, :], b4[:, l, :]))
                for m, (r, n) in enumerate(M1):
                    lch.link(dve.tensor_copy(l_down[0:n, m, :], w4down[0:n, l, m, :]))
                sc = qk_scale[:, l, :, :]
                for b in range(BATCH):
                    t0 = b * QT
                    for n in range(2):
                        lch.link(dve.tensor_tensor(rot_c[:, t0:t0 + QT, n, :], base_c[:, :, n, :],
                                                   sc[:, n:n + 1, :].to_broadcast([P, QT, HD2]), ALU.mult))
                        for half in range(2):
                            d, e = 32 * half, 32 * (1 - half)
                            lch.link(dve.tensor_tensor(rot_s[:, t0:t0 + QT, n, d:d + 32], base_s[:, :, n, d:d + 32],
                                                       sc[:, n:n + 1, e:e + 32].to_broadcast([P, QT, 32]), ALU.mult))
                shift()
                dve.sem_inc(s_d_wst, 1)

                def copy_hq(t, par):
                    if exists(t, -2):
                        dve.wait_ge(s_d_qkp, T0 + t - 1)
                    dve.tensor_scalar(hq[:, par, :], hT[:, bass.ds(WIN + t * P, P)], 0.0, None, ALU.add)\
                       .then_inc(s_d_hq, 1)

                def copy_hv(t, par):
                    if exists(t, -2):
                        dve.wait_ge(s_d_vp, T0 + t - 1)
                    dve.tensor_scalar(hv[:, par, :], hT[:, bass.ds(t * P, P + WIN)], 0.0, None, ALU.add)\
                       .then_inc(s_d_hv, 1)

                def rotate(t, par):
                    n = T0 + t
                    qk = ps[:, 0:2, :].rearrange("p n (h d) -> p n h d", d=HD2)
                    mA = d_mA[:, par, :].rearrange("p (n h d) -> p n h d", n=2, d=HD2)
                    mB = d_mB[:, par, :].rearrange("p (n h d) -> p n h d", n=2, d=HD2)

                    def heads(v):
                        return v.rearrange("p t n d -> p n t d").to_broadcast([P, 2, H2, v.shape[3]])

                    dve.wait_ge(s_d_sq, n + 1)
                    dve.tensor_tensor(mA, qk, heads(rot_c[:, bass.ds(t, 1), :, :]), ALU.mult)
                    for d, e in ((0, 32), (32, 0)):
                        ins = dve.tensor_tensor(mB[:, :, :, d:d + 32], qk[:, :, :, e:e + 32],
                                                heads(rot_s[:, bass.ds(t, 1), :, d:d + 32]), ALU.mult)
                    ins.then_inc(s_d_m, 1)
                    dve.tensor_reduce(ss[:, par, :], d_sq[:, par, :].rearrange("p (h d) -> p h d", d=HD2),
                                      AX_X, ALU.add).then_inc(s_d_ss, 1)
                    dve.wait_ge(s_d_ss, n + 1)
                    dve.tensor_scalar(ss[:, par, :], ss[:, par, :], 1e-24, None, ALU.max).then_inc(s_d_cl, 1)

                def step(t, par):
                    n = T0 + t
                    if exists(t, 2):
                        rotate(t + 2, par)
                    if exists(t, -1):
                        dve.wait_ge(s_d_pt, n)
                        dve.tensor_copy(d_pT[:, :, :].rearrange("p h c -> p (h c)"),
                                        ps[:, 4:6, :].rearrange("p n c -> p (n c)")).then_inc(s_d_pT, 1)
                    if exists(t, 0):
                        dve.wait_ge(s_d_s, n + 1)
                        dve.tensor_reduce(d_nm[:, par, :], ps[:, 6:8, :].rearrange("p n (h c) -> p (n h) c", c=P),
                                          AX_X, ALU.max).then_inc(s_d_nm, 1)
                        dve.wait_ge(s_d_nm, n + 1)
                        dve.tensor_scalar(d_nm8[:, par, :], d_nm[:, par, :], -QK, None, ALU.mult)\
                           .then_inc(s_d_nm8, 1)
                    if exists(t, -2):
                        dve.wait_ge(s_d_w, n - 1)
                        z = xT[:, bass.ds((t - 2) * P, P)]
                        dve.tensor_tensor(z, ps[:, 3, 0:P], z, ALU.add).then_inc(s_d_z, 1)
                    if exists(t, 3):
                        copy_hq(t + 3, 1 - par)
                    if exists(t, 1):
                        copy_hv(t + 1, 1 - par)
                    if exists(t, 0):
                        dve.wait_ge(s_d_e, n + 1)
                        dve.reciprocal(d_rr[:, par, :], d_sum[:, par, :]).then_inc(s_d_rr, 1)

                copy_hq(0, 0)
                copy_hq(1, 1)
                rotate(0, 0)
                copy_hq(2, 0)
                copy_hv(0, 0)
                rotate(1, 1)
                walk(dve, step, TILES + 2)

                dve.wait_ge(s_d_z, T0 + TILES)
                shift()
                dve.sem_inc(s_f_hT, 1)
                for t in range(TILES):
                    if t % 4 == 0:
                        dve.wait_ge(s_f_hp, NCH * l + t // 4 + 1)
                    lch.link(dve.bn_stats(stats[:, t, :], ps[:, t // 4, (t % 4) * P:(t % 4 + 1) * P]))
                lch.settle()
                dve.sem_inc(s_f_go, 1)
                for t in range(TILES):
                    ins = dve.bn_aggr(mv[:, t, :], stats[:, t, :])
                ins.then_inc(s_f_var, 1)
                dve.wait_ge(s_f_sd, l + 1)
                lch.step(dve.reciprocal(rstd[:, :], sd[:, :]))
                for t in range(TILES):
                    ins = dve.tensor_scalar(xn[:, t, :], ps[:, t // 4, (t % 4) * P:(t % 4 + 1) * P],
                                            mv[:, t, 0:1], rstd[:, t:t + 1], ALU.subtract, ALU.mult)
                    if t % 4 == 3:
                        ins.then_inc(s_f_xn, 1)

                def add_down(c):
                    dve.wait_ge(s_f_y, NCH * l + c + 1)
                    z = xT[:, c * CH:(c + 1) * CH]
                    dve.scalar_tensor_tensor(out=z, in0=ps[:, 6 + c % 2, :], scalar=l_b[:, 6:7], in1=z,
                                             op0=ALU.add, op1=ALU.add).then_inc(s_f_z, 1)

                for c in range(NCH):
                    for m, (r, n) in enumerate(M1):
                        k = 3 * NCH * l + 3 * c + m
                        dve.wait_ge(s_f_a, k + 1)
                        dve.wait_ge(s_f_ge, k + 1)
                        dve.scalar_tensor_tensor(out=gbuf[0:n, c % 2, m, :], in0=ps[0:n, 3 + m, :],
                                                 scalar=l_b[0:n, m:m + 1], in1=gbuf[0:n, c % 2, m, :],
                                                 op0=ALU.add, op1=ALU.mult).then_inc(s_f_u, 1)
                    if c >= 1:
                        add_down(c - 1)
                add_down(NCH - 1)
                dve.wait_ge(s_f_z, NCH * l + NCH)
                assert lch.n == PER_LAYER, lch.n
            norm_out(3)


        @block.scalar
        def _(act):
            def norm_in(k):
                act.wait_ge(s_var, 2 * k + 1)
                act.activation(sd[:, :], mv[:, :, 1], ACT.Sqrt, bias=eps_c[:, 0:1]).then_inc(s_sd, 1)
                for g in range(NCH):
                    act.wait_ge(s_xTp, NCH * k + g + 1)
                    act.copy(xT[:, g * CH:(g + 1) * CH], ps[:, g, :]).then_inc(s_xT, 1)

            def norm_out(k):
                act.wait_ge(s_var, 2 * k + 2)
                act.activation(sd[:, :], mv[:, :, 1], ACT.Sqrt, bias=eps_c[:, 0:1]).then_inc(s_sd, 1)

            act.sem_inc(s_a_evA, 1)
            act.wait_ge(s_eps, 1)
            norm_in(0)

            def a_evac_q(m):
                act.wait_ge(s_a_projq, m)
                act.copy(q_st[:, :].rearrange("p (n c) -> p n c", n=2), ps[:, 0:2, :]).then_inc(s_a_q, 1)

            def a_evac_v(m):
                act.wait_ge(s_a_projv0, m)
                act.copy(v_st[:, 0:4, :].rearrange("p (n k) c -> p n (k c)", n=2), ps[:, 0:2, :]).then_inc(s_a_v0, 1)

            a_evac_q(1)
            a_evac_v(1)
            with act.Fori(0, PAIRS) as p:
                for b in range(BATCH):
                    n0 = 2 * NU * p + NU * b
                    m = 2 * p + b

                    def soft(u):
                        act.wait_ge(s_a_negmax, n0 + u + 1)
                        if u >= NPB:
                            act.wait_ge(s_a_trans, 2 * (n0 + u - NPB) + 2)
                        s2 = ps[:, 2 * (u % 2):2 * (u % 2) + 2, :].rearrange("p n c -> p (n c)")
                        act.activation(probs[:, u % NPB, :], s2, ACT.Exp, bias=negmax[:, u:u + 1],
                                       accum_out=rowsum[:, u:u + 1]).then_inc(s_a_exp, 1)

                    def copy_out(u):
                        act.wait_ge(s_a_trans, 2 * (n0 + u) + 1)
                        c, q = u // 4, (u % 4) * P
                        act.copy(probsT[:, c % 2, 0:4, q:q + P],
                                 ps[:, 4, :].rearrange("p (k c) -> p k c", k=4)).then_inc(s_a_evA, 1)

                    for u in range(NU):
                        if u >= 2:
                            copy_out(u - 2)
                        soft(u)
                    copy_out(NU - 2)
                    a_evac_q(m + 2)
                    copy_out(NU - 1)
                    a_evac_v(m + 2)
            norm_out(0)

            norm_in(1)
            act.wait_ge(s_gshift, 1)
            act.activation(gw[:, 1], gw[:, 0], ACT.Exp).then_inc(s_gexp, 1)

            for k in range(2 * NCH):
                act.wait_ge(s_sh_g, k + 1)
                if k >= 2:
                    act.wait_ge(s_sh_h, k - 1)
                if k == 0:
                    act.wait_ge(s_G, 1)
                act.activation(e_sg[:, k % 2, :], ps[:, k % 2, :], ACT.Silu).then_inc(s_sh_silu, 1)
                if k >= 3 and k % 2 == 1:
                    c = k // 2 - 1
                    act.wait_ge(s_sh_z, c + 1)
                    act.copy(yT[:, c * CH:(c + 1) * CH], ps[:, 4 + c % 2, :]).then_inc(s_sh_y, 1)
            act.wait_ge(s_sh_z, NCH)
            act.copy(yT[:, (NCH - 1) * CH:NCH * CH], ps[:, 4 + (NCH - 1) % 2, :]).then_inc(s_sh_y, 1)
            for g in range(NCH):
                act.wait_ge(s_gTp, g + 1)
                act.copy(gT[:, g * CH:(g + 1) * CH], ps[0:STRIP, 6 + g % 2, :]).then_inc(s_gT, 1)

            with act.Fori(0, E0 // 2) as i:
                n0 = 2 * NCH * i

                def mask(k):
                    act.wait_ge(s_e_bc, n0 + k + 1)
                    if k >= 2:
                        act.wait_ge(s_e_t3, n0 + k - 1)
                    act.copy(e_mask[:, k % 2, :], ps[:, 2, :]).then_inc(s_e_mask, 1)

                mask(0)
                for k in range(2 * NCH):
                    if k < 2 * NCH - 1:
                        mask(k + 1)
                    act.wait_ge(s_e_h1, n0 + k + 1)
                    act.activation(e_h[:, k % 2, :], ps[:, 3 + k % 2, :], ACT.Silu,
                                   bias=e_b[:, k // NCH, 0:1]).then_inc(s_e_h, 1)
            norm_out(1)

            norm_in(2)
            act.sem_inc(s_c_evA, 1)
            act.sem_inc(s_c_o, 2)

            def c_evac_k(m):
                act.wait_ge(s_c_projk, m)
                act.activation(k_st[:, :].rearrange("p (n c) -> p n c", n=2), ps[:, 2:4, :], ACT.Identity,
                               bias=c_b[:, 1:2]).then_inc(s_c_k, 1)

            def c_evac_v(m):
                act.wait_ge(s_c_projv, m)
                act.copy(v_st[:, :, 0:P].rearrange("p (n k) c -> p n k c", n=2),
                         ps[:, 0:2, :].rearrange("p n (k c) -> p n k c", k=4)).then_inc(s_c_v, 1)

            c_evac_k(1)
            c_evac_v(1)
            CU = 4 * QT
            with act.Fori(0, GROUPS) as g:
                for b in range(BATCH):
                    n0 = 2 * CU * g + CU * b
                    m = 2 * g + b
                    h0 = CU // 2 * m

                    def soft(u):
                        qt = u // 4
                        w = (qt + 1) * P
                        act.wait_ge(s_c_negmax, n0 + u + 1)
                        if u >= NPB:
                            v = u - NPB
                            if v // 4 >= 4:
                                act.wait_ge(s_c_transB, h0 + v - CU // 2 + 1)
                            else:
                                act.wait_ge(s_c_transA, n0 + v + 1)
                        act.activation(probs[:, u % NPB, 0:w], c_sb[:, u % 2, 0:w], ACT.Exp,
                                       bias=negmax[:, u:u + 1], accum_out=rowsum[:, u:u + 1]).then_inc(s_c_exp, 1)

                    def copy_out(u):
                        j, qt = u % 4, u // 4
                        k = min(4, qt + 1)
                        act.wait_ge(s_c_transA, n0 + u + 1)
                        act.copy(c_pT[:, qt % 2, j, 0:k, :],
                                 ps[:, 4, 0:k * P].rearrange("p (k c) -> p k c", c=P)).then_inc(s_c_evA, 1)

                    def out_tile(qt):
                        act.wait_ge(s_c_pv, QT * m + qt + 1)
                        act.copy(c_o[:, 0, qt * P:(qt + 1) * P], ps[:, 6 + qt % 2, 0:P]).then_inc(s_c_o, 1)

                    for u in range(CU):
                        if u >= 3:
                            copy_out(u - 3)
                        if u >= 8 and u % 4 == 0:
                            out_tile((u - 8) // 4)
                        soft(u)
                    copy_out(CU - 3)
                    copy_out(CU - 2)
                    c_evac_k(m + 2)
                    copy_out(CU - 1)
                    out_tile(QT - 2)
                    out_tile(QT - 1)
                    act.wait_ge(s_c_rrp, m + 1)
                    act.copy(c_rT[:, :], ps[0:STRIP, 4, 0:P]).then_inc(s_c_rT, 1)
                    c_evac_v(m + 2)
            for c in range(NCH):
                act.wait_ge(s_c_y, c + 1)
                act.activation(yT[:, c * CH:(c + 1) * CH], ps[:, 4 + c, :], ACT.Identity,
                               bias=bias_y[:, 0:1]).then_inc(s_c_yc, 1)
            act.wait_ge(s_c_yc, NCH)
            act.sem_inc(s_y[2], 1)
            norm_out(2)

            norm_in(3)
            with act.Fori(0, DEPTH) as l:
                T0 = TILES * l

                def square(t, par):
                    act.wait_ge(s_d_qkp, T0 + t + 1)
                    act.activation(d_sq[:, par, :], ps[:, 0:2, :].rearrange("p n c -> p (n c)"), ACT.Square)\
                       .then_inc(s_d_sq, 1)

                def step(t, par):
                    n = T0 + t
                    if exists(t, 0):
                        act.wait_ge(s_d_qkt, n + 1)
                        act.copy(d_qT, ps[:, 4, :].rearrange("p (m c) -> p m c", m=4)).then_inc(s_d_qT, 1)
                        act.copy(d_kT[:, par, :, :], ps[:, 5, :].rearrange("p (m c) -> p m c", m=4))\
                           .then_inc(s_d_kT, 1)
                    if exists(t, 2):
                        square(t + 2, par)
                    if exists(t, 0):
                        act.wait_ge(s_d_vp, n + 1)
                        act.copy(d_va[:, par, :], ps[:, 2, :])
                        act.copy(d_vs[:, par, :], ps[:, 3, :]).then_inc(s_d_v, 1)
                        act.wait_ge(s_d_nm8, n + 1)
                        for h in range(H2):
                            ins = act.activation(d_p[:, par, h, :], ps[:, 6 + h // 4, (h % 4) * P:(h % 4 + 1) * P],
                                                 ACT.Exp, bias=d_nm8[:, par, h:h + 1], scale=QK,
                                                 accum_out=d_sum[:, par, h:h + 1])
                        ins.then_inc(s_d_e, 1)
                    if exists(t, -1):
                        act.wait_ge(s_d_o, n)
                        act.copy(d_o[:, 1 - par, :, :], ps[:, 2, :].rearrange("p (m c) -> p m c", m=4))\
                           .then_inc(s_d_oT, 1)

                square(0, 0)
                square(1, 1)
                walk(act, step, TILES + 1)

                act.wait_ge(s_f_var, l + 1)
                act.activation(sd[:, :], mv[:, :, 1], ACT.Sqrt, bias=eps_c[:, 0:1]).then_inc(s_f_sd, 1)
                for g in range(NCH):
                    act.wait_ge(s_f_xp, NCH * l + g + 1)
                    act.activation(yT[:, g * CH:(g + 1) * CH], ps[:, 4 + g, :], ACT.Identity,
                                   bias=l_b[:, 8:9], scale=l_b[:, 7:8]).then_inc(s_f_yT, 1)
                for c in range(NCH):
                    for m, (r, n) in enumerate(M1):
                        k = 3 * NCH * l + 3 * c + m
                        act.wait_ge(s_f_g, k + 1)
                        if c >= 2:
                            act.wait_ge(s_f_y, NCH * l + c - 1)
                        act.activation(gbuf[0:n, c % 2, m, :], ps[0:n, m, :], ACT.Gelu,
                                       bias=l_b[0:n, 3 + m:4 + m]).then_inc(s_f_ge, 1)
            norm_out(3)


        @block.gpsimd
        def _(pool):
            def a_weights(p):
                pool.tensor_copy(wq_st[:, :], w0q[:, p, :])
                pool.tensor_copy(wk_st[:, :], w0k[:, p, :])
                pool.tensor_copy(wv_st[:, :], w0v[:, p, :]).then_inc(s_a_wst, 1)

            pool.wait_ge(s_w0t, 1)
            a_weights(0)
            with pool.Fori(0, PAIRS) as p:
                for b in range(BATCH):
                    if b == 1:
                        pool.wait_ge(s_a_scores, 2 * NU * p + NU + 1)
                        a_weights(p + 1)

            pool.sem_inc(s_e_y, 2)
            pool.wait_ge(s_sh_y, NCH)
            with pool.Fori(0, E0 // 2) as i:
                for k in range(2 * NCH):
                    c = k % NCH
                    y = yT[:, c * CH:(c + 1) * CH]
                    pool.wait_ge(s_e_t, 2 * NCH * i + k + 1)
                    pool.wait_ge(s_e_y, 2 * NCH * i + k + 2)
                    pool.tensor_tensor(y, y, e_t[:, k % 2, :], ALU.add).then_inc(s_e_y, 1)
            pool.wait_ge(s_e_y, E0 * NCH + 2)
            pool.sem_inc(s_y[1], 1)

            pool.sem_inc(s_c_oT, 1)
            pool.wait_ge(s_ld_c, 16 * 23)
            for i in range(3):
                ins = pool.tensor_copy(w3[:, 0:GROUPS, i, :].rearrange("p g (j e) -> p g j e", e=STRIP)[:, :, :, 0:HD1],
                                       nat3[:, i, :].rearrange("p (g j e) -> p g j e", j=4, e=HD1))
            ins.then_inc(s_c_pad, 1)
            pool.wait_ge(s_c_pad, 1)

            def c_weights(g):
                pool.tensor_copy(c_w[:, :, :], w3[:, g, :, :])
                pool.tensor_copy(c_b[:, :], b3[:, g, :]).then_inc(s_c_wst, 1)

            c_weights(0)
            with pool.Fori(0, GROUPS) as g:
                pool.wait_ge(s_c_scores, 8 * QT * g + 4 * QT + 1)
                c_weights(g + 1)

            pool.wait_ge(s_d_init, 1)
            with pool.Fori(0, DEPTH) as l:
                T0 = TILES * l

                def unit_norm(t, par):
                    n = T0 + t
                    kq = d_kq[par]
                    pool.wait_ge(s_d_m, n + 1)
                    pool.tensor_tensor(kq, d_mA[:, par, :], d_mB[:, par, :], ALU.add).then_inc(s_d_add, 1)
                    pool.wait_ge(s_d_cl, n + 1)
                    pool.tensor_tensor(ss[:, par, :], ss[:, par, :], half_c[:, :], ALU.pow).then_inc(s_d_rn, 1)
                    pool.wait_ge(s_d_add, n + 1)
                    pool.wait_ge(s_d_rn, n + 1)
                    v = kq.rearrange("p (h d) -> p h d", d=HD2)
                    pool.tensor_tensor(v, v, ss[:, par, :].unsqueeze(2).to_broadcast([P, 2 * H2, HD2]), ALU.mult)\
                        .then_inc(s_d_kq, 1)

                def step(t, par):
                    if exists(t, 2):
                        unit_norm(t + 2, par)
                    if exists(t, 0):
                        v = d_p[:, par, :, :]
                        pool.wait_ge(s_d_rr, T0 + t + 1)
                        pool.tensor_tensor(v, v, d_rr[:, par, :].unsqueeze(2).to_broadcast([P, H2, P]), ALU.mult)\
                            .then_inc(s_d_p, 1)

                unit_norm(0, 0)
                unit_norm(1, 1)
                walk(pool, step, TILES)



def _constants():
    import numpy as np
    f = np.float32
    c = {"c_ident": np.eye(128, dtype=f)}
    e, part, r = np.meshgrid(np.arange(E0), np.arange(2), np.arange(STRIP), indexing="ij")
    pick = np.where(part == 0, (r < 24) & (r % 8 == e), r == 24 + e).astype(f)
    c["c_sel"] = np.ascontiguousarray(np.broadcast_to(pick.transpose(2, 0, 1)[..., None], (STRIP, E0, 2, P)))
    c["c_iota8"] = np.ascontiguousarray(np.broadcast_to(np.arange(E0, dtype=f), (P, TILES, E0)))
    p, k = np.arange(P)[:, None], np.arange(SEQ)[None, :] - (SEQ - P)
    c["c_rel"] = np.where(k <= p, k - p, -1e32).astype(f)
    c["c_slopes"] = np.ascontiguousarray(np.broadcast_to(
        np.power(f(2.0 ** (-8.0 / H1)), np.arange(1, H1 + 1, dtype=f)), (P, H1))).astype(f)
    r, q, s = np.meshgrid(np.arange(STRIP), np.arange(QT), np.arange(P), indexing="ij")
    c["c_selq"] = ((r // 4 == q) & (r % 4 == s // STRIP)).astype(f)
    half = np.arange(0, HD2, 2, dtype=f)
    pos = np.arange(SEQ, dtype=f)
    angle = pos[:, None] * (f(1.0) / np.power(f(10000.0), half / f(HD2)))[None, :]
    base = (half + f(0.4 * HD2)) / f(1.4 * HD2)
    scale = np.power(base[None, :], ((pos - SEQ // 2) / f(WIN // 2))[:, None])
    cos, sin = np.cos(angle), np.sin(angle)
    both = lambda u, v: np.concatenate([u, v], axis=1)
    c["c_rotc"] = np.stack([both(cos * scale, cos * scale), both(cos / scale, cos / scale)], 1).astype(f)
    c["c_rots"] = np.stack([both(-sin * scale, sin * scale), both(-sin / scale, sin / scale)], 1).astype(f)
    q, k = np.arange(P)[:, None], np.arange(P)[None, :]
    seen = (q % WIN <= k) & (k <= q % WIN + WIN)
    first = seen & ~((q < WIN) & (k < WIN))
    c["c_mask"] = np.ascontiguousarray(np.where(np.stack([first, seen], 1), 0.0, NEG).astype(f))
    return c


_INS = [
    "L0_attn_x",
    "L0_attn_Wq",
    "L0_attn_Wk",
    "L0_attn_Wv",
    "L0_ffn_w1",
    "L0_ffn_w2",
    "L0_ffn_w3",
    "L0_ffn_sw1",
    "L0_ffn_sw2",
    "L0_ffn_sw3",
    "L0_ffn_gate_w",
    "L0_ffn_b1",
    "L0_ffn_b2",
    "L0_ffn_b3",
    "L1_attn_Wq",
    "L1_attn_Wk",
    "L1_attn_Wv",
    "L1_attn_bo",
    "L1_attn_Wo",
    "L1_attn_bq",
    "L1_attn_bk",
    "L1_attn_bv",
    "L1_ffn_wqkv",
    "L1_ffn_wo",
    "L1_ffn_w1",
    "L1_ffn_w2",
    "L1_ffn_b1",
    "L1_ffn_b2",
    "L1_ffn_ln_g",
    "L1_ffn_ln_b",
    "L1_ffn_q_scale",
    "L1_ffn_k_scale",
]


def kernel(**inputs):
    import numpy as _np
    import concourse.bacc as _bacc
    from concourse import mybir as _mybir
    from concourse.bass_utils import run_bass_kernel_spmd as _run

    nc = _bacc.Bacc("TRN2", target_bir_lowering=False, num_devices=1)
    arrays, aps = {}, {}
    for name, a in [(n, _np.ascontiguousarray(inputs[n])) for n in _INS] + list(_constants().items()):
        arrays[f"in_{name}_dram"] = a
        aps[name] = nc.dram_tensor(f"in_{name}_dram", a.shape, _mybir.dt.from_np(a.dtype), kind="ExternalInput").ap()
    out = nc.dram_tensor("out_0_dram", (BATCH, SEQ, D), F32, kind="ExternalOutput").ap()
    build(nc, aps, out)
    r = _run(nc, [arrays], core_ids=[0])
    return r.results[0]["out_0_dram"]
```

```python
from contextlib import ExitStack

import concourse.bass as bass
from concourse import mybir

F32 = mybir.dt.float32
BF16 = mybir.dt.bfloat16
U32 = mybir.dt.uint32
ALU = mybir.AluOpType
ACT = mybir.ActivationFunctionType
AX_X = mybir.AxisListType.X

P = 128
D = 128
BATCH, SEQ = 2, 1024
TOK = BATCH * SEQ
TILES = TOK // P
QT = SEQ // P
CH = 512
NCH = TOK // CH
EPS = 1e-5
NEG = -1e30

H0, R0 = 8, 64
PAIRS = H0 // 2
E0 = 8
H1, HD1 = 16, 8
GROUPS = H1 // 4
STRIP = 32
DEPTH, H2, HD2, WIN = 2, 8, 64, 64
INNER = H2 * HD2
QK = 8.0
HID = int(D * 4 * 2 / 3)
ARENA = 15360
NPB = 4


class Chain:

    def __init__(self, eng, sem, base=0):
        self.eng, self.sem, self.base, self.n = eng, sem, base, 0

    def link(self, ins):
        ins.then_inc(self.sem, 1)
        self.n += 1

    def settle(self):
        self.eng.wait_ge(self.sem, self.base + self.n)

    def step(self, ins):
        self.link(ins)
        self.settle()


def build(nc, a, out):
    with ExitStack() as ctx:
        def sb(name, shape, dt=F32):
            return ctx.enter_context(nc.sbuf_tensor(name, shape, dt))

        def sem(name):
            return ctx.enter_context(nc.semaphore(name))

        x_sb = sb("x_sb", [P, TILES, D])
        xn = sb("xn", [P, TILES, D])
        xT = sb("xT", [P, TOK])
        yT = sb("yT", [P, TOK])
        ident = sb("ident", [P, P])
        stats = sb("stats", [P, TILES, 6])
        mv = sb("mv", [P, TILES, 2])
        sd = sb("sd", [P, TILES])
        rstd = sb("rstd", [P, TILES])
        eps_c = sb("eps_c", [P, 1])
        ps = ctx.enter_context(nc.psum_tensor("ps", [P, 8, CH], F32))

        q_st = sb("q_st", [P, SEQ])
        k_st = sb("k_st", [P, SEQ])
        v_st = sb("v_st", [P, QT, 256])
        probs = sb("probs", [P, NPB, SEQ])
        probsT = sb("probsT", [P, 2, QT, CH])
        negmax = sb("negmax", [P, 2 * STRIP])
        rowsum = sb("rowsum", [P, 2 * STRIP])
        rrow = sb("rrow", [P, 2 * STRIP])
        wq_st = sb("wq_st", [P, P])
        wk_st = sb("wk_st", [P, P])
        wv_st = sb("wv_st", [P, 256])
        w0qk = sb("w0qk", [P, 2, PAIRS + 1, P])
        w0q, w0k = w0qk[:, 0, :, :], w0qk[:, 1, :, :]
        w0v = sb("w0v", [P, PAIRS + 1, 256])
        wnat = probsT[:, 0, :, :].rearrange("p k (n c) -> p (k n) c", c=P)[:, 0:16, :]

        arena = sb("arena", [P, ARENA])

        def carve(at, *shape):
            n = 1
            for x in shape:
                n *= x
            v = arena[:, at:at + n]
            if len(shape) > 1:
                names = "abcd"[:len(shape)]
                v = v.rearrange(f"p ({' '.join(names)}) -> p {' '.join(names)}",
                                **{c: x for c, x in zip(names[1:], shape[1:])})
            return v, at + n

        fnat, at = carve(0, 30, P)
        gnat = sb("gnat", [STRIP, P])
        fT, at = carve(at, E0 + 1, 3, P)
        swT, at = carve(at, 6, P)
        gateT = sb("gateT", [P, E0])
        work2 = sb("work2", [P, DEPTH * 3 * INNER])
        fb = sb("fb", [P, E0 + 1, 3])
        sel_f, at = carve(at, E0, 2, P)
        sel_f = sel_f[0:STRIP]
        sel, at = carve(at, (E0 + 1) * P)
        sel = sel[0:STRIP].bitcast(BF16).rearrange("p (e n c) -> p e n c", e=E0 + 1, n=2)
        iota8 = sb("iota8", [P, TILES, E0])
        G = work2[:, 0:512].rearrange("p (t e) -> p t e", e=STRIP)
        gT = work2[0:STRIP, 512:1536].bitcast(BF16)
        e_w = work2[:, 1536:2304].rearrange("p (s n c) -> p s n c", s=2, n=3)
        e_b = sb("e_b", [P, 2, 3])
        e_sel = work2[0:STRIP, 2304:2560].bitcast(BF16).rearrange("p (s n c) -> p s n c", s=2, n=2)
        ws = probsT[:, :, :, :].rearrange("p a k c -> p (a k) c")
        e_xs, e_mask, e_h, e_t3, e_t = (ws[:, 2 * i:2 * i + 2, :] for i in range(5))
        e_sg, e_sh = ws[:, 10:12, :], ws[:, 12:14, :]
        gw = probs[:, 0, :].rearrange("p (n t e) -> p n t e", t=TILES, e=E0)
        gmax = sb("gmax", [P, TILES])
        gsum = sb("gsum", [P, TILES])
        top_i = sb("top_i", [P, TILES, E0], U32)

        nat3 = sb("nat3", [P, 4, P])
        b3n = sb("b3n", [P, 3])
        w3o = sb("w3o", [P, GROUPS, P])
        b3o = sb("b3o", [P, 1])
        bias_y = sb("bias_y", [P, 1])
        slopes = sb("slopes", [P, H1 + 4])
        rel = sb("rel", [P, SEQ])
        sel_q = sb("sel_q", [STRIP, QT, P])
        v_nat = sb("v_nat", [P, TILES, P])
        scr = nc.dram_tensor("c_parts", (2, 3, BATCH, P, SEQ), BF16, kind="Internal").ap()
        c_qs = [q_st[:, :].bitcast(BF16).rearrange("p (c n) -> p c n", c=2),
                yT[:, 0:SEQ].bitcast(BF16).rearrange("p (c n) -> p c n", c=2)]
        c_ks = [k_st[:, :].bitcast(BF16).rearrange("p (c n) -> p c n", c=2),
                yT[:, SEQ:TOK].bitcast(BF16).rearrange("p (c n) -> p c n", c=2)]
        c_v = v_st[:, :, :].rearrange("p a b -> p (a b)").rearrange("p (b k c) -> p b k c", b=2, k=QT)
        c_sb, at = carve(0, 2, SEQ)
        c_T, at = carve(at, 4, SEQ)
        c_part = arena[:, ARENA - 6 * SEQ:ARENA].bitcast(BF16).rearrange("p (w b n c) -> p w b n c", w=2, b=2, n=3)
        oT1, at = carve(at, GROUPS + 1, SEQ)
        oT0, at = carve(at, GROUPS, SEQ)
        c_o = w0qk[:, :, :, :].rearrange("p a b c -> p (a b c)")[:, 0:SEQ]
        c_rT = sb("c_rT", [STRIP, P])
        cmax = sb("cmax", [P, STRIP])
        c_pT = probsT[:, :, :, :].rearrange("p a k c -> p a (k c)").rearrange("p a (j k q) -> p a j k q", j=4, k=QT)

        M1 = [(0, P), (P, P), (2 * P, HID - 2 * P)]
        w4qkv = work2[:, :].rearrange("p (l n) -> p l n", l=DEPTH)
        w4o = w0v[:, 0:4, :].rearrange("p s c -> p (s c)").rearrange("p (l n c) -> p l n c", l=DEPTH, c=P)
        b4 = sb("b4", [P, DEPTH, 9])
        half_c = sb("half_c", [P, 2 * H2])
        ident_b = sb("ident_b", [P, P], BF16)
        mask_b = rel[:, :].bitcast(BF16).rearrange("p (t c) -> p t c", c=P)
        rot_c, at = carve(0, TILES, 2, HD2)
        rot_s, at = carve(at, TILES, 2, HD2)
        base_c, at = carve(at, QT, 2, HD2)
        base_s, at = carve(at, QT, 2, HD2)
        mask_f, at = carve(at, 2, P)
        hT, at = carve(at, WIN + TOK)
        l_qkv, at = carve(at, 3 * INNER)
        l_o, at = carve(at, 4, P)
        l_up, at = carve(at, 2 * HID)
        l_down, at = carve(at, 3, P)
        w4up, at = carve(at, DEPTH, 2 * HID)
        w4down, at = carve(at, DEPTH, 3, P)
        qk_scale, at = carve(at, DEPTH, 2, HD2)
        hq, at = carve(at, 2, P)
        hv, at = carve(at, 2, P)
        assert at <= ARENA
        l_b = sb("l_b", [P, 9])
        ss = sb("ss", [P, 2, 2 * H2])
        d_nm = sb("d_nm", [P, 2, H2])
        d_nm8 = sb("d_nm8", [P, 2, H2])
        d_sum = sb("d_sum", [P, 2, H2])
        d_rr = sb("d_rr", [P, 2, H2])
        d_mA = probs[:, 0:2, :]
        d_mB = probs[:, 2:4, :]
        gbuf = probs[:, :, :].rearrange("p n c -> p (n c)")[:, 0:2 * 3 * CH]\
            .rearrange("p (n m c) -> p n m c", n=2, m=3)
        d_kq = [q_st[:, :], k_st[:, :]]
        d_sq = v_st[:, :, :].rearrange("p a b -> p (a b)").rearrange("p (n c) -> p n c", n=2)
        pf = probsT[:, :, :, :].rearrange("p a k c -> p (a k c)")
        d_p = pf[:, 0:2048].rearrange("p (n h c) -> p n h c", n=2, h=H2)
        d_pT = pf[:, 2048:3072].rearrange("p (h c) -> p h c", h=H2)
        d_kT = pf[:, 3072:4096].rearrange("p (n m c) -> p n m c", n=2, m=4)
        d_qT = pf[:, 4096:4608].rearrange("p (m c) -> p m c", m=4)
        d_o = pf[:, 4608:5632].rearrange("p (n m c) -> p n m c", n=2, m=4)
        d_va = pf[:, 5632:6656].rearrange("p (n c) -> p n c", n=2)
        d_vs = pf[:, 6656:7680].rearrange("p (n c) -> p n c", n=2)

        s_ld_x = sem("s_ld_x")
        s_ld_w0 = sem("s_ld_w0")
        s_ld_f = sem("s_ld_f")
        s_ld_c = sem("s_ld_c")
        s_ld_z = sem("s_ld_z")
        s_out = sem("s_out")
        s_eps = sem("s_eps")
        s_var = sem("s_var")
        s_sd = sem("s_sd")
        s_xn = sem("s_xn")
        s_xTp = sem("s_xTp")
        s_xT = sem("s_xT")
        s_yp = sem("s_yp")
        s_dve = sem("s_dve")
        s_yn = sem("s_yn")
        s_res = sem("s_res")
        s_y = [sem(f"s_y{n}") for n in range(4)]
        s_w0p = sem("s_w0p")
        s_w0t = sem("s_w0t")
        s_a_wst = sem("s_a_wst")
        s_a_projq = sem("s_a_projq")
        s_a_projk = sem("s_a_projk")
        s_a_projv0 = sem("s_a_projv0")
        s_a_projv1 = sem("s_a_projv1")
        s_a_q = sem("s_a_q")
        s_a_k = sem("s_a_k")
        s_a_v0 = sem("s_a_v0")
        s_a_v1 = sem("s_a_v1")
        s_a_scores = sem("s_a_scores")
        s_a_negmax = sem("s_a_negmax")
        s_a_exp = sem("s_a_exp")
        s_a_rrow = sem("s_a_rrow")
        s_a_norm = sem("s_a_norm")
        s_a_trans = sem("s_a_trans")
        s_a_evA = sem("s_a_evA")
        s_a_evB = sem("s_a_evB")
        s_a_pv = sem("s_a_pv")
        s_a_oadd = sem("s_a_oadd")
        s_a_ozero = sem("s_a_ozero")
        s_fp = sem("s_fp")
        s_ft = sem("s_ft")
        s_selc = sem("s_selc")
        s_logits = sem("s_logits")
        s_gshift = sem("s_gshift")
        s_gexp = sem("s_gexp")
        s_G = sem("s_G")
        s_gTp = sem("s_gTp")
        s_gT = sem("s_gT")
        s_sh_g = sem("s_sh_g")
        s_sh_u = sem("s_sh_u")
        s_sh_silu = sem("s_sh_silu")
        s_sh_h = sem("s_sh_h")
        s_sh_z = sem("s_sh_z")
        s_sh_y = sem("s_sh_y")
        s_e_wA = sem("s_e_wA")
        s_e_wB = sem("s_e_wB")
        s_e_bc = sem("s_e_bc")
        s_e_xs = sem("s_e_xs")
        s_e_mask = sem("s_e_mask")
        s_e_h1 = sem("s_e_h1")
        s_e_x3 = sem("s_e_x3")
        s_e_h = sem("s_e_h")
        s_e_t3 = sem("s_e_t3")
        s_e_x2 = sem("s_e_x2")
        s_e_t = sem("s_e_t")
        s_e_y = sem("s_e_y")
        s_c_go = sem("s_c_go")
        s_c_proj = sem("s_c_proj")
        s_c_qe = sem("s_c_qe")
        s_c_ke = sem("s_c_ke")
        s_c_kr = sem("s_c_kr")
        s_c_pq = sem("s_c_pq")
        s_c_pk = sem("s_c_pk")
        s_c_scr = sem("s_c_scr")
        s_c_st = [sem(f"s_c_st{b}") for b in range(BATCH)]
        s_c_projv = sem("s_c_projv")
        s_c_v = sem("s_c_v")
        s_c_vz = sem("s_c_vz")
        s_c_vst = sem("s_c_vst")
        s_c_T = sem("s_c_T")
        s_c_scores = sem("s_c_scores")
        s_c_bias = sem("s_c_bias")
        s_c_negmax = sem("s_c_negmax")
        s_c_exp = sem("s_c_exp")
        s_c_transA = sem("s_c_transA")
        s_c_transB = sem("s_c_transB")
        s_c_evA = sem("s_c_evA")
        s_c_evB = sem("s_c_evB")
        s_c_pv = sem("s_c_pv")
        s_c_o = sem("s_c_o")
        s_c_rr = sem("s_c_rr")
        s_c_rrp = sem("s_c_rrp")
        s_c_rT = sem("s_c_rT")
        s_c_bc = sem("s_c_bc")
        s_c_oT = sem("s_c_oT")
        s_c_bp = sem("s_c_bp")
        s_c_by = sem("s_c_by")
        s_c_y = sem("s_c_y")
        s_c_yc = sem("s_c_yc")
        s_ld_d = sem("s_ld_d")
        s_ld_r = sem("s_ld_r")
        s_d_layer = sem("s_d_layer")
        s_d_go = sem("s_d_go")
        s_d_wst = sem("s_d_wst")
        s_d_wa = sem("s_d_wa")
        s_d_hq = sem("s_d_hq")
        s_d_hv = sem("s_d_hv")
        s_d_qkp = sem("s_d_qkp")
        s_d_vp = sem("s_d_vp")
        s_d_m = sem("s_d_m")
        s_d_sq = sem("s_d_sq")
        s_d_ss = sem("s_d_ss")
        s_d_cl = sem("s_d_cl")
        s_d_rn = sem("s_d_rn")
        s_d_add = sem("s_d_add")
        s_d_kq = sem("s_d_kq")
        s_d_qkt = sem("s_d_qkt")
        s_d_qT = sem("s_d_qT")
        s_d_kT = sem("s_d_kT")
        s_d_v = sem("s_d_v")
        s_d_vs = sem("s_d_vs")
        s_d_s = sem("s_d_s")
        s_d_nm = sem("s_d_nm")
        s_d_nm8 = sem("s_d_nm8")
        s_d_e = sem("s_d_e")
        s_d_rr = sem("s_d_rr")
        s_d_p = sem("s_d_p")
        s_d_pt = sem("s_d_pt")
        s_d_pT = sem("s_d_pT")
        s_d_pTa = sem("s_d_pTa")
        s_d_o = sem("s_d_o")
        s_d_oT = sem("s_d_oT")
        s_d_w = sem("s_d_w")
        s_d_z = sem("s_d_z")
        s_d_chain = sem("s_d_chain")
        s_f_hT = sem("s_f_hT")
        s_f_go = sem("s_f_go")
        s_f_hp = sem("s_f_hp")
        s_f_var = sem("s_f_var")
        s_f_sd = sem("s_f_sd")
        s_f_xn = sem("s_f_xn")
        s_f_xp = sem("s_f_xp")
        s_f_yT = sem("s_f_yT")
        s_f_g = sem("s_f_g")
        s_f_a = sem("s_f_a")
        s_f_ge = sem("s_f_ge")
        s_f_u = sem("s_f_u")
        s_f_y = sem("s_f_y")
        s_f_z = sem("s_f_z")
        s_d_init = sem("s_d_init")


        STACK = 16 * 24
        CU = 4 * QT

        block = ctx.enter_context(nc.Block())

        @block.sync
        def _(sp):
            for b in range(BATCH):
                sp.dma_start(x_sb[:, b * QT:(b + 1) * QT, :],
                             a["L0_attn_x"][b].rearrange("(t p) d -> p t d", p=P)).then_inc(s_ld_x, 16)
            sp.dma_start(ident[:, :], a["c_ident"]).then_inc(s_ld_w0, 16)
            sp.dma_start(wnat[:, 0:4, :], a["L0_attn_Wq"].rearrange("(n p) d -> p n d", p=P)).then_inc(s_ld_w0, 16)
            sp.dma_start(wnat[:, 4:8, :], a["L0_attn_Wk"].rearrange("(n p) d -> p n d", p=P)).then_inc(s_ld_w0, 16)
            sp.dma_start(wnat[:, 8:16, :], a["L0_attn_Wv"].rearrange("(n p) d -> p n d", p=P)).then_inc(s_ld_w0, 16)
            for i, w in enumerate(("L0_ffn_w1", "L0_ffn_w2", "L0_ffn_w3")):
                sp.dma_start(fnat[:, 8 * i:8 * i + 8, :], a[w].rearrange("e h d -> h e d")).then_inc(s_ld_f, 16)
            sp.dma_start(fnat[:, 24:26, :], a["L0_ffn_sw1"].rearrange("(n p) d -> p n d", p=P)).then_inc(s_ld_f, 16)
            sp.dma_start(fnat[:, 26:28, :], a["L0_ffn_sw2"].rearrange("(n p) d -> p n d", p=P)).then_inc(s_ld_f, 16)
            sp.dma_start(fnat[:, 28:30, :], a["L0_ffn_sw3"].rearrange("d (n i) -> d n i", n=2)).then_inc(s_ld_f, 16)
            for i, w in enumerate(("L0_ffn_gate_w", "L0_ffn_b1", "L0_ffn_b2", "L0_ffn_b3")):
                sp.dma_start(gnat[8 * i:8 * i + 8, :], a[w]).then_inc(s_ld_f, 16)
            sp.dma_start(sel_f[:, :, :, :], a["c_sel"]).then_inc(s_ld_f, 16)
            sp.dma_start(iota8[:, :, :], a["c_iota8"]).then_inc(s_ld_f, 16)
            for i, w in enumerate(("L1_attn_Wq", "L1_attn_Wk", "L1_attn_Wv", "L1_attn_Wo")):
                sp.dma_start(nat3[:, i, :], a[w]).then_inc(s_ld_c, 16)
            for i, w in enumerate(("L1_attn_bq", "L1_attn_bk", "L1_attn_bv")):
                sp.dma_start(b3n[:, i:i + 1], a[w].rearrange("(d o) -> d o", o=1)).then_inc(s_ld_c, 16)
            sp.dma_start(slopes[:, :], a["c_slopes"]).then_inc(s_ld_c, 16)
            sp.dma_start(rel[:, :], a["c_rel"]).then_inc(s_ld_c, 16)
            sp.dma_start(sel_q[:, :, :], a["c_selq"]).then_inc(s_ld_c, 16)
            sp.dma_start(b3o[:, :], a["L1_attn_bo"].rearrange("(d o) -> d o", o=1)).then_inc(s_ld_c, 16)
            sp.wait_ge(s_ld_z, 1)
            for j in range(4):
                r = STRIP * j
                sp.dma_start(w3o[r:r + HD1, :, :],
                             a["L1_attn_Wo"].rearrange("(g j e) o -> j e g o", j=4, e=HD1)[j]).then_inc(s_ld_c, 16)
            sp.wait_ge(s_y[1], 1)
            sp.dma_start(w4qkv[:, :, :], a["L1_ffn_wqkv"].rearrange("l d n -> d l n")).then_inc(s_ld_d, 16)
            sp.dma_start(w4o, a["L1_ffn_wo"].rearrange("l (n p) d -> p l n d", p=P)).then_inc(s_ld_d, 16)
            def c_stack(g, b):
                for j in range(4):
                    head = bass.ds((4 * g + j) * HD1, HD1)
                    for part, times in enumerate((3, 3, 2)):
                        r = 64 * (j % 2) + 24 * part
                        sp.dma_start(c_qs[b][r:r + HD1 * times, j // 2, :],
                                     scr[0, part, b, head, :].unsqueeze(0).to_broadcast([times, HD1, SEQ]))\
                          .then_inc(s_c_st[b], 16)
                        sp.dma_start(c_ks[b][r:r + HD1 * times, j // 2, :], scr[1, 0:times, b, head, :])\
                          .then_inc(s_c_st[b], 16)

            for b in range(BATCH):
                for w, whole in ((0, s_c_pq), (1, s_c_pk)):
                    sp.wait_ge(whole, b + 1)
                    sp.dma_start(scr[w, :, b, :, :].rearrange("n p c -> p n c"), c_part[:, w, b, :, :])\
                      .then_inc(s_c_scr, 16)
                sp.wait_ge(s_c_scr, 32 * (b + 1))
                c_stack(0, b)
            with sp.Fori(0, GROUPS - 1) as g:
                for b in range(BATCH):
                    sp.wait_ge(s_c_scores, 8 * QT * g + 4 * QT * (b + 1))
                    sp.sem_inc(s_c_go, 1)
                    c_stack(g + 1, b)
            sp.wait_ge(s_c_scores, 2 * CU * (GROUPS - 1) + 1)
            sp.sem_inc(s_c_st[0], STACK)
            sp.wait_ge(s_y[2], 1)
            sp.dma_start(base_c, a["c_rotc"].rearrange("(t p) n d -> p t n d", p=P)).then_inc(s_ld_r, 16)
            sp.dma_start(base_s, a["c_rots"].rearrange("(t p) n d -> p t n d", p=P)).then_inc(s_ld_r, 16)
            sp.dma_start(mask_f, a["c_mask"]).then_inc(s_ld_r, 16)
            sp.dma_start(w4up[:, :, :], a["L1_ffn_w1"].rearrange("l d n -> d l n")).then_inc(s_ld_d, 16)
            for l in range(DEPTH):
                for m, (r, n) in enumerate(M1):
                    sp.dma_start(w4down[0:n, l, m, :], a["L1_ffn_w2"][l, r:r + n, :]).then_inc(s_ld_d, 16)
                    for part in range(2):
                        sp.dma_start(b4[0:n, l, 3 * part + m:3 * part + m + 1],
                                     a["L1_ffn_b1"][l, HID * part + r:HID * part + r + n]
                                     .rearrange("(d o) -> d o", o=1)).then_inc(s_ld_d, 16)
                for m, w in enumerate(("L1_ffn_b2", "L1_ffn_ln_g", "L1_ffn_ln_b")):
                    sp.dma_start(b4[:, l, 6 + m:7 + m], a[w][l].rearrange("(d o) -> d o", o=1)).then_inc(s_ld_d, 16)
                for m, w in enumerate(("L1_ffn_q_scale", "L1_ffn_k_scale")):
                    sp.dma_start(qk_scale[:, l, m, :], a[w][l].partition_broadcast(P)).then_inc(s_ld_d, 16)
            for b in range(BATCH):
                sp.wait_ge(s_res, 3 * NCH + 2 * (b + 1))
                sp.dma_start(out[b].rearrange("(t p) d -> p t d", p=P),
                             x_sb[:, b * QT:(b + 1) * QT, :]).then_inc(s_out, 16)
            sp.wait_ge(s_out, 16 * BATCH)

        NU = 16

        def exists(t, shift):
            return not isinstance(t, int) or 0 <= t + shift < TILES

        def walk(eng, step, last):
            step(0, 0)
            step(1, 1)
            with eng.Fori(1, 6) as i:
                step(2 * i, 0)
                step(2 * i + 1, 1)
            for t in range(12, last):
                step(t, t % 2)

        @block.tensor
        def _(pe):
            def norm_in(k):
                for g in range(NCH):
                    pe.wait_ge(s_xn, NCH * k + g + 1)
                    for i in range(4):
                        ins = pe.transpose(ps[:, g, i * P:(i + 1) * P], xn[:, 4 * g + i, :], ident[:, :])
                    ins.then_inc(s_xTp, 1)

            def norm_out(k, src=yT):
                for g in range(NCH):
                    for i in range(4):
                        t = 4 * g + i
                        ins = pe.transpose(ps[:, g, i * P:(i + 1) * P], src[:, t * P:(t + 1) * P], ident[:, :])
                    ins.then_inc(s_yp, 1)

            pe.wait_ge(s_ld_w0, 16 * 4)
            for g in range(4):
                for i in range(4):
                    ins = pe.transpose(ps[:, 4 + g, i * P:(i + 1) * P], wnat[:, 4 * g + i, :], ident[:, :])
                ins.then_inc(s_w0p, 1)
            norm_in(0)
            pe.wait_ge(s_ld_f, 16 * 12)
            for g in range(9):
                if g < 4:
                    pe.wait_ge(s_w0t, 1)
                else:
                    pe.wait_ge(s_ft, g - 3)
                if g == 8:
                    ins = pe.transpose(ps[:, 4, 0:STRIP], gnat[:, :], ident[0:STRIP, 0:STRIP])
                else:
                    for i in range(min(4, 30 - 4 * g)):
                        ins = pe.transpose(ps[:, 4 + g % 4, i * P:(i + 1) * P], fnat[:, 4 * g + i, :], ident[:, :])
                ins.then_inc(s_fp, 1)

            def a_proj_q(b):
                for n in range(2):
                    ins = pe.matmul(ps[:, n, :], wq_st[:, :], xT[:, b * SEQ + n * CH:b * SEQ + (n + 1) * CH],
                                    start=True, stop=True)
                ins.then_inc(s_a_projq, 1)

            def a_proj_k(b):
                for n in range(2):
                    ins = pe.matmul(ps[:, 2 + n, :], wk_st[:, :], xT[:, b * SEQ + n * CH:b * SEQ + (n + 1) * CH],
                                    start=True, stop=True)
                ins.then_inc(s_a_projk, 1)

            def a_proj_v(b, m):
                pe.wait_ge(s_a_q, m)
                for half, done in ((0, s_a_projv0), (1, s_a_projv1)):
                    if half:
                        pe.wait_ge(s_a_k, m)
                    for i in range(4):
                        kt = 4 * half + i
                        t = b * QT + kt
                        ins = pe.matmul(ps[:, kt // 2, (kt % 2) * 256:(kt % 2) * 256 + 256],
                                        xT[:, t * P:(t + 1) * P], wv_st[:, :], start=True, stop=True)
                    ins.then_inc(done, 1)

            pe.wait_ge(s_xT, NCH)
            pe.wait_ge(s_a_wst, 1)
            a_proj_q(0)
            a_proj_k(0)
            a_proj_v(0, 1)

            with pe.Fori(0, PAIRS) as p:
                for b in range(BATCH):
                    n0 = 2 * NU * p + NU * b
                    m = 2 * p + b

                    def scores(u):
                        r, qt = R0 * (u // QT), u % QT
                        if u == 0:
                            pe.wait_ge(s_a_q, m + 1)
                            pe.wait_ge(s_a_k, m + 1)
                            pe.wait_ge(s_a_v0, m + 1)
                        elif u == 1:
                            pe.wait_ge(s_a_v1, m + 1)
                        else:
                            pe.wait_ge(s_a_exp, n0 + u - 1)
                        for n in range(2):
                            ins = pe.matmul(ps[:, 2 * (u % 2) + n, :], q_st[r:r + R0, qt * P:(qt + 1) * P],
                                            k_st[r:r + R0, n * CH:(n + 1) * CH], start=True, stop=True)
                        ins.then_inc(s_a_scores, 1)

                    def turn(u):
                        pe.wait_ge(s_a_norm, n0 + u + 1)
                        for half, free in ((0, s_a_evA), (1, s_a_evB)):
                            pe.wait_ge(free, n0 + u + 1)
                            for i in range(4):
                                kt = 4 * half + i
                                ins = pe.transpose(ps[:, 4 + half, i * P:(i + 1) * P],
                                                   probs[:, u % NPB, kt * P:(kt + 1) * P], ident[:, :])
                            ins.then_inc(s_a_trans, 1)

                    def weigh(c, k0, k1):
                        head, qc = c // 2, c % 2
                        if k0 == 0:
                            pe.wait_ge(s_a_evA, n0 + 4 * c + 5)
                            pe.wait_ge(s_a_evB, n0 + 4 * c + 5)
                            if head == 0:
                                pe.wait_ge(s_a_oadd, 2 * m + 1)
                        for kt in range(k0, k1):
                            ins = pe.matmul(ps[:, 6 + qc, :], v_st[:, kt, head * P:(head + 1) * P],
                                            probsT[:, c % 2, kt, :], start=(head == 0 and kt == 0),
                                            stop=(head == 1 and kt == QT - 1), skip_group_check=True)
                        if head == 1 and k1 == QT:
                            ins.then_inc(s_a_pv, 1)

                    for u in range(NU):
                        scores(u)
                        if u >= 2:
                            turn(u - 2)
                        if u >= 6:
                            c, k = (u - 6) // 4, (u - 6) % 4
                            weigh(c, 2 * k, 2 * k + 2)
                    nb = 1 - b
                    if b == 1:
                        pe.wait_ge(s_a_wst, p + 2)
                    pe.wait_ge(s_a_exp, n0 + NU - 1)
                    a_proj_q(nb)
                    turn(NU - 2)
                    weigh(2, 4, 6)
                    pe.wait_ge(s_a_exp, n0 + NU)
                    a_proj_k(nb)
                    turn(NU - 1)
                    weigh(2, 6, 8)
                    weigh(3, 0, 8)
                    a_proj_v(nb, m + 2)

            pe.wait_ge(s_y[0], 1)
            pe.wait_ge(s_a_v0, 2 * PAIRS + 1)
            pe.wait_ge(s_a_v1, 2 * PAIRS + 1)
            norm_out(0)

            norm_in(1)
            pe.wait_ge(s_xT, NCH * 2)
            pe.wait_ge(s_ft, 9)
            for t in range(TILES):
                ins = pe.matmul(ps[:, 7, t * E0:(t + 1) * E0], xT[:, t * P:(t + 1) * P], gateT[:, :],
                                start=True, stop=True)
            ins.then_inc(s_logits, 1)

            def shared_down(k):
                c, m = k // 2, k % 2
                pe.wait_ge(s_sh_h, k + 1)
                if m == 0 and c >= 2:
                    pe.wait_ge(s_sh_y, c - 1)
                ins = pe.matmul(ps[:, 4 + c % 2, :], swT[:, 4 + m, :], e_sh[:, k % 2, :],
                                start=(m == 0), stop=(m == 1))
                if m == 1:
                    ins.then_inc(s_sh_z, 1)

            for k in range(2 * NCH):
                c, m = k // 2, k % 2
                x = xT[:, c * CH:(c + 1) * CH]
                if k >= 2:
                    pe.wait_ge(s_sh_silu, k - 1)
                    pe.wait_ge(s_sh_h, k - 1)
                pe.matmul(ps[:, k % 2, :], swT[:, m, :], x, start=True, stop=True).then_inc(s_sh_g, 1)
                pe.matmul(ps[:, 2 + k % 2, :], swT[:, 2 + m, :], x, start=True, stop=True).then_inc(s_sh_u, 1)
                if k >= 1:
                    shared_down(k - 1)
            shared_down(2 * NCH - 1)
            pe.wait_ge(s_G, 1)
            for g in range(NCH):
                if g >= 2:
                    pe.wait_ge(s_gT, g - 1)
                for i in range(4):
                    ins = pe.transpose(ps[0:STRIP, 6 + g % 2, i * P:(i + 1) * P], G[:, 4 * g + i, :], ident[:, :])
                ins.then_inc(s_gTp, 1)

            pe.wait_ge(s_gT, NCH)
            pe.wait_ge(s_sh_y, NCH)
            with pe.Fori(0, E0 // 2) as i:
                n0 = 2 * NCH * i

                def spread(k):
                    s, c = k // NCH, k % NCH
                    if k == 0:
                        pe.wait_ge(s_e_wA, i + 1)
                    if k == NCH:
                        pe.wait_ge(s_e_wB, i + 1)
                    if k >= 2:
                        pe.wait_ge(s_e_xs, n0 + k - 1)
                    if k >= 1:
                        pe.wait_ge(s_e_mask, n0 + k)
                    g = gT[:, c * CH:(c + 1) * CH]
                    pe.matmul(ps[:, k % 2, :], e_sel[:, s, 0, :], g, start=True, stop=True)
                    pe.matmul(ps[:, 2, :], e_sel[:, s, 1, :], g, start=True, stop=True).then_inc(s_e_bc, 1)

                def down(k):
                    pe.wait_ge(s_e_h, n0 + k + 1)
                    if k >= 1:
                        pe.wait_ge(s_e_t, n0 + k)
                    pe.matmul(ps[:, 7, :], e_w[:, k // NCH, 2, :], e_h[:, k % 2, :],
                              start=True, stop=True).then_inc(s_e_x2, 1)

                spread(0)
                for k in range(2 * NCH):
                    s = k // NCH
                    pe.wait_ge(s_e_xs, n0 + k + 1)
                    pe.matmul(ps[:, 3 + k % 2, :], e_w[:, s, 0, :], e_xs[:, k % 2, :],
                              start=True, stop=True).then_inc(s_e_h1, 1)
                    if k < 2 * NCH - 1:
                        spread(k + 1)
                    if k >= 2:
                        pe.wait_ge(s_e_t3, n0 + k - 1)
                    pe.matmul(ps[:, 5 + k % 2, :], e_w[:, s, 1, :], e_xs[:, k % 2, :],
                              start=True, stop=True).then_inc(s_e_x3, 1)
                    if k >= 1:
                        down(k - 1)
                down(2 * NCH - 1)
            pe.wait_ge(s_y[1], 1)
            norm_out(1)

            norm_in(2)

            pe.wait_ge(s_xT, NCH * 3)
            pe.wait_ge(s_ld_c, 16 * 15)
            pe.matmul(ps[:, 4, 0:1], nat3[:, 3, :], b3n[:, 2:3], start=True, stop=True).then_inc(s_c_bp, 1)
            for b in range(BATCH):
                if b == 1:
                    pe.wait_ge(s_c_by, 1)
                for w in range(2):
                    for n in range(2):
                        ins = pe.matmul(ps[:, 4 * b + 2 * w + n, :], nat3[:, w, :],
                                        xT[:, b * SEQ + n * CH:b * SEQ + (n + 1) * CH], start=True, stop=True)
                    ins.then_inc(s_c_proj, 1)
            pe.wait_ge(s_c_qe, 1)
            pe.wait_ge(s_c_ke, 1)
            for t in range(TILES):
                ins = pe.matmul(ps[:, t // 4, (t % 4) * P:(t % 4 + 1) * P], xT[:, t * P:(t + 1) * P],
                                nat3[:, 2, :], start=True, stop=True)
            ins.then_inc(s_c_projv, 1)
            pe.wait_ge(s_c_qe, 2)
            pe.wait_ge(s_c_ke, 4)
            pe.wait_ge(s_c_v, 1)

            def c_scores(b, u):
                r, c, qt = 64 * (u % 2), u % 4 // 2, u // 4
                w = (qt + 1) * P
                for n in range((w + CH - 1) // CH):
                    e = min(w, (n + 1) * CH)
                    ins = pe.matmul(ps[:, 2 * (u % 2) + n, 0:e - n * CH],
                                    c_qs[b][r:r + 64, c, qt * P:(qt + 1) * P],
                                    c_ks[b][r:r + 64, c, n * CH:e], start=True, stop=True)
                ins.then_inc(s_c_scores, 1)

            def c_turn_sums(f, b, h0):
                pe.wait_ge(s_c_rr, f + 1)
                pe.wait_ge(s_c_evB, h0 + 1)
                pe.transpose(ps[0:STRIP, 5, 0:P], rrow[:, CU * (1 - b):CU * (2 - b)], ident[:, :])\
                  .then_inc(s_c_rrp, 1)

            def c_spread(f, qt):
                if qt == 0:
                    pe.wait_ge(s_c_rT, f + 1)
                if qt == 4:
                    pe.wait_ge(s_c_oT, 2 * f + 1)
                ins = pe.matmul(ps[:, 5, (qt % 4) * P:(qt % 4 + 1) * P], sel_q[:, qt, :], c_rT[:, :],
                                start=True, stop=True)
                if qt % 4 == 3:
                    ins.then_inc(s_c_bc, 1)

            def c_weigh(b, qt, k0, k1):
                for kt in range(k0, k1):
                    for j in range(4):
                        ins = pe.matmul(ps[STRIP * j:STRIP * j + STRIP, 6 + qt % 2, 0:P],
                                        c_v[:, b, kt, STRIP * j:STRIP * j + STRIP],
                                        c_pT[:, qt % 2, j, kt, :], start=(kt == 0), stop=(kt == qt),
                                        tile_position=(0, STRIP * j))
                if k1 == qt + 1:
                    ins.then_inc(s_c_pv, 1)

            def c_weigh_last(m, b, i):
                if i == 0:
                    pe.wait_ge(s_c_evA, CU * m + 1)
                    pe.wait_ge(s_c_evB, CU // 2 * m + 1)
                    pe.wait_ge(s_c_o, QT * m + 1)
                c_weigh(1 - b, QT - 1, (0, 3, 6)[i], (3, 6, 8)[i])

            pe.wait_ge(s_c_vst, 2)
            pe.wait_ge(s_c_st[0], STACK)
            c_scores(0, 0)
            c_scores(0, 1)
            with pe.Fori(0, GROUPS) as g:
                for b in range(BATCH):
                    n0 = 2 * CU * g + CU * b
                    m = 2 * g + b
                    h0 = CU // 2 * m

                    def turn(u):
                        qt = u // 4
                        pe.wait_ge(s_c_exp, n0 + u + 1)
                        pe.wait_ge(s_c_evA, n0 + u + 1)
                        for kt in range(min(4, qt + 1)):
                            ins = pe.transpose(ps[:, 4, kt * P:(kt + 1) * P],
                                               probs[:, u % NPB, kt * P:(kt + 1) * P], ident[:, :])
                        ins.then_inc(s_c_transA, 1)
                        if qt >= 4:
                            if u == CU // 2:
                                pe.wait_ge(s_c_oT, 2 * m + 2)
                            pe.wait_ge(s_c_evB, h0 + u - CU // 2 + 1)
                            for kt in range(4, qt + 1):
                                ins = pe.transpose(ps[:, 5, (kt - 4) * P:(kt - 3) * P],
                                                   probs[:, u % NPB, kt * P:(kt + 1) * P], ident[:, :])
                            ins.then_inc(s_c_transB, 1)

                    def weigh(qt, i):
                        parts = min(4, qt + 1)
                        if i >= parts:
                            return
                        if i == 0:
                            if qt == 0:
                                pe.wait_ge(s_c_vst, m + 1)
                            pe.wait_ge(s_c_evA, n0 + 4 * qt + 5)
                            if qt >= 4:
                                pe.wait_ge(s_c_evB, h0 + 4 * (qt - 4) + 5)
                            pe.wait_ge(s_c_o, QT * m + qt + 1)
                        c_weigh(b, qt, (qt + 1) * i // parts, (qt + 1) * (i + 1) // parts)

                    for u in range(CU):
                        if u >= 2:
                            pe.wait_ge(s_c_bias, n0 + u - 1)
                            c_scores(b, u)
                        if u >= 3:
                            turn(u - 3)
                        if u == 2:
                            c_turn_sums(m, b, h0)
                        if 4 <= u < 8:
                            c_spread(m, u - 4)
                        if 9 <= u < 13:
                            c_spread(m, u - 5)
                        if 2 <= u < 5:
                            c_weigh_last(m, b, u - 2)
                        if u >= 7:
                            weigh((u - 7) // 4, (u - 7) % 4)
                    pe.wait_ge(s_c_st[1 - b], STACK * (g + 1 + b))
                    pe.wait_ge(s_c_bias, n0 + CU - 1)
                    c_scores(1 - b, 0)
                    turn(CU - 3)
                    weigh(QT - 2, 1)
                    turn(CU - 2)
                    weigh(QT - 2, 2)
                    pe.wait_ge(s_c_bias, n0 + CU)
                    c_scores(1 - b, 1)
                    turn(CU - 1)
                    weigh(QT - 2, 3)
            m = 2 * GROUPS
            for i in range(3):
                c_weigh_last(m, 0, i)
            c_turn_sums(m, 0, CU // 2 * m)
            for qt in range(QT):
                c_spread(m, qt)

            pe.wait_ge(s_c_oT, 4 * GROUPS + 2)
            pe.wait_ge(s_c_o, QT * m + 2)
            for c in range(NCH):
                for g in range(GROUPS):
                    o = (oT0[:, g, :], oT1[:, g + 1, :])[c // 2]
                    ins = pe.matmul(ps[:, 4 + c, :], w3o[:, g, :], o[:, (c % 2) * CH:(c % 2 + 1) * CH],
                                    start=(g == 0), stop=(g == GROUPS - 1))
                ins.then_inc(s_c_y, 1)
            pe.wait_ge(s_c_yc, NCH)
            norm_out(2)

            norm_in(3)
            pe.wait_ge(s_d_init, 1)
            with pe.Fori(0, DEPTH) as l:
                T0 = TILES * l

                def proj_qk(t, par):
                    n = T0 + t
                    pe.wait_ge(s_d_hq, n + 1)
                    if exists(t, -1):
                        pe.wait_ge(s_d_m, n)
                        pe.wait_ge(s_d_sq, n)
                    for i in range(2):
                        ins = pe.matmul(ps[:, i, :], hq[:, par, :], l_qkv[:, i * INNER:(i + 1) * INNER],
                                        start=True, stop=True)
                    ins.then_inc(s_d_qkp, 1)

                def step(t, par):
                    n = T0 + t
                    if exists(t, 0):
                        pe.wait_ge(s_d_kq, n + 1)
                        if exists(t, -2):
                            pe.wait_ge(s_d_pTa, n - 1)
                            pe.wait_ge(s_d_pT, n - 1)
                        for i in range(2 * 4):
                            ins = pe.transpose(ps[:, 4 + i // 4, (i % 4) * P:(i % 4 + 1) * P],
                                               d_kq[par][:, i * P:(i + 1) * P], ident[:, :])
                        ins.then_inc(s_d_qkt, 1)
                    if exists(t, 2):
                        proj_qk(t + 2, par)
                    if exists(t, 0):
                        pe.wait_ge(s_d_hv, n + 1)
                        if exists(t, -2):
                            pe.wait_ge(s_d_z, n - 1)
                        if exists(t, -1):
                            pe.wait_ge(s_d_v, n)
                        pe.matmul(ps[:, 3, :], hv[:, par, :], l_qkv[:, 2 * INNER:3 * INNER],
                                  start=True, stop=True).then_inc(s_d_vp, 1)
                        pe.wait_ge(s_d_qT, n + 1)
                        pe.wait_ge(s_d_kT, n + 1)
                    if exists(t, -1):
                        pe.wait_ge(s_d_p, n)
                        for h in range(H2):
                            ins = pe.transpose(ps[:, 4 + h // 4, (h % 4) * P:(h % 4 + 1) * P],
                                               d_p[:, 1 - par, h, :], ident[:, :])
                        ins.then_inc(s_d_pt, 1)
                    if exists(t, 0):
                        if exists(t, -1):
                            pe.wait_ge(s_d_e, n)
                        for i in range(2):
                            pe.matmul(ps[:, 6 + i, :].rearrange("p (h c) -> p h c", c=P), ident_b[:, :],
                                      mask_b[:, bass.ds(t, 1), :].to_broadcast([P, 4, P]),
                                      start=True, stop=False, skip_group_check=True)
                        for h in range(H2):
                            r, m = HD2 * (h % 2), h // 2
                            o = ps[:, 6 + h % 2, m * P:(m + 1) * P]
                            pe.matmul(o[0:WIN, 0:WIN], d_qT[r:r + HD2, m, 0:WIN], d_kT[r:r + HD2, par, m, 0:WIN],
                                      start=False, stop=False, skip_group_check=True)
                            pe.matmul(o[0:WIN, WIN:P], d_qT[r:r + HD2, m, 0:WIN], d_kT[r:r + HD2, 1 - par, m, WIN:P],
                                      start=False, stop=False, skip_group_check=True)
                            ins = pe.matmul(o[WIN:P, :], d_qT[r:r + HD2, m, WIN:P], d_kT[r:r + HD2, par, m, :],
                                            start=False, stop=True, skip_group_check=True)
                        ins.then_inc(s_d_s, 1)
                    if exists(t, -2):
                        pe.wait_ge(s_d_oT, n - 1)
                        if exists(t, 0):
                            pe.wait_ge(s_d_v, n + 1)
                        elif t == TILES + 1:
                            pe.wait_ge(s_d_z, n - 1)
                        for m in range(4):
                            ins = pe.matmul(ps[:, 3, 0:P], l_o[:, m, :], d_o[:, par, m, :],
                                            start=(m == 0), stop=(m == 3))
                        ins.then_inc(s_d_w, 1)
                    if exists(t, -1):
                        pe.wait_ge(s_d_pTa, n)
                        pe.wait_ge(s_d_pT, n)
                        pe.wait_ge(s_d_vs, n)
                        pe.wait_ge(s_d_v, n)
                        if exists(t, -2):
                            pe.wait_ge(s_d_oT, n - 1)
                        for h in range(H2):
                            r, m = HD2 * (h % 2), h // 2
                            for i, v in enumerate((d_vs, d_va)):
                                ins = pe.matmul(ps[r:r + HD2, 2, m * P + i * WIN:m * P + (i + 1) * WIN],
                                                v[:, 1 - par, h * HD2:(h + 1) * HD2],
                                                d_pT[:, 4 * (h % 2) + m, i * WIN:(i + 1) * WIN], start=True, stop=True,
                                                skip_group_check=True)
                        ins.then_inc(s_d_o, 1)

                pe.wait_ge(s_d_wa, l + 1)
                pe.wait_ge(s_d_wst, l + 1)
                proj_qk(0, 0)
                proj_qk(1, 1)
                walk(pe, step, TILES + 2)

                pe.wait_ge(s_f_hT, l + 1)
                for g in range(NCH):
                    for i in range(4):
                        t = 4 * g + i
                        ins = pe.transpose(ps[:, g, i * P:(i + 1) * P], hT[:, WIN + t * P:WIN + (t + 1) * P],
                                           ident[:, :])
                    ins.then_inc(s_f_hp, 1)
                for g in range(NCH):
                    pe.wait_ge(s_f_xn, NCH * l + g + 1)
                    for i in range(4):
                        ins = pe.transpose(ps[:, 4 + g, i * P:(i + 1) * P], xn[:, 4 * g + i, :], ident[:, :])
                    ins.then_inc(s_f_xp, 1)

                def down(c):
                    for m, (r, n) in enumerate(M1):
                        pe.wait_ge(s_f_u, 3 * NCH * l + 3 * c + m + 1)
                        if m == 0 and c >= 2:
                            pe.wait_ge(s_f_z, NCH * l + c - 1)
                        ins = pe.matmul(ps[:, 6 + c % 2, :], l_down[0:n, m, :], gbuf[0:n, c % 2, m, :],
                                        start=(m == 0), stop=(m == 2))
                    ins.then_inc(s_f_y, 1)

                pe.wait_ge(s_f_yT, NCH * l + NCH)
                for c in range(NCH):
                    for m, (r, n) in enumerate(M1):
                        k = 3 * NCH * l + 3 * c + m
                        if c >= 1:
                            pe.wait_ge(s_f_ge, k - 2)
                            pe.wait_ge(s_f_u, k - 2)
                        x = yT[:, c * CH:(c + 1) * CH]
                        pe.matmul(ps[0:n, m, :], l_up[:, HID + r:HID + r + n], x, start=True, stop=True)\
                          .then_inc(s_f_g, 1)
                        pe.matmul(ps[0:n, 3 + m, :], l_up[:, r:r + n], x, start=True, stop=True)\
                          .then_inc(s_f_a, 1)
                    if c >= 1:
                        down(c - 1)
                down(NCH - 1)
            pe.wait_ge(s_f_z, DEPTH * NCH)
            norm_out(3, xT)


        @block.vector
        def _(dve):
            ch = Chain(dve, s_dve)

            def normalise_stats(n, src):
                for t in range(TILES):
                    ch.link(dve.bn_stats(stats[:, t, :], src(t)))
                ch.settle()
                for t in range(TILES):
                    ins = dve.bn_aggr(mv[:, t, :], stats[:, t, :])
                ins.then_inc(s_var, 1)
                dve.wait_ge(s_sd, n)
                ch.step(dve.reciprocal(rstd[:, :], sd[:, :]))

            def norm_in(k):
                def tile(t):
                    if k > 0 and t % 4 == 0:
                        dve.wait_ge(s_res, NCH * (k - 1) + t // 4 + 1)
                    return x_sb[:, t, :]

                normalise_stats(2 * k + 1, tile)
                for t in range(TILES):
                    ins = dve.tensor_scalar(xn[:, t, :], x_sb[:, t, :], mv[:, t, 0:1], rstd[:, t:t + 1],
                                            ALU.subtract, ALU.mult)
                    if t % 4 == 3:
                        ins.then_inc(s_xn, 1)

            def norm_out(k):
                def tile(t):
                    if t % 4 == 0:
                        dve.wait_ge(s_yp, NCH * k + t // 4 + 1)
                    return ps[:, t // 4, (t % 4) * P:(t % 4 + 1) * P]

                normalise_stats(2 * k + 2, tile)
                for t in range(TILES):
                    ins = dve.tensor_scalar(xn[:, t, :], ps[:, t // 4, (t % 4) * P:(t % 4 + 1) * P],
                                            mv[:, t, 0:1], rstd[:, t:t + 1], ALU.subtract, ALU.mult)
                    if t % 4 == 3:
                        ins.then_inc(s_yn, 1)

            dve.memset(w3o[:, :, :], 0.0)
            dve.memset(b4[:, :, :], 0.0).then_inc(s_ld_z, 1)
            dve.sem_inc(s_c_evB, 1)
            dve.memset(eps_c[:, :], EPS).then_inc(s_eps, 1)
            dve.sem_inc(s_a_evB, 1)
            dve.sem_inc(s_a_oadd, 1)
            dve.wait_ge(s_ld_x, 16 * BATCH)
            norm_in(0)
            for g, dst in enumerate((w0q[:, 0:4, :], w0k[:, 0:4, :], w0v[:, 0:2, :], w0v[:, 2:4, :])):
                dve.wait_ge(s_w0p, g + 1)
                ch.link(dve.tensor_copy(dst, ps[:, 4 + g, :].rearrange("p (n c) -> p n c", n=dst.shape[1])))
            ch.settle()
            for w in (w0q, w0k, w0v):
                ins = dve.tensor_copy(w[:, PAIRS, :], w[:, 0, :])
            ins.then_inc(s_w0t, 1)
            for g in range(9):
                dve.wait_ge(s_fp, g + 1)
                src = ps[:, 4 + g % 4, :]
                if g < 6:
                    slot = (0, 2, 1)[g // 2]
                    ins = dve.tensor_copy(fT[:, 4 * (g % 2):4 * (g % 2) + 4, slot, :],
                                          src.rearrange("p (n c) -> p n c", n=4))
                elif g < 8:
                    n = (4, 2)[g - 6]
                    ins = dve.tensor_copy(swT[:, 4 * (g - 6):4 * (g - 6) + n, :],
                                          src[:, 0:n * P].rearrange("p (n c) -> p n c", n=n))
                else:
                    dve.tensor_copy(gateT[:, :], src[:, 0:E0])
                    ins = dve.tensor_copy(fb[:, 0:E0, :],
                                          src[:, E0:4 * E0].rearrange("p (n e) -> p e n", n=3))
                ins.then_inc(s_ft, 1)
            dve.memset(fT[:, E0, :, :], 0.0)
            dve.memset(fb[:, E0, :], 0.0)
            dve.memset(sel[:, E0, :, :], 0.0)
            dve.tensor_copy(sel[:, 0:E0, :, :], sel_f[:, :, :, :]).then_inc(s_selc, 1)
            dve.memset(yT[:, :], 0.0).then_inc(s_a_ozero, 1)

            def a_evac_k(m):
                dve.wait_ge(s_a_projk, m)
                dve.tensor_copy(k_st[:, :].rearrange("p (n c) -> p n c", n=2), ps[:, 2:4, :]).then_inc(s_a_k, 1)

            def a_evac_v(m):
                dve.wait_ge(s_a_projv1, m)
                dve.tensor_copy(v_st[:, 4:8, :].rearrange("p (n k) c -> p n (k c)", n=2),
                                ps[:, 2:4, :]).then_inc(s_a_v1, 1)

            a_evac_k(1)
            a_evac_v(1)
            dve.wait_ge(s_a_ozero, 1)
            with dve.Fori(0, PAIRS) as p:
                for b in range(BATCH):
                    n0 = 2 * NU * p + NU * b
                    m = 2 * p + b

                    def rowmax(u):
                        dve.wait_ge(s_a_scores, n0 + u + 1)
                        s2 = ps[:, 2 * (u % 2):2 * (u % 2) + 2, :].rearrange("p n c -> p (n c)")
                        dve.tensor_reduce(negmax[:, u:u + 1], s2, AX_X, ALU.max, negate=True)\
                           .then_inc(s_a_negmax, 1)

                    def rrecip(u):
                        dve.wait_ge(s_a_exp, n0 + u + 1)
                        dve.reciprocal(rrow[:, u:u + 1], rowsum[:, u:u + 1]).then_inc(s_a_rrow, 1)
                        dve.wait_ge(s_a_rrow, n0 + u + 1)
                        dve.tensor_scalar(probs[:, u % NPB, :], probs[:, u % NPB, :], rrow[:, u:u + 1], None,
                                          ALU.mult).then_inc(s_a_norm, 1)

                    def copy_out(u):
                        dve.wait_ge(s_a_trans, 2 * (n0 + u) + 2)
                        c, q = u // 4, (u % 4) * P
                        dve.tensor_copy(probsT[:, c % 2, 4:8, q:q + P],
                                        ps[:, 5, :].rearrange("p (k c) -> p k c", k=4)).then_inc(s_a_evB, 1)

                    def add_out(qc):
                        dve.wait_ge(s_a_pv, 2 * m + qc + 1)
                        dve.wait_ge(s_a_oadd, 2 * m + qc + 1)
                        y = yT[:, b * SEQ + qc * CH:b * SEQ + (qc + 1) * CH]
                        dve.tensor_tensor(y, ps[:, 6 + qc, :], y, ALU.add).then_inc(s_a_oadd, 1)

                    for u in range(NU):
                        rowmax(u)
                        if u >= 1:
                            rrecip(u - 1)
                        if u >= 2:
                            copy_out(u - 2)
                    rrecip(NU - 1)
                    copy_out(NU - 2)
                    a_evac_k(m + 2)
                    copy_out(NU - 1)
                    add_out(0)
                    add_out(1)
                    a_evac_v(m + 2)
            dve.wait_ge(s_a_oadd, 4 * PAIRS + 1)
            dve.sem_inc(s_y[0], 1)
            norm_out(0)

            norm_in(1)
            lg = ps[:, 7, 0:TILES * E0].rearrange("p (t e) -> p t e", e=E0)

            def per_token(v):
                return v.unsqueeze(2).to_broadcast([P, TILES, E0])

            dve.wait_ge(s_logits, 1)
            ch.step(dve.tensor_reduce(gmax[:, :], lg, AX_X, ALU.max))
            dve.tensor_tensor(gw[:, 0], lg, per_token(gmax[:, :]), ALU.subtract).then_inc(s_gshift, 1)
            dve.wait_ge(s_gexp, 1)
            ch.step(dve.tensor_reduce(gsum[:, :], gw[:, 1], AX_X, ALU.add))
            ch.step(dve.reciprocal(gmax[:, :], gsum[:, :]))
            ch.step(dve.tensor_tensor(gw[:, 2], gw[:, 1], per_token(gmax[:, :]), ALU.mult))
            for t in range(TILES):
                ch.link(dve.max(gw[:, 3, t, :], gw[:, 2, t, :]))
            ch.settle()
            for t in range(TILES):
                ch.link(dve.max_index(top_i[:, t, :], gw[:, 3, t, :], gw[:, 2, t, :]))
            ch.settle()
            ch.step(dve.tensor_copy(gw[:, 4], top_i[:, :, :]))
            for r in range(2):
                ch.link(dve.tensor_tensor(gw[:, 5 + r], iota8[:, :, :], per_token(gw[:, 4, :, r]), ALU.is_equal))
            ch.settle()
            ch.step(dve.tensor_tensor(G[:, :, 24:32], gw[:, 5], gw[:, 6], ALU.add))
            gb = e_sg[:, 0, 0:3 * TILES * E0 // 2].bitcast(BF16).rearrange("p (n t e) -> p n t e", t=TILES, e=E0)
            rest = gw[:, 2]
            for r in range(3):
                ch.step(dve.tensor_copy(gb[:, r], rest))
                ch.step(dve.tensor_copy(G[:, :, 8 * r:8 * r + 8], gb[:, r]))
                if r < 2:
                    ch.step(dve.tensor_tensor(gw[:, 5 + r], rest, gb[:, r], ALU.subtract))
                    rest = gw[:, 5 + r]
            dve.sem_inc(s_G, 1)

            for k in range(2 * NCH):
                dve.wait_ge(s_sh_u, k + 1)
                dve.wait_ge(s_sh_silu, k + 1)
                dve.tensor_tensor(e_sh[:, k % 2, :], ps[:, 2 + k % 2, :], e_sg[:, k % 2, :], ALU.mult)\
                   .then_inc(s_sh_h, 1)

            def e_weights(s, e, done):
                dve.tensor_copy(e_w[:, s, :, :], fT[:, e, :, :])
                dve.tensor_copy(e_b[:, s, :], fb[:, e, :])
                dve.tensor_copy(e_sel[:, s, :, :], sel[:, e, :, :]).then_inc(done, 1)

            e_weights(0, 0, s_e_wA)
            with dve.Fori(0, E0 // 2) as i:
                n0 = 2 * NCH * i

                def scale(k):
                    c = k % NCH
                    dve.wait_ge(s_e_bc, n0 + k + 1)
                    if k >= 2:
                        dve.wait_ge(s_e_x3, n0 + k - 1)
                    dve.tensor_tensor(e_xs[:, k % 2, :], ps[:, k % 2, :], xT[:, c * CH:(c + 1) * CH], ALU.mult)\
                       .then_inc(s_e_xs, 1)

                def product(k):
                    dve.wait_ge(s_e_t3, n0 + k + 1)
                    dve.wait_ge(s_e_x2, n0 + k + 1)
                    dve.wait_ge(s_e_y, n0 + k + 1)
                    dve.scalar_tensor_tensor(out=e_t[:, k % 2, :], in0=ps[:, 7, :], scalar=e_b[:, k // NCH, 1:2],
                                             in1=e_t3[:, k % 2, :], op0=ALU.add, op1=ALU.mult)\
                       .then_inc(s_e_t, 1)

                scale(0)
                for k in range(2 * NCH):
                    s = k // NCH
                    if k < 2 * NCH - 1:
                        scale(k + 1)
                    if k >= 2:
                        dve.wait_ge(s_e_t, n0 + k - 1)
                    dve.wait_ge(s_e_x3, n0 + k + 1)
                    dve.wait_ge(s_e_mask, n0 + k + 1)
                    dve.scalar_tensor_tensor(out=e_t3[:, k % 2, :], in0=ps[:, 5 + k % 2, :], scalar=e_b[:, s, 2:3],
                                             in1=e_mask[:, k % 2, :], op0=ALU.add, op1=ALU.mult)\
                       .then_inc(s_e_t3, 1)
                    if k >= 1:
                        product(k - 1)
                    if k == 1:
                        e_weights(1, 2 * i + 1, s_e_wB)
                    if k == NCH + 1:
                        e_weights(0, 2 * i + 2, s_e_wA)
                product(2 * NCH - 1)
            norm_out(1)

            norm_in(2)
            dve.wait_ge(s_c_bp, 1)
            dve.tensor_tensor(bias_y[:, :], ps[:, 4, 0:1], b3o[:, :], ALU.add).then_inc(s_c_by, 1)

            def c_table(g, j):
                dve.tensor_scalar(c_T[:, j, :], rel[:, :], slopes[:, bass.ds(4 * g + j, 1)], None, ALU.mult)\
                   .then_inc(s_c_T, 1)

            def c_recip(b):
                dve.reciprocal(rrow[:, CU * (1 - b):CU * (2 - b)], rowsum[:, CU * (1 - b):CU * (2 - b)])\
                   .then_inc(s_c_rr, 1)

            def c_divide(f, b, g, half):
                n = slice(half * CH, (half + 1) * CH)
                o = oT0[:, g, n] if b else oT1[:, g, n]
                dve.wait_ge(s_c_o, QT * f + 2)
                dve.wait_ge(s_c_bc, 2 * f + half + 1)
                dve.tensor_tensor(o, ps[:, 5, :], c_o[:, n], ALU.mult).then_inc(s_c_oT, 1)

            for b in range(BATCH):
                q = probs[:, 2 * b, :]
                dve.wait_ge(s_c_proj, 2 * b + 1)
                dve.tensor_scalar(q.rearrange("p (n c) -> p n c", n=2), ps[:, 4 * b:4 * b + 2, :], b3n[:, 0:1],
                                  HD1 ** -0.5, ALU.add, ALU.mult).then_inc(s_c_qe, 1)
                dve.wait_ge(s_c_qe, b + 1)
                ch.step(dve.tensor_copy(c_part[:, 0, b, 0, :], q))
                ch.step(dve.tensor_tensor(q, q, c_part[:, 0, b, 0, :], ALU.subtract))
                ch.step(dve.tensor_copy(c_part[:, 0, b, 1, :], q))
                dve.tensor_tensor(c_part[:, 0, b, 2, :], q, c_part[:, 0, b, 1, :], ALU.subtract).then_inc(s_c_pq, 1)
                if b == 0:
                    for j in range(4):
                        c_table(0, j)
            dve.memset(c_o, 0.0)
            ch.step(dve.memset(rowsum[:, :], 1.0))

            def c_bias(n0, u):
                j, qt = u % 4, u // 4
                w = (qt + 1) * P
                dve.wait_ge(s_c_scores, n0 + u + 1)
                if u >= 2 or not isinstance(n0, int):
                    dve.wait_ge(s_c_exp, n0 + u - 1)
                dve.sem_inc(s_c_go, 1)
                s2 = ps[:, 2 * (u % 2):2 * (u % 2) + 2, :].rearrange("p n c -> p (n c)")[:, 0:w]
                dve.tensor_tensor_reduce(c_sb[:, u % 2, 0:w], s2, c_T[:, j, SEQ - w:SEQ], 1.0, -3.0e38,
                                         ALU.add, ALU.max, cmax[:, u:u + 1]).then_inc(s_c_bias, 1)
                dve.wait_ge(s_c_bias, n0 + u + 1)
                dve.tensor_scalar(negmax[:, u:u + 1], cmax[:, u:u + 1], -1.0, None, ALU.mult)\
                   .then_inc(s_c_negmax, 1)

            dve.wait_ge(s_c_T, 4)
            c_bias(0, 0)
            c_bias(0, 1)
            with dve.Fori(0, GROUPS) as g:
                for b in range(BATCH):
                    n0 = 2 * CU * g + CU * b
                    m = 2 * g + b
                    h0 = CU // 2 * m

                    def copy_out(u):
                        j, qt = u % 4, u // 4
                        if qt >= 4:
                            dve.wait_ge(s_c_transB, h0 + u - CU // 2 + 1)
                            dve.tensor_copy(c_pT[:, qt % 2, j, 4:qt + 1, :],
                                            ps[:, 5, 0:(qt - 3) * P].rearrange("p (k c) -> p k c", c=P))\
                               .then_inc(s_c_evB, 1)

                    for u in range(2, CU):
                        c_bias(n0, u)
                        if u >= 3:
                            copy_out(u - 3)
                        if u == 2:
                            dve.wait_ge(s_c_exp, n0 + 1)
                            c_recip(b)
                        if u == 8:
                            c_divide(m, b, g, 0)
                        if u == 13:
                            c_divide(m, b, g, 1)
                        if b == 1 and u >= CU - 4:
                            c_table(g + 1, u % 4)
                    if b == 1:
                        dve.wait_ge(s_c_T, 4 * g + 8)
                    copy_out(CU - 3)
                    c_bias(n0 + CU, 0)
                    copy_out(CU - 2)
                    c_bias(n0 + CU, 1)
                    copy_out(CU - 1)
            dve.wait_ge(s_c_exp, 2 * GROUPS * CU)
            c_recip(0)
            c_divide(2 * GROUPS, 0, GROUPS, 0)
            c_divide(2 * GROUPS, 0, GROUPS, 1)
            norm_out(2)

            norm_in(3)
            ch.link(dve.memset(half_c[:, :], -0.5))
            ch.link(dve.tensor_copy(ident_b[:, :], ident[:, :]))
            ch.link(dve.memset(hT[:, :], 0.0))
            ch.link(dve.memset(d_vs[:, 0, :], 0.0))
            ch.link(dve.memset(d_kT[:, :, :, :], 0.0))
            dve.wait_ge(s_ld_r, 16 * 3)
            ch.link(dve.tensor_copy(mask_b, mask_f[:, 1:2, :].to_broadcast([P, TILES, P])))
            ch.settle()
            for b in range(BATCH):
                ch.link(dve.tensor_copy(mask_b[:, b * QT, :], mask_f[:, 0, :]))
            ch.settle()
            dve.wait_ge(s_ld_d, 16 * 31)
            dve.wait_ge(s_xT, NCH * 4)
            dve.sem_inc(s_d_z, 1)
            dve.sem_inc(s_d_init, 1)

            PER_LAYER = 36
            with dve.Fori(0, DEPTH) as l:
                T0 = TILES * l
                lch = Chain(dve, s_d_chain, PER_LAYER * l)

                def shift():
                    lch.link(dve.tensor_copy(hT[0:64, WIN:WIN + TOK], xT[0:64, :]))
                    for b in range(BATCH):
                        lch.link(dve.tensor_copy(hT[64:P, WIN + b * SEQ + 1:WIN + (b + 1) * SEQ],
                                                 xT[64:P, b * SEQ:(b + 1) * SEQ - 1]))
                    lch.settle()

                dve.sem_inc(s_d_layer, 1)
                lch.link(dve.tensor_copy(l_b[:, :], b4[:, l, :]))
                shift()
                dve.sem_inc(s_d_wst, 1)
                dve.tensor_scalar(hq[:, 0, :], hT[:, WIN:WIN + P], 0.0, None, ALU.add).then_inc(s_d_hq, 1)
                dve.tensor_scalar(hq[:, 1, :], hT[:, WIN + P:WIN + 2 * P], 0.0, None, ALU.add).then_inc(s_d_hq, 1)
                sc = qk_scale[:, l, :, :]
                for b in range(BATCH):
                    t0 = b * QT
                    for n in range(2):
                        lch.link(dve.tensor_tensor(rot_c[:, t0:t0 + QT, n, :], base_c[:, :, n, :],
                                                   sc[:, n:n + 1, :].to_broadcast([P, QT, HD2]), ALU.mult))
                        for half in range(2):
                            d, e = 32 * half, 32 * (1 - half)
                            lch.link(dve.tensor_tensor(rot_s[:, t0:t0 + QT, n, d:d + 32], base_s[:, :, n, d:d + 32],
                                                       sc[:, n:n + 1, e:e + 32].to_broadcast([P, QT, 32]), ALU.mult))
                lch.settle()

                def copy_hq(t, par):
                    if exists(t, -2):
                        dve.wait_ge(s_d_qkp, T0 + t - 1)
                    dve.tensor_scalar(hq[:, par, :], hT[:, bass.ds(WIN + t * P, P)], 0.0, None, ALU.add)\
                       .then_inc(s_d_hq, 1)

                def copy_hv(t, par):
                    if exists(t, -2):
                        dve.wait_ge(s_d_vp, T0 + t - 1)
                    dve.tensor_scalar(hv[:, par, :], hT[:, bass.ds(WIN + t * P, P)], 0.0, None, ALU.add)\
                       .then_inc(s_d_hv, 1)

                def rotate(t, par):
                    n = T0 + t
                    qk = ps[:, 0:2, :].rearrange("p n (h d) -> p n h d", d=HD2)
                    mA = d_mA[:, par, :].rearrange("p (n h d) -> p n h d", n=2, d=HD2)
                    mB = d_mB[:, par, :].rearrange("p (n h d) -> p n h d", n=2, d=HD2)

                    def heads(v):
                        return v.rearrange("p t n d -> p n t d").to_broadcast([P, 2, H2, v.shape[3]])

                    dve.wait_ge(s_d_sq, n + 1)
                    dve.tensor_tensor(mA, qk, heads(rot_c[:, bass.ds(t, 1), :, :]), ALU.mult)
                    for d, e in ((0, 32), (32, 0)):
                        ins = dve.tensor_tensor(mB[:, :, :, d:d + 32], qk[:, :, :, e:e + 32],
                                                heads(rot_s[:, bass.ds(t, 1), :, d:d + 32]), ALU.mult)
                    ins.then_inc(s_d_m, 1)

                def norms(t, par):
                    n = T0 + t
                    dve.tensor_reduce(ss[:, par, :], d_sq[:, par, :].rearrange("p (h d) -> p h d", d=HD2),
                                      AX_X, ALU.add).then_inc(s_d_ss, 1)
                    dve.wait_ge(s_d_ss, n + 1)
                    dve.tensor_scalar(ss[:, par, :], ss[:, par, :], 1e-24, None, ALU.max).then_inc(s_d_cl, 1)

                def step(t, par):
                    n = T0 + t
                    if exists(t, 0):
                        if exists(t, -1):
                            dve.wait_ge(s_d_v, n)
                            if exists(t, -2):
                                dve.wait_ge(s_d_o, n - 1)
                            dve.tensor_scalar(d_vs[WIN:P, par, :], d_va[WIN:P, 1 - par, :], 0.0, None, ALU.add)\
                               .then_inc(s_d_vs, 1)
                        else:
                            dve.sem_inc(s_d_vs, 1)
                    if exists(t, 2):
                        rotate(t + 2, par)
                    if exists(t, -1):
                        dve.wait_ge(s_d_pt, n)
                        dve.tensor_copy(d_pT[:, 4:8, :].rearrange("p h c -> p (h c)"), ps[:, 5, :])\
                           .then_inc(s_d_pT, 1)
                    if exists(t, 0):
                        dve.wait_ge(s_d_s, n + 1)
                        dve.tensor_reduce(d_nm[:, par, :], ps[:, 6:8, :].rearrange("p n (h c) -> p (n h) c", c=P),
                                          AX_X, ALU.max).then_inc(s_d_nm, 1)
                        dve.wait_ge(s_d_nm, n + 1)
                        dve.tensor_scalar(d_nm8[:, par, :], d_nm[:, par, :], -QK, None, ALU.mult)\
                           .then_inc(s_d_nm8, 1)
                    if exists(t, 2):
                        norms(t + 2, par)
                    if exists(t, -2):
                        dve.wait_ge(s_d_w, n - 1)
                        z = xT[:, bass.ds((t - 2) * P, P)]
                        dve.tensor_tensor(z, ps[:, 3, 0:P], z, ALU.add).then_inc(s_d_z, 1)
                    if exists(t, 3):
                        copy_hq(t + 3, 1 - par)
                    if exists(t, 1):
                        copy_hv(t + 1, 1 - par)
                    if exists(t, 0):
                        dve.wait_ge(s_d_e, n + 1)
                        dve.reciprocal(d_rr[:, par, :], d_sum[:, par, :]).then_inc(s_d_rr, 1)

                rotate(0, 0)
                norms(0, 0)
                copy_hq(2, 0)
                copy_hv(0, 0)
                rotate(1, 1)
                norms(1, 1)
                walk(dve, step, TILES + 2)

                dve.wait_ge(s_d_z, T0 + TILES + 1)
                shift()
                dve.sem_inc(s_f_hT, 1)
                for t in range(TILES):
                    if t % 4 == 0:
                        dve.wait_ge(s_f_hp, NCH * l + t // 4 + 1)
                    lch.link(dve.bn_stats(stats[:, t, :], ps[:, t // 4, (t % 4) * P:(t % 4 + 1) * P]))
                lch.settle()
                dve.sem_inc(s_f_go, 1)
                for t in range(TILES):
                    ins = dve.bn_aggr(mv[:, t, :], stats[:, t, :])
                ins.then_inc(s_f_var, 1)
                dve.wait_ge(s_f_sd, l + 1)
                lch.step(dve.reciprocal(rstd[:, :], sd[:, :]))
                for t in range(TILES):
                    ins = dve.tensor_scalar(xn[:, t, :], ps[:, t // 4, (t % 4) * P:(t % 4 + 1) * P],
                                            mv[:, t, 0:1], rstd[:, t:t + 1], ALU.subtract, ALU.mult)
                    if t % 4 == 3:
                        ins.then_inc(s_f_xn, 1)

                def add_down(c):
                    dve.wait_ge(s_f_y, NCH * l + c + 1)
                    z = xT[:, c * CH:(c + 1) * CH]
                    dve.scalar_tensor_tensor(out=z, in0=ps[:, 6 + c % 2, :], scalar=l_b[:, 6:7], in1=z,
                                             op0=ALU.add, op1=ALU.add).then_inc(s_f_z, 1)

                for c in range(NCH):
                    for m, (r, n) in enumerate(M1):
                        k = 3 * NCH * l + 3 * c + m
                        dve.wait_ge(s_f_a, k + 1)
                        dve.wait_ge(s_f_ge, k + 1)
                        dve.scalar_tensor_tensor(out=gbuf[0:n, c % 2, m, :], in0=ps[0:n, 3 + m, :],
                                                 scalar=l_b[0:n, m:m + 1], in1=gbuf[0:n, c % 2, m, :],
                                                 op0=ALU.add, op1=ALU.mult).then_inc(s_f_u, 1)
                    if c >= 1:
                        add_down(c - 1)
                add_down(NCH - 1)
                dve.wait_ge(s_f_z, NCH * l + NCH)
                assert lch.n == PER_LAYER, lch.n
            norm_out(3)


        @block.scalar
        def _(act):
            def norm_in(k):
                act.wait_ge(s_var, 2 * k + 1)
                act.activation(sd[:, :], mv[:, :, 1], ACT.Sqrt, bias=eps_c[:, 0:1]).then_inc(s_sd, 1)
                for g in range(NCH):
                    act.wait_ge(s_xTp, NCH * k + g + 1)
                    act.copy(xT[:, g * CH:(g + 1) * CH], ps[:, g, :]).then_inc(s_xT, 1)

            def norm_out(k):
                act.wait_ge(s_var, 2 * k + 2)
                act.activation(sd[:, :], mv[:, :, 1], ACT.Sqrt, bias=eps_c[:, 0:1]).then_inc(s_sd, 1)

            act.sem_inc(s_a_evA, 1)
            act.wait_ge(s_eps, 1)
            norm_in(0)

            def a_evac_q(m):
                act.wait_ge(s_a_projq, m)
                act.copy(q_st[:, :].rearrange("p (n c) -> p n c", n=2), ps[:, 0:2, :]).then_inc(s_a_q, 1)

            def a_evac_v(m):
                act.wait_ge(s_a_projv0, m)
                act.copy(v_st[:, 0:4, :].rearrange("p (n k) c -> p n (k c)", n=2), ps[:, 0:2, :]).then_inc(s_a_v0, 1)

            act.activation(sd[:, 0:1], eps_c[:, 0:1], ACT.Exp)
            a_evac_q(1)
            a_evac_v(1)
            with act.Fori(0, PAIRS) as p:
                for b in range(BATCH):
                    n0 = 2 * NU * p + NU * b
                    m = 2 * p + b

                    def soft(u):
                        act.wait_ge(s_a_negmax, n0 + u + 1)
                        if u >= NPB:
                            act.wait_ge(s_a_trans, 2 * (n0 + u - NPB) + 2)
                        s2 = ps[:, 2 * (u % 2):2 * (u % 2) + 2, :].rearrange("p n c -> p (n c)")
                        act.activation(probs[:, u % NPB, :], s2, ACT.Exp, bias=negmax[:, u:u + 1],
                                       accum_out=rowsum[:, u:u + 1]).then_inc(s_a_exp, 1)

                    def copy_out(u):
                        act.wait_ge(s_a_trans, 2 * (n0 + u) + 1)
                        c, q = u // 4, (u % 4) * P
                        act.copy(probsT[:, c % 2, 0:4, q:q + P],
                                 ps[:, 4, :].rearrange("p (k c) -> p k c", k=4)).then_inc(s_a_evA, 1)

                    for u in range(NU):
                        if u >= 2:
                            copy_out(u - 2)
                        soft(u)
                    copy_out(NU - 2)
                    a_evac_q(m + 2)
                    copy_out(NU - 1)
                    a_evac_v(m + 2)
            norm_out(0)

            norm_in(1)
            act.wait_ge(s_gshift, 1)
            act.activation(gw[:, 1], gw[:, 0], ACT.Exp).then_inc(s_gexp, 1)

            for k in range(2 * NCH):
                act.wait_ge(s_sh_g, k + 1)
                if k >= 2:
                    act.wait_ge(s_sh_h, k - 1)
                if k == 0:
                    act.wait_ge(s_G, 1)
                act.activation(e_sg[:, k % 2, :], ps[:, k % 2, :], ACT.Silu).then_inc(s_sh_silu, 1)
                if k >= 3 and k % 2 == 1:
                    c = k // 2 - 1
                    act.wait_ge(s_sh_z, c + 1)
                    act.copy(yT[:, c * CH:(c + 1) * CH], ps[:, 4 + c % 2, :]).then_inc(s_sh_y, 1)
            act.wait_ge(s_sh_z, NCH)
            act.copy(yT[:, (NCH - 1) * CH:NCH * CH], ps[:, 4 + (NCH - 1) % 2, :]).then_inc(s_sh_y, 1)
            for g in range(NCH):
                act.wait_ge(s_gTp, g + 1)
                act.copy(gT[:, g * CH:(g + 1) * CH], ps[0:STRIP, 6 + g % 2, :]).then_inc(s_gT, 1)

            with act.Fori(0, E0 // 2) as i:
                n0 = 2 * NCH * i

                def mask(k):
                    act.wait_ge(s_e_bc, n0 + k + 1)
                    if k >= 2:
                        act.wait_ge(s_e_t3, n0 + k - 1)
                    act.copy(e_mask[:, k % 2, :], ps[:, 2, :]).then_inc(s_e_mask, 1)

                mask(0)
                for k in range(2 * NCH):
                    if k < 2 * NCH - 1:
                        mask(k + 1)
                    act.wait_ge(s_e_h1, n0 + k + 1)
                    act.activation(e_h[:, k % 2, :], ps[:, 3 + k % 2, :], ACT.Silu,
                                   bias=e_b[:, k // NCH, 0:1]).then_inc(s_e_h, 1)
            norm_out(1)

            norm_in(2)
            act.sem_inc(s_c_evA, 1)
            act.sem_inc(s_c_o, 1)

            def c_key(b, part):
                k = probs[:, 2 * b + 1, :]
                if part == 0:
                    act.wait_ge(s_c_proj, 2 * b + 2)
                    act.activation(k.rearrange("p (n c) -> p n c", n=2), ps[:, 4 * b + 2:4 * b + 4, :], ACT.Identity,
                                   bias=b3n[:, 1:2]).then_inc(s_c_ke, 1)
                    act.wait_ge(s_c_ke, 3 * b + 1)
                else:
                    act.wait_ge(s_c_kr, 2 * b + 1)
                act.copy(c_part[:, 1, b, part, :], k).then_inc(s_c_ke, 1)

            def c_keep_sums(f):
                act.wait_ge(s_c_rrp, f + 1)
                act.copy(c_rT[:, :], ps[0:STRIP, 5, 0:P]).then_inc(s_c_rT, 1)

            c_key(0, 0)
            c_key(0, 1)
            c_key(1, 0)
            act.wait_ge(s_c_projv, 1)
            act.copy(v_nat[:, :, :].rearrange("p (n k) c -> p n (k c)", n=4), ps[:, 0:4, :]).then_inc(s_c_v, 1)
            c_key(1, 1)
            act.wait_ge(s_c_kr, 4)

            def c_soft(b, n0, h0, u):
                w = (u // 4 + 1) * P
                act.wait_ge(s_c_negmax, n0 + u + 1)
                if u >= NPB:
                    v = u - NPB
                    if v // 4 >= 4:
                        act.wait_ge(s_c_transB, h0 + v - CU // 2 + 1)
                    else:
                        act.wait_ge(s_c_transA, n0 + v + 1)
                act.activation(probs[:, u % NPB, 0:w], c_sb[:, u % 2, 0:w], ACT.Exp, bias=negmax[:, u:u + 1],
                               accum_out=rowsum[:, CU * b + u:CU * b + u + 1]).then_inc(s_c_exp, 1)

            def c_out(m, qt):
                if qt == 0:
                    act.wait_ge(s_c_oT, 2 * m + 2)
                act.wait_ge(s_c_pv, QT * m + qt + 2)
                act.copy(c_o[:, qt * P:(qt + 1) * P], ps[:, 6 + qt % 2, 0:P]).then_inc(s_c_o, 1)

            def c_out_last(m):
                act.wait_ge(s_c_pv, QT * m + 1)
                act.copy(c_o[:, (QT - 1) * P:QT * P], ps[:, 7, 0:P]).then_inc(s_c_o, 1)

            c_soft(0, 0, 0, 0)
            c_soft(0, 0, 0, 1)
            with act.Fori(0, GROUPS) as g:
                for b in range(BATCH):
                    n0 = 2 * CU * g + CU * b
                    m = 2 * g + b
                    h0 = CU // 2 * m

                    def copy_out(u):
                        j, qt = u % 4, u // 4
                        k = min(4, qt + 1)
                        act.wait_ge(s_c_transA, n0 + u + 1)
                        act.copy(c_pT[:, qt % 2, j, 0:k, :],
                                 ps[:, 4, 0:k * P].rearrange("p (k c) -> p k c", c=P)).then_inc(s_c_evA, 1)

                    for u in range(2, CU):
                        if u >= 3:
                            copy_out(u - 3)
                        if u == 14:
                            c_out(m, 0)
                        if u >= 16 and u % 4 == 0:
                            c_out(m, (u - 12) // 4)
                        c_soft(b, n0, h0, u)
                        if u == 3:
                            c_keep_sums(m)
                        if u == 6:
                            c_out_last(m)
                    copy_out(CU - 3)
                    c_soft(1 - b, n0 + CU, None, 0)
                    copy_out(CU - 2)
                    c_soft(1 - b, n0 + CU, None, 1)
                    copy_out(CU - 1)
                    c_out(m, QT - 3)
                    c_out(m, QT - 2)
            c_keep_sums(2 * GROUPS)
            c_out_last(2 * GROUPS)
            for c in range(NCH):
                act.wait_ge(s_c_y, c + 1)
                act.activation(yT[:, c * CH:(c + 1) * CH], ps[:, 4 + c, :], ACT.Identity,
                               bias=bias_y[:, 0:1]).then_inc(s_c_yc, 1)
            act.wait_ge(s_c_yc, NCH)
            act.sem_inc(s_y[2], 1)
            norm_out(2)

            norm_in(3)
            with act.Fori(0, DEPTH) as l:
                T0 = TILES * l

                def square(t, par):
                    act.wait_ge(s_d_qkp, T0 + t + 1)
                    act.activation(d_sq[:, par, :], ps[:, 0:2, :].rearrange("p n c -> p (n c)"), ACT.Square)\
                       .then_inc(s_d_sq, 1)

                def step(t, par):
                    n = T0 + t
                    if exists(t, 0):
                        act.wait_ge(s_d_qkt, n + 1)
                        act.copy(d_qT, ps[:, 4, :].rearrange("p (m c) -> p m c", m=4)).then_inc(s_d_qT, 1)
                        act.copy(d_kT[:, par, :, :], ps[:, 5, :].rearrange("p (m c) -> p m c", m=4))\
                           .then_inc(s_d_kT, 1)
                    if exists(t, 2):
                        square(t + 2, par)
                    if exists(t, 0):
                        act.wait_ge(s_d_vp, n + 1)
                        if exists(t, -1):
                            act.wait_ge(s_d_vs, n)
                        act.copy(d_va[:, par, :], ps[:, 3, :])
                        act.copy(d_vs[0:WIN, par, :], ps[0:WIN, 3, :]).then_inc(s_d_v, 1)
                    if exists(t, -1):
                        act.wait_ge(s_d_pt, n)
                        act.copy(d_pT[:, 0:4, :].rearrange("p h c -> p (h c)"), ps[:, 4, :]).then_inc(s_d_pTa, 1)
                    if exists(t, 0):
                        act.wait_ge(s_d_nm8, n + 1)
                        for h in range(H2):
                            ins = act.activation(d_p[:, par, h, :], ps[:, 6 + h // 4, (h % 4) * P:(h % 4 + 1) * P],
                                                 ACT.Exp, bias=d_nm8[:, par, h:h + 1], scale=QK,
                                                 accum_out=d_sum[:, par, h:h + 1])
                        ins.then_inc(s_d_e, 1)
                    if exists(t, -1):
                        act.wait_ge(s_d_o, n)
                        act.copy(d_o[:, 1 - par, :, :], ps[:, 2, :].rearrange("p (m c) -> p m c", m=4))\
                           .then_inc(s_d_oT, 1)

                act.wait_ge(s_d_layer, l + 1)
                act.sem_inc(s_d_go, 1)
                act.copy(l_qkv, w4qkv[:, l, :])
                act.copy(l_up, w4up[:, l, :])
                for m, (r, n) in enumerate(M1):
                    act.copy(l_down[0:n, m, :], w4down[0:n, l, m, :])
                act.copy(l_o, w4o[:, l, :, :]).then_inc(s_d_wa, 1)
                square(0, 0)
                square(1, 1)
                walk(act, step, TILES + 1)

                act.wait_ge(s_f_var, l + 1)
                act.activation(sd[:, :], mv[:, :, 1], ACT.Sqrt, bias=eps_c[:, 0:1]).then_inc(s_f_sd, 1)
                for g in range(NCH):
                    act.wait_ge(s_f_xp, NCH * l + g + 1)
                    act.activation(yT[:, g * CH:(g + 1) * CH], ps[:, 4 + g, :], ACT.Identity,
                                   bias=l_b[:, 8:9], scale=l_b[:, 7:8]).then_inc(s_f_yT, 1)
                for c in range(NCH):
                    for m, (r, n) in enumerate(M1):
                        k = 3 * NCH * l + 3 * c + m
                        act.wait_ge(s_f_g, k + 1)
                        if c >= 2:
                            act.wait_ge(s_f_y, NCH * l + c - 1)
                        act.activation(gbuf[0:n, c % 2, m, :], ps[0:n, m, :], ACT.Gelu,
                                       bias=l_b[0:n, 3 + m:4 + m]).then_inc(s_f_ge, 1)
            norm_out(3)


        @block.gpsimd
        def _(pool):
            def a_weights(p):
                pool.tensor_copy(wq_st[:, :], w0q[:, p, :])
                pool.tensor_copy(wk_st[:, :], w0k[:, p, :])
                pool.tensor_copy(wv_st[:, :], w0v[:, p, :]).then_inc(s_a_wst, 1)

            def norm_out(k):
                for g in range(NCH):
                    x = x_sb[:, 4 * g:4 * g + 4, :]
                    pool.wait_ge(s_yn, NCH * k + g + 1)
                    pool.tensor_tensor(x, x, xn[:, 4 * g:4 * g + 4, :], ALU.add).then_inc(s_res, 1)

            pool.wait_ge(s_w0t, 1)
            a_weights(0)
            with pool.Fori(0, PAIRS) as p:
                for b in range(BATCH):
                    if b == 1:
                        pool.wait_ge(s_a_scores, 2 * NU * p + NU + 1)
                        a_weights(p + 1)

            norm_out(0)

            pool.sem_inc(s_e_y, 2)
            pool.wait_ge(s_sh_y, NCH)
            with pool.Fori(0, E0 // 2) as i:
                for k in range(2 * NCH):
                    c = k % NCH
                    y = yT[:, c * CH:(c + 1) * CH]
                    pool.wait_ge(s_e_t, 2 * NCH * i + k + 1)
                    pool.wait_ge(s_e_y, 2 * NCH * i + k + 2)
                    pool.tensor_tensor(y, y, e_t[:, k % 2, :], ALU.add).then_inc(s_e_y, 1)
            pool.wait_ge(s_e_y, E0 * NCH + 2)
            pool.sem_inc(s_y[1], 1)
            norm_out(1)

            pool.memset(v_st[:, :, :], 0.0).then_inc(s_c_vz, 1)
            for b in range(BATCH):
                k = probs[:, 2 * b + 1, :]
                pool.wait_ge(s_c_ke, 3 * b + 2)
                pool.tensor_tensor(k, k, c_part[:, 1, b, 0, :], ALU.subtract).then_inc(s_c_kr, 1)
                pool.wait_ge(s_c_ke, 3 * b + 3)
                pool.wait_ge(s_c_kr, 2 * b + 1)
                pool.tensor_tensor(c_part[:, 1, b, 2, :], k, c_part[:, 1, b, 1, :], ALU.subtract).then_inc(s_c_kr, 1)
                pool.wait_ge(s_c_kr, 2 * b + 2)
                pool.sem_inc(s_c_pk, 1)

            def c_values(g, b):
                pool.tensor_copy(c_v[:, b, :, :].rearrange("p k (j e) -> p k j e", j=4)[:, :, :, 0:HD1],
                                 v_nat[:, b * QT:(b + 1) * QT, bass.ds(4 * HD1 * g, 4 * HD1)]
                                 .rearrange("p k (j e) -> p k j e", j=4)).then_inc(s_c_vst, 1)

            pool.wait_ge(s_c_v, 1)
            pool.wait_ge(s_c_vz, 1)
            c_values(0, 0)
            c_values(0, 1)
            with pool.Fori(0, GROUPS - 1) as g:
                for b in range(BATCH):
                    pool.wait_ge(s_c_pv, 2 * QT * g + QT * (b + 1) + 1)
                    c_values(g + 1, b)

            norm_out(2)

            pool.wait_ge(s_d_init, 1)
            with pool.Fori(0, DEPTH) as l:
                T0 = TILES * l

                def unit_norm(t, par):
                    n = T0 + t
                    kq = d_kq[par]
                    pool.wait_ge(s_d_m, n + 1)
                    pool.tensor_tensor(kq, d_mA[:, par, :], d_mB[:, par, :], ALU.add).then_inc(s_d_add, 1)
                    pool.wait_ge(s_d_cl, n + 1)
                    pool.tensor_tensor(ss[:, par, :], ss[:, par, :], half_c[:, :], ALU.pow).then_inc(s_d_rn, 1)
                    pool.wait_ge(s_d_add, n + 1)
                    pool.wait_ge(s_d_rn, n + 1)
                    v = kq.rearrange("p (h d) -> p h d", d=HD2)
                    pool.tensor_tensor(v, v, ss[:, par, :].unsqueeze(2).to_broadcast([P, 2 * H2, HD2]), ALU.mult)\
                        .then_inc(s_d_kq, 1)

                def step(t, par):
                    if exists(t, 0):
                        v = d_p[:, par, :, :]
                        pool.wait_ge(s_d_rr, T0 + t + 1)
                        pool.tensor_tensor(v, v, d_rr[:, par, :].unsqueeze(2).to_broadcast([P, H2, P]), ALU.mult)\
                            .then_inc(s_d_p, 1)
                    if exists(t, 2):
                        unit_norm(t + 2, par)

                unit_norm(0, 0)
                unit_norm(1, 1)
                walk(pool, step, TILES)
            norm_out(3)



def _constants():
    import numpy as np
    f = np.float32
    c = {"c_ident": np.eye(128, dtype=f)}
    e, part, r = np.meshgrid(np.arange(E0), np.arange(2), np.arange(STRIP), indexing="ij")
    pick = np.where(part == 0, (r < 24) & (r % 8 == e), r == 24 + e).astype(f)
    c["c_sel"] = np.ascontiguousarray(np.broadcast_to(pick.transpose(2, 0, 1)[..., None], (STRIP, E0, 2, P)))
    c["c_iota8"] = np.ascontiguousarray(np.broadcast_to(np.arange(E0, dtype=f), (P, TILES, E0)))
    p, k = np.arange(P)[:, None], np.arange(SEQ)[None, :] - (SEQ - P)
    c["c_rel"] = np.where(k <= p, k - p, -1e32).astype(f)
    c["c_slopes"] = np.ascontiguousarray(np.broadcast_to(
        np.power(f(2.0 ** (-8.0 / H1)), np.arange(1, H1 + 5, dtype=f)), (P, H1 + 4))).astype(f)
    r, q, s = np.meshgrid(np.arange(STRIP), np.arange(QT), np.arange(P), indexing="ij")
    c["c_selq"] = ((r // 4 == q) & (r % 4 == s // STRIP)).astype(f)
    half = np.arange(0, HD2, 2, dtype=f)
    pos = np.arange(SEQ, dtype=f)
    angle = pos[:, None] * (f(1.0) / np.power(f(10000.0), half / f(HD2)))[None, :]
    base = (half + f(0.4 * HD2)) / f(1.4 * HD2)
    scale = np.power(base[None, :], ((pos - SEQ // 2) / f(WIN // 2))[:, None])
    cos, sin = np.cos(angle), np.sin(angle)
    both = lambda u, v: np.concatenate([u, v], axis=1)
    c["c_rotc"] = np.stack([both(cos * scale, cos * scale), both(cos / scale, cos / scale)], 1).astype(f)
    c["c_rots"] = np.stack([both(-sin * scale, sin * scale), both(-sin / scale, sin / scale)], 1).astype(f)
    q, k = np.arange(P)[:, None], np.arange(P)[None, :]
    seen = (q % WIN <= k) & (k <= q % WIN + WIN)
    first = seen & ~((q < WIN) & (k < WIN))
    swap = lambda m: np.where(q < WIN, np.roll(m, WIN, axis=1), m)
    first, seen = swap(first), swap(seen)
    c["c_mask"] = np.ascontiguousarray(np.where(np.stack([first, seen], 1), 0.0, NEG).astype(f))
    return c


_INS = [
    "L0_attn_x",
    "L0_attn_Wq",
    "L0_attn_Wk",
    "L0_attn_Wv",
    "L0_ffn_w1",
    "L0_ffn_w2",
    "L0_ffn_w3",
    "L0_ffn_sw1",
    "L0_ffn_sw2",
    "L0_ffn_sw3",
    "L0_ffn_gate_w",
    "L0_ffn_b1",
    "L0_ffn_b2",
    "L0_ffn_b3",
    "L1_attn_Wq",
    "L1_attn_Wk",
    "L1_attn_Wv",
    "L1_attn_Wo",
    "L1_attn_bq",
    "L1_attn_bk",
    "L1_attn_bv",
    "L1_attn_bo",
    "L1_ffn_wqkv",
    "L1_ffn_wo",
    "L1_ffn_w1",
    "L1_ffn_w2",
    "L1_ffn_b1",
    "L1_ffn_b2",
    "L1_ffn_ln_g",
    "L1_ffn_ln_b",
    "L1_ffn_q_scale",
    "L1_ffn_k_scale",
]


def kernel(**inputs):
    import numpy as _np
    import concourse.bacc as _bacc
    from concourse import mybir as _mybir
    from concourse.bass_utils import run_bass_kernel_spmd as _run

    nc = _bacc.Bacc("TRN2", target_bir_lowering=False, num_devices=1)
    arrays, aps = {}, {}
    for name, a in [(n, _np.ascontiguousarray(inputs[n])) for n in _INS] + list(_constants().items()):
        arrays[f"in_{name}_dram"] = a
        aps[name] = nc.dram_tensor(f"in_{name}_dram", a.shape, _mybir.dt.from_np(a.dtype), kind="ExternalInput").ap()
    out = nc.dram_tensor("out_0_dram", (BATCH, SEQ, D), F32, kind="ExternalOutput").ap()
    build(nc, aps, out)
    r = _run(nc, [arrays], core_ids=[0])
    return r.results[0]["out_0_dram"]
```
